# Optimizing a Trainium2 kernel written in Bass

```python
import numpy as np
import jax
import jax.numpy as jnp

def _softmax(x, axis=-1):
    return jax.nn.softmax(x, axis=axis)

def _gelu(x):
    return jax.nn.gelu(x, approximate=True)

def _silu(x):
    return jax.nn.silu(x)

def _sigmoid(x):
    return jax.nn.sigmoid(x)

def _layernorm(x, axis=-1, eps=1e-05):
    m = jnp.mean(x, axis=axis, keepdims=True)
    v = jnp.var(x, axis=axis, keepdims=True)
    return (x - m) / jnp.sqrt(v + eps)

def _scatter_add(tgt, idx, src, axis=0):
    return tgt.at[idx].add(src)

def _segment_sum(src, seg, n):
    return jax.ops.segment_sum(src, seg, n)
kernel_name = 'mk_gnn_resnorm_d4_gnn_r8_19fdfd'

def setup_inputs(seed: int=0):
    np.random.seed(seed)
    _w = jnp.asarray

    def _rec_inputs():
        import jax
        import jax.numpy as jnp
        _gk = jax.random.key(seed)
        x = -6.415e-05 + 1 * jax.random.normal(jax.random.fold_in(_gk, 1), (1250, 512), jnp.float32)
        _s = jax.random.randint(jax.random.fold_in(_gk, 2), (10000,), 0, 1250, jnp.int32)
        _d = jax.random.randint(jax.random.fold_in(_gk, 3), (10000,), 0, 1250, jnp.int32)
        _loop = jnp.arange(1250, dtype=jnp.int32)
        src = jnp.concatenate([_s, _d, _loop])
        dst = jnp.concatenate([_d, _s, _loop])
        _o = jnp.argsort(dst, stable=True)
        src = src[_o]
        dst = dst[_o]
        edge_attr_64 = 0.000279952 + 1.00013 * jax.random.normal(jax.random.fold_in(_gk, 13), (21250, 64), jnp.float32)
        return (x, src, dst, edge_attr_64)
    x, src, dst, edge_attr_64 = _rec_inputs()

    def _L0_gnn_setup():
        import jax, jax.numpy as jnp
        import numpy as np
        N_NODES = 2500
        N_EDGES = 40000
        HIDDEN = 512
        EDGE_DIM = 64
        LN_EPS = 1e-05

        def mish(x):
            return x * jnp.tanh(jax.nn.softplus(x))
        key = jax.random.key(seed)
        ks = jax.random.split(key, 8)
        s = lambda fan_in: 1.0 / np.sqrt(fan_in)
        return {'x': jax.random.normal(ks[0], (N_NODES, HIDDEN), dtype=jnp.float32), 'edge_index': jax.random.randint(ks[1], (2, N_EDGES), 0, N_NODES, dtype=jnp.int64), 'edge_attr': jax.random.normal(ks[2], (N_EDGES, EDGE_DIM), dtype=jnp.float32), 'W1': jax.random.normal(ks[3], (2 * HIDDEN + EDGE_DIM, HIDDEN), dtype=jnp.float32) * s(2 * HIDDEN + EDGE_DIM), 'b1': jnp.zeros((HIDDEN,), dtype=jnp.float32), 'W2': jax.random.normal(ks[4], (HIDDEN, HIDDEN), dtype=jnp.float32) * s(HIDDEN), 'b2': jnp.zeros((HIDDEN,), dtype=jnp.float32), 'W3': jax.random.normal(ks[5], (2 * HIDDEN, HIDDEN), dtype=jnp.float32) * s(2 * HIDDEN), 'b3': jnp.zeros((HIDDEN,), dtype=jnp.float32), 'W4': jax.random.normal(ks[6], (HIDDEN, HIDDEN), dtype=jnp.float32) * s(HIDDEN), 'b4': jnp.zeros((HIDDEN,), dtype=jnp.float32), 'gamma': jnp.ones((HIDDEN,), dtype=jnp.float32), 'beta': jnp.zeros((HIDDEN,), dtype=jnp.float32)}
    _L0_gnn_all = _L0_gnn_setup()
    _L0_gnn_in = {k: v for k, v in _L0_gnn_all.items() if k in ('W1', 'b1', 'W2', 'b2', 'W3', 'b3', 'W4', 'b4', 'gamma', 'beta')}
    del _L0_gnn_all

    def _L1_gnn_setup():
        import jax, jax.numpy as jnp
        import numpy as np
        N, D, E = (6250, 512, 50000)
        EPS = 1e-05
        SLOPE = 0.01
        key = jax.random.key(seed)
        k1, k2, k3, k4 = jax.random.split(key, 4)
        x = jax.random.normal(k1, (N, D), dtype=jnp.float32)
        edge_index = jax.random.randint(k2, (2, E), 0, N, dtype=jnp.int64)
        s = 1.0 / np.sqrt(D)
        W_l = jax.random.normal(k3, (D, D), dtype=jnp.float32) * s
        b_l = jnp.zeros((D,), dtype=jnp.float32)
        W_r = jax.random.normal(k4, (D, D), dtype=jnp.float32) * s
        gamma = jnp.ones((D,), dtype=jnp.float32)
        beta = jnp.zeros((D,), dtype=jnp.float32)
        return {'x': x, 'edge_index': edge_index, 'W_l': W_l, 'b_l': b_l, 'W_r': W_r, 'gamma': gamma, 'beta': beta}
    _L1_gnn_all = _L1_gnn_setup()
    _L1_gnn_in = {k: v for k, v in _L1_gnn_all.items() if k in ('W_l', 'b_l', 'W_r', 'gamma', 'beta')}
    del _L1_gnn_all

    def _L2_gnn_setup():
        import jax, jax.numpy as jnp
        import numpy as np
        N = 6250
        E = 100000
        F_IN = 512
        F_OUT = 512
        key = jax.random.key(seed)
        k_feat, k_src, k_dst, k_w1, k_b1, k_w2, k_b2 = jax.random.split(key, 7)
        feat = jax.random.normal(k_feat, (N, F_IN), dtype=jnp.float32)
        src_idx = jax.random.randint(k_src, (E,), 0, N, dtype=jnp.int32)
        dst_idx = jax.random.randint(k_dst, (E,), 0, N, dtype=jnp.int32)
        deg = jax.ops.segment_sum(jnp.ones((E,), jnp.float32), dst_idx, num_segments=N)
        in_deg = jnp.maximum(deg, 1.0)
        stdv = 1.0 / np.sqrt(F_IN)
        W1 = jax.random.uniform(k_w1, (F_OUT, F_IN), jnp.float32, -stdv, stdv)
        b1 = jax.random.uniform(k_b1, (F_OUT,), jnp.float32, -stdv, stdv)
        W2 = jax.random.uniform(k_w2, (F_OUT, F_IN), jnp.float32, -stdv, stdv)
        b2 = jax.random.uniform(k_b2, (F_OUT,), jnp.float32, -stdv, stdv)
        return {'feat': feat, 'src_idx': src_idx, 'dst_idx': dst_idx, 'in_deg': in_deg, 'W1': W1, 'b1': b1, 'W2': W2, 'b2': b2}
    _L2_gnn_all = _L2_gnn_setup()
    _L2_gnn_in = {k: v for k, v in _L2_gnn_all.items() if k in ('W1', 'b1', 'W2', 'b2')}
    del _L2_gnn_all

    def _L3_gnn_setup():
        import jax, jax.numpy as jnp
        import numpy as np
        N_NODES, N_EDGES, D_IN, D_OUT = (6250, 50000, 512, 512)
        key = jax.random.key(seed)
        k = jax.random.split(key, 7)
        s = 1.0 / np.sqrt(D_IN)
        return {'x': jax.random.normal(k[0], (N_NODES, D_IN), dtype=jnp.float32), 'src': jax.random.randint(k[1], (N_EDGES,), 0, N_NODES), 'dst': jax.random.randint(k[2], (N_EDGES,), 0, N_NODES), 'W1': jax.random.uniform(k[3], (D_IN, D_OUT), jnp.float32, -s, s), 'b1': jax.random.uniform(k[4], (D_OUT,), jnp.float32, -s, s), 'W2': jax.random.uniform(k[5], (D_IN, D_OUT), jnp.float32, -s, s), 'b2': jax.random.uniform(k[6], (D_OUT,), jnp.float32, -s, s)}
    _L3_gnn_all = _L3_gnn_setup()
    _L3_gnn_in = {k: v for k, v in _L3_gnn_all.items() if k in ('W1', 'b1', 'W2', 'b2')}
    del _L3_gnn_all
    return {'x': x, 'src': src, 'dst': dst, 'edge_attr_64': edge_attr_64, 'L0_gnn_W1': _L0_gnn_in['W1'], 'L0_gnn_b1': _L0_gnn_in['b1'], 'L0_gnn_W2': _L0_gnn_in['W2'], 'L0_gnn_b2': _L0_gnn_in['b2'], 'L0_gnn_W3': _L0_gnn_in['W3'], 'L0_gnn_b3': _L0_gnn_in['b3'], 'L0_gnn_W4': _L0_gnn_in['W4'], 'L0_gnn_b4': _L0_gnn_in['b4'], 'L0_gnn_gamma': _L0_gnn_in['gamma'], 'L0_gnn_beta': _L0_gnn_in['beta'], 'L1_gnn_W_l': _L1_gnn_in['W_l'], 'L1_gnn_b_l': _L1_gnn_in['b_l'], 'L1_gnn_W_r': _L1_gnn_in['W_r'], 'L1_gnn_gamma': _L1_gnn_in['gamma'], 'L1_gnn_beta': _L1_gnn_in['beta'], 'L2_gnn_W1': _L2_gnn_in['W1'], 'L2_gnn_b1': _L2_gnn_in['b1'], 'L2_gnn_W2': _L2_gnn_in['W2'], 'L2_gnn_b2': _L2_gnn_in['b2'], 'L3_gnn_W1': _L3_gnn_in['W1'], 'L3_gnn_b1': _L3_gnn_in['b1'], 'L3_gnn_W2': _L3_gnn_in['W2'], 'L3_gnn_b2': _L3_gnn_in['b2']}

def reference(x, src, dst, edge_attr_64, L0_gnn_W1, L0_gnn_b1, L0_gnn_W2, L0_gnn_b2, L0_gnn_W3, L0_gnn_b3, L0_gnn_W4, L0_gnn_b4, L0_gnn_gamma, L0_gnn_beta, L1_gnn_W_l, L1_gnn_b_l, L1_gnn_W_r, L1_gnn_gamma, L1_gnn_beta, L2_gnn_W1, L2_gnn_b1, L2_gnn_W2, L2_gnn_b2, L3_gnn_W1, L3_gnn_b1, L3_gnn_W2, L3_gnn_b2):
    import jax
    import jax.numpy as jnp

    def _L0_gnn_ref(x, edge_index, edge_attr, W1, b1, W2, b2, W3, b3, W4, b4, gamma, beta):
        import jax, jax.numpy as jnp
        import numpy as np
        N_NODES = 2500
        N_EDGES = 40000
        HIDDEN = 512
        EDGE_DIM = 64
        LN_EPS = 1e-05

        def mish(x):
            return x * jnp.tanh(jax.nn.softplus(x))
        src, dst = (edge_index[0], edge_index[1])
        edge_feat = jnp.concatenate([x[src], x[dst], edge_attr], axis=-1)
        h = mish(edge_feat @ W1 + b1)
        messages = mish(h @ W2 + b2)
        agg = jax.ops.segment_sum(messages, dst, num_segments=x.shape[0])
        u = mish(jnp.concatenate([x, agg], axis=-1) @ W3 + b3)
        out = u @ W4 + b4
        y = x + out
        mu = jnp.mean(y, axis=-1, keepdims=True)
        var = jnp.mean(jnp.square(y - mu), axis=-1, keepdims=True)
        return (y - mu) * jax.lax.rsqrt(var + LN_EPS) * gamma + beta

    def _L1_gnn_ref(x, edge_index, W_l, b_l, W_r, gamma, beta):
        import jax, jax.numpy as jnp
        import numpy as np
        N, D, E = (6250, 512, 50000)
        EPS = 1e-05
        SLOPE = 0.01
        src, dst = (edge_index[0], edge_index[1])
        n = x.shape[0]
        summed = jax.ops.segment_sum(x[src], dst, num_segments=n)
        deg = jax.ops.segment_sum(jnp.ones((src.shape[0],), x.dtype), dst, num_segments=n)
        agg = summed / jnp.maximum(deg, 1.0)[:, None]
        out = agg @ W_l + b_l + x @ W_r
        mean = out.mean(axis=0)
        var = out.var(axis=0)
        out = (out - mean) * jax.lax.rsqrt(var + EPS) * gamma + beta
        out = jnp.where(out >= 0, out, SLOPE * out)
        out = out + x
        return out

    def _L2_gnn_ref(feat, src_idx, dst_idx, in_deg, W1, b1, W2, b2):
        import jax, jax.numpy as jnp
        import numpy as np
        N = 6250
        E = 100000
        F_IN = 512
        F_OUT = 512
        num_dst = in_deg.shape[0]
        agg = jax.ops.segment_sum(feat[src_idx], dst_idx, num_segments=num_dst)
        ah = agg / in_deg[:, None]
        out = jnp.einsum('nf,of->no', feat[:num_dst], W1) + b1 + jnp.einsum('nf,of->no', ah, W2) + b2
        return out

    def _L3_gnn_ref(x, src, dst, W1, b1, W2, b2):
        import jax, jax.numpy as jnp
        import numpy as np
        N_NODES, N_EDGES, D_IN, D_OUT = (6250, 50000, 512, 512)
        n_nodes = x.shape[0]
        msg_sum = jax.ops.segment_sum(x[src], dst, num_segments=n_nodes)
        counts = jax.ops.segment_sum(jnp.ones_like(dst, dtype=x.dtype), dst, num_segments=n_nodes)
        mean = msg_sum / jnp.maximum(counts, 1.0)[:, None]
        out = x @ W1 + b1 + ((x - mean) @ W2 + b2)
        return jnp.where((counts > 0)[:, None], out, x)
    edge_index = jnp.stack([src, dst])
    deg = jnp.maximum(jax.ops.segment_sum(jnp.ones(dst.shape, jnp.float32), dst, num_segments=1250), 1.0)
    x = _layernorm(x + _L0_gnn_ref(x, edge_index, edge_attr_64, L0_gnn_W1, L0_gnn_b1, L0_gnn_W2, L0_gnn_b2, L0_gnn_W3, L0_gnn_b3, L0_gnn_W4, L0_gnn_b4, L0_gnn_gamma, L0_gnn_beta), axis=-1)
    x = _layernorm(x + _L1_gnn_ref(x, edge_index, L1_gnn_W_l, L1_gnn_b_l, L1_gnn_W_r, L1_gnn_gamma, L1_gnn_beta), axis=-1)
    x = _layernorm(x + _L2_gnn_ref(x, src, dst, deg, L2_gnn_W1, L2_gnn_b1, L2_gnn_W2, L2_gnn_b2), axis=-1)
    x = _layernorm(x + _L3_gnn_ref(x, src, dst, L3_gnn_W1, L3_gnn_b1, L3_gnn_W2, L3_gnn_b2), axis=-1)
    return x

_drawn_inputs = setup_inputs


def setup_inputs(seed=0):
    import zlib

    import numpy as np

    out = dict(_drawn_inputs(seed))
    spreads = {'L0_gnn_b1': (0.0, 0.1),
     'L0_gnn_b2': (0.0, 0.1),
     'L0_gnn_b3': (0.0, 0.528),
     'L0_gnn_b4': (0.0, 0.458),
     'L0_gnn_gamma': (1.0, 0.2),
     'L0_gnn_beta': (0.0, 0.1),
     'L1_gnn_b_l': (0.0, 0.8),
     'L1_gnn_gamma': (1.0, 0.2),
     'L1_gnn_beta': (0.0, 0.1)}
    factors = {'L2_gnn_b1': 3.836, 'L2_gnn_b2': 3.711, 'L3_gnn_b1': 3.46, 'L3_gnn_b2': 3.369}
    for name, (base, spread) in spreads.items():
        noise = np.random.default_rng([zlib.crc32(name.encode()), seed]).standard_normal(out[name].shape)
        drawn = base * np.exp(spread * noise) if base else spread * noise
        out[name] = jnp.asarray(drawn.astype(out[name].dtype))
    for name, factor in factors.items():
        out[name] = (out[name] * factor).astype(out[name].dtype)
    return out
```

```python
import concourse.bass as bass
from concourse import mybir
from contextlib import ExitStack

F32 = mybir.dt.float32
F32R = mybir.dt.float32r
F16 = mybir.dt.float16
I32 = mybir.dt.int32
ACT = mybir.ActivationFunctionType
ALU = mybir.AluOpType
AX = mybir.AxisListType

P = 128
N = 1250
D = 512
KD = D // P
E = 21250
ED = 64
R = -(-N // P)
NP = R * P
LASTR = N - (R - 1) * P
TE = 4
BE = TE * P
NB = -(-E // BE)
NB += NB % 2
LASTE = E - (NB - 1) * BE
PADE = 1 << 20
DROWS = NP + P
MAXPASS = -(-N // P)
SRC_CHUNKS = [(0, 427), (427, 427), (854, NP - 854)]
EXACT = 4096
EPS = 1e-5
HALF_PI = 1.5707963267948966


class Blk:

    def __init__(self, k, lead, half, it2=None, total=NB):
        self.k, self.it2, self.total = k, it2, total
        self.lead, self.half = lead, half

    def at(self, off):
        return Blk(self.k + off, self.lead, self.half, self.it2, self.total)

    def real(self):
        return self.it2 is not None or 0 <= self.k < self.total

    def count(self, per, part=None):
        return self.lead * per + (self.k * per + (per if part is None else part))

    def slot_count(self, per):
        return self.half * per + (self.k // 2 + 1) * per

    @property
    def slot(self):
        return self.k % 2

    def number(self):
        return self.k if self.it2 is None else self.it2 + self.k


FIRST_STEP, LOOP_FROM, LOOP_TO, LAST_STEP = -3, 4, NB - 5, NB + 1
assert (LOOP_TO - LOOP_FROM + 1) % 2 == 0


def steps(eng, p, body):
    lead, half = eng.snap(p * NB), eng.snap(p * (NB // 2))
    for k in range(FIRST_STEP, LOOP_FROM):
        body(Blk(k, lead, half))
    with eng.Fori(0, (LOOP_TO - LOOP_FROM + 1) // 2) as it:
        it2 = eng.snap(it * 2)
        lead2, half2 = eng.snap(lead + it2), eng.snap(half + it)
        for u in range(2):
            body(Blk(LOOP_FROM + u, lead2, half2, it2))
    for k in range(LOOP_TO + 1, LAST_STEP + 1):
        body(Blk(k, lead, half))


def cols(r, n=D):
    return bass.ds(r * n, n)


def gnn(nc, x, src, dst, eaT, w0a, w0b, w0c, b01, w02, b02, w03, b03, w04, b04, g0, be0,
        w1l, b1l, w1r, g1, be1, w21, b21, w22, b22, w31, b31, w32, b32, out):
    top = ExitStack()
    with top:
        def sb(name, shape, dt=F32, ctx=top):
            return ctx.enter_context(nc.sbuf_tensor(name, shape, dt))

        def pb(name, shape, ctx):
            return ctx.enter_context(nc.psum_tensor(name, shape, F32))

        def sem(name):
            return top.enter_context(nc.semaphore(name))

        def dram(name, shape):
            return nc.dram_tensor(name, shape, F32, kind="Internal").ap()

        p_dram = dram("p_dram", [NP, D])
        q_dram = dram("q_dram", [NP, D])
        agg_dram = dram("agg_dram", [DROWS, D])
        adj_dram = dram("adj_dram", [DROWS, NP])
        adjT_dram = dram("adjT_dram", [R * P, NP])

        ident = sb("ident", [P, P])
        deg = sb("deg", [P, R])
        rdeg = sb("rdeg", [P, R])
        nrdeg = sb("nrdeg", [P, R])
        has = sb("has", [P, R])
        eps_col = sb("eps_col", [P, 1])
        half_pi = sb("half_pi", [P, 1])
        relT = sb("relT", [P, TE, NB])
        srcT = sb("srcT", [P, TE, NB])
        idx_all = sb("idx_all", [P, NB * 2 * TE], I32)
        base_f = sb("base_f", [1, NB])
        base_i = sb("base_i", [1, NB], I32)
        npass = sb("npass", [1, 1], I32)
        slow = sb("slow", [1, 1], I32)

        with ExitStack() as ctx:
            X = sb("X0", [P, R * D], F32, ctx)
            dst_i = sb("dst_i", [NB, BE], I32, ctx)
            src_i = sb("src_i", [NB, BE], I32, ctx)
            dst_f = sb("dst_f", [NB, BE], F32, ctx)
            src_f = sb("src_f", [NB, BE], F32, ctx)
            rel_f = sb("rel_f", [NB, BE], F32, ctx)
            dstc_f = sb("dstc_f", [NB, BE], F32, ctx)
            real_f = sb("real_f", [NB, BE], F32, ctx)
            bounds = sb("bounds", [NB, 2], F32, ctx)
            span = sb("span", [1, NB], F32, ctx)
            mspan = sb("mspan", [1, 1], F32, ctx)
            mspan_i = sb("mspan_i", [1, 1], I32, ctx)
            w_raw = sb("w_raw", [P, 2 * KD, D], F32, ctx)
            w_hi = sb("w_hi", [P, 2 * KD, D], F32R, ctx)
            w_lo = sb("w_lo", [P, 2 * KD, D], F32R, ctx)
            b1_bc = sb("b1_bc", [P, D], F32, ctx)
            zeros = sb("zeros", [P, NP], F32, ctx)
            xs = sb("xs", [P, 2, D], F32, ctx)
            xT_hi = sb("xT_hi", [P, 2, D], F32R, ctx)
            xT_lo = sb("xT_lo", [P, 2, D], F32R, ctx)
            p_sb = sb("p_sb", [P, 2, D], F32, ctx)
            q_sb = sb("q_sb", [P, 2, D], F32, ctx)
            ps_idx = pb("ps_idx", [P, 3, TE, NB], ctx)
            ps_row = pb("ps_row", [P, 2, 64], ctx)
            ps_t = [pb(f"ps_t{i}", [P, D], ctx) for i in range(2)]
            ps_p, ps_q = pb("ps_p", [P, D], ctx), pb("ps_q", [P, D], ctx)
            (z_ready, ident_ready, x_in, w_in, b_in, idx_in, pad_set, dve, w_split, idx_tr, xs_ready, t_ready,
             hi_ready, lo_ready, p_ready, q_ready, p_evac, q_evac, tab_out, zero_out, act_turn) = [
                sem("prep_" + n) for n in (
                    "z_ready", "ident_ready", "x_in", "w_in", "b_in", "idx_in", "pad_set", "dve", "w_split", "idx_tr",
                    "xs_ready", "t_ready", "hi_ready", "lo_ready", "p_ready", "q_ready", "p_evac", "q_evac",
                    "tab_out", "zero_out", "act_turn")]
            p_out = [sem(f"prep_p_out{i}") for i in range(2)]
            q_out = [sem(f"prep_q_out{i}") for i in range(2)]

            with nc.Block() as block:
                @block.sync
                def _(sp):
                    sp.wait_ge(pad_set, 1)
                    sp.dma_start(X[:, 0:(R - 1) * D].rearrange("p (r d) -> p r d", d=D), x[0:(R - 1) * P, :].rearrange("(r p) d -> p r d", p=P)).then_inc(x_in, 16)
                    sp.dma_start(X[0:LASTR, (R - 1) * D:], x[(R - 1) * P:N, :]).then_inc(x_in, 16)
                    sp.dma_start(w_raw[:, 0:KD, :], w0a.rearrange("(k p) d -> p k d", p=P)).then_inc(w_in, 16)
                    sp.dma_start(w_raw[:, KD:2 * KD, :], w0b.rearrange("(k p) d -> p k d", p=P)).then_inc(w_in, 16)
                    sp.dma_start(b1_bc[:, :], b01.rearrange("(a d) -> a d", a=1).to_broadcast([P, D])).then_inc(b_in, 16)
                    sp.wait_ge(z_ready, 1)
                    for r in range(DROWS // P):
                        sp.dma_start(adj_dram[r * P:(r + 1) * P, :], zeros[:, :]).then_inc(zero_out, 16)
                        sp.dma_start(agg_dram[r * P:(r + 1) * P, :], zeros[:, 0:D]).then_inc(zero_out, 16)

                    def store(half, u):
                        row = half * 2 * P + u * P
                        sp.wait_ge(p_evac, half * 2 + (u + 1))
                        sp.dma_start(p_dram[bass.ds(row, P), :], p_sb[:, u, :]).then_inc(p_out[u], 16)
                        sp.wait_ge(q_evac, half * 2 + (u + 1))
                        sp.dma_start(q_dram[bass.ds(row, P), :], q_sb[:, u, :]).then_inc(q_out[u], 16)
                    with sp.Fori(0, R // 2) as half:
                        store(half, 0)
                        store(half, 1)
                    for u in range(2):
                        sp.wait_ge(p_out[u], 16 * (R // 2))
                        sp.wait_ge(q_out[u], 16 * (R // 2))
                    sp.wait_ge(zero_out, 32 * (DROWS // P))

                @block.gpsimd
                def _(pool):
                    nc.gpsimd.memset(zeros[:, :], 0.0).then_inc(z_ready, 1)
                    nc.gpsimd.memset(ident[:, :], 0.0).then_inc(ident_ready, 1)
                    pool.wait_ge(ident_ready, 1)
                    nc.gpsimd.affine_select(out=ident[:, :], in_=ident[:, :], compare_op=ALU.not_equal, fill=1.0, base=0,
                                            pattern=[[-1, P]], channel_multiplier=1).then_inc(ident_ready, 1)

                @block.vector
                def _(dve_):
                    v = nc.vector
                    n = [0]

                    def then(ins):
                        n[0] += 1
                        ins.then_inc(dve, 1)
                        dve_.wait_ge(dve, n[0])

                    v.memset(X[:, (R - 1) * D:], 0.0).then_inc(pad_set, 1)
                    v.memset(dst_i[:, :], PADE).then_inc(pad_set, 1)
                    v.memset(src_i[:, :], 0).then_inc(pad_set, 1)
                    v.memset(eps_col[:, :], EPS)
                    v.memset(half_pi[:, :], HALF_PI)
                    dve_.wait_ge(idx_in, 64)
                    v.tensor_copy(src_f[:, :], src_i[:, :])
                    then(v.tensor_copy(dst_f[:, :], dst_i[:, :]))
                    v.tensor_reduce(bounds[:, 0:1], dst_f[:, :], AX.X, ALU.min)
                    then(v.scalar_tensor_tensor(real_f[:, :], dst_f[:, :], float(PADE), dst_f[:, :], ALU.is_lt, ALU.mult))
                    v.tensor_scalar(dstc_f[:, :], dst_f[:, :], float(N - 1), None, ALU.min)
                    then(v.tensor_reduce(bounds[:, 1:2], real_f[:, :], AX.X, ALU.max))
                    v.tensor_scalar(rel_f[:, :], dst_f[:, :], bounds[:, 0:1], None, ALU.subtract).then_inc(idx_tr, 1)
                    dve_.wait_ge(idx_tr, 2)
                    v.tensor_copy(idx_all[:, :].rearrange("p (b c) -> p c b", c=2 * TE)[:, 0:TE, :], ps_idx[:, 1, :, :])
                    v.tensor_copy(idx_all[:, :].rearrange("p (b c) -> p c b", c=2 * TE)[:, TE:, :], ps_idx[:, 2, :, :])
                    v.tensor_copy(srcT[:, :, :], ps_idx[:, 1, :, :])
                    v.tensor_copy(relT[:, :, :], ps_idx[:, 0, :, :])
                    then(v.tensor_copy(base_f[:, :], ps_row[0:1, 0, 0:NB]))
                    v.tensor_copy(base_i[:, :], base_f[:, :])
                    then(v.tensor_tensor(span[:, :], ps_row[0:1, 1, 0:NB], base_f[:, :], ALU.subtract))
                    then(v.tensor_reduce(mspan[:, :], span[:, :], AX.X, ALU.max))
                    then(v.tensor_copy(mspan_i[:, :], mspan[:, :]))
                    then(v.tensor_scalar(mspan_i[:, :], mspan_i[:, :], 7, None, ALU.arith_shift_right))
                    then(v.tensor_scalar(npass[:, :], mspan_i[:, :], 1.0, None, ALU.add))
                    dve_.wait_ge(w_split, 1)
                    v.tensor_tensor(w_lo[:, :, :], w_raw[:, :, :], w_hi[:, :, :].bitcast(F32), ALU.subtract).then_inc(w_split, 1)
                    dve_.wait_ge(b_in, 16)

                    def low(cnt, u):
                        dve_.wait_ge(hi_ready, cnt)
                        v.tensor_tensor(xT_lo[:, u, :], ps_t[u][:, :], xT_hi[:, u, :].bitcast(F32), ALU.subtract).then_inc(lo_ready, 1)

                    def bias(cnt, u, reuse):
                        if reuse is not None:
                            dve_.wait_ge(q_out[u], reuse)
                        dve_.wait_ge(q_ready, cnt)
                        v.tensor_tensor(q_sb[:, u, :], ps_q[:, :], b1_bc[:, :], ALU.add).then_inc(q_evac, 1)
                    low(1, 0)
                    low(2, 1)
                    bias(1, 0, None)
                    low(3, 0)
                    bias(2, 1, None)
                    with dve_.Fori(1, R // 2 - 1) as h:
                        low(h * 2 + 2, 1)
                        bias(h * 2 + 1, 0, h * 16)
                        low(h * 2 + 3, 0)
                        bias(h * 2 + 2, 1, h * 16)
                    low(R, 1)
                    bias(R - 1, 0, 16 * (R // 2 - 1))
                    bias(R, 1, 16 * (R // 2 - 1))

                @block.scalar
                def _(act):
                    act.wait_ge(pad_set, 3)
                    for t, (raw, dram_idx) in enumerate(((dst_i, dst), (src_i, src))):
                        act.dma_start(raw[0:NB - 1, :], dram_idx[0:(NB - 1) * BE].rearrange("(b e) -> b e", e=BE)).then_inc(idx_in, 16)
                        act.dma_start(raw[NB - 1:NB, 0:LASTE], dram_idx[(NB - 1) * BE:E].rearrange("(b e) -> b e", b=1)).then_inc(idx_in, 16)
                    act.wait_ge(w_in, 32)
                    nc.scalar.copy(w_hi[:, :, :], w_raw[:, :, :]).then_inc(w_split, 1)
                    act.wait_ge(x_in, 32)

                    def fetch(r, reuse, u):
                        if reuse is not None:
                            act.wait_ge(t_ready, reuse)
                            act.sem_inc(act_turn, 1)
                        nc.scalar.copy(xs[:, u, :], X[:, cols(r)]).then_inc(xs_ready, 1)

                    def high(cnt, u):
                        act.wait_ge(t_ready, cnt)
                        nc.scalar.copy(xT_hi[:, u, :], ps_t[u][:, :]).then_inc(hi_ready, 1)

                    def p_store(cnt, u, reuse):
                        if reuse is not None:
                            act.wait_ge(p_out[u], reuse)
                        act.wait_ge(p_ready, cnt)
                        nc.scalar.copy(p_sb[:, u, :], ps_p[:, :]).then_inc(p_evac, 1)
                    fetch(0, None, 0)
                    fetch(1, None, 1)
                    high(1, 0)
                    high(2, 1)
                    fetch(2, 1, 0)
                    p_store(1, 0, None)
                    high(3, 0)
                    fetch(3, 2, 1)
                    p_store(2, 1, None)
                    with act.Fori(1, R // 2 - 1) as h:
                        high(h * 2 + 2, 1)
                        fetch(h * 2 + 2, h * 2 + 1, 0)
                        p_store(h * 2 + 1, 0, h * 16)
                        high(h * 2 + 3, 0)
                        fetch(h * 2 + 3, h * 2 + 2, 1)
                        p_store(h * 2 + 2, 1, h * 16)
                    high(R, 1)
                    p_store(R - 1, 0, 16 * (R // 2 - 1))
                    p_store(R, 1, 16 * (R // 2 - 1))

                @block.tensor
                def _(pe):
                    pe.wait_ge(ident_ready, 2)
                    pe.wait_ge(idx_tr, 1)
                    for q, t in enumerate((rel_f, src_f, dstc_f)):
                        for c in range(TE):
                            nc.tensor.transpose(ps_idx[:, q, c, :], t[:, c * P:(c + 1) * P], ident[0:NB, 0:NB])
                    nc.tensor.transpose(ps_row[0:1, 0, 0:NB], bounds[:, 0:1], ident[0:NB, 0:NB])
                    nc.tensor.transpose(ps_row[0:1, 1, 0:NB], bounds[:, 1:2], ident[0:NB, 0:NB]).then_inc(idx_tr, 1)

                    def turn(cnt, u):
                        pe.wait_ge(xs_ready, cnt)
                        for k in range(KD):
                            last = nc.tensor.transpose(ps_t[u][:, k * P:(k + 1) * P], xs[:, u, k * P:(k + 1) * P], ident[:, :])
                        last.then_inc(t_ready, 1)

                    def products(cnt, u, reuse):
                        pe.wait_ge(lo_ready, cnt)
                        for j, (ps, ready, evac) in enumerate(((ps_p, p_ready, p_evac), (ps_q, q_ready, q_evac))):
                            if reuse is not None:
                                pe.wait_ge(evac, reuse)
                            for k in range(KD):
                                for i, (a, w) in enumerate(((xT_hi, w_hi), (xT_hi, w_lo), (xT_lo, w_hi))):
                                    last = nc.tensor.matmul(ps[:, :], a[:, u, k * P:(k + 1) * P], w[:, j * KD + k, :],
                                                            start=(k == 0 and i == 0), stop=(k == KD - 1 and i == 2))
                            last.then_inc(ready, 1)
                    turn(1, 0)
                    turn(2, 1)
                    pe.wait_ge(w_split, 2)
                    products(1, 0, None)
                    turn(3, 0)
                    products(2, 1, 1)
                    with pe.Fori(1, R // 2 - 1) as h:
                        turn(h * 2 + 2, 1)
                        products(h * 2 + 1, 0, h * 2)
                        turn(h * 2 + 3, 0)
                        products(h * 2 + 2, 1, h * 2 + 1)
                    turn(R, 1)
                    products(R - 1, 0, R - 2)
                    products(R, 1, R - 1)

        edge_phase(nc, sb, pb, sem, ident, half_pi, relT, srcT, idx_all, base_f, base_i, npass,
                   p_dram, q_dram, agg_dram, adj_dram, eaT, w0c, w02, b02)
        X = sb("X", [P, R * D])
        first_layer(nc, sb, pb, sem, ident, half_pi, eps_col, X, x, deg, rdeg, nrdeg, has, slow, agg_dram,
                    adj_dram, adjT_dram, w03, b03, w04, b04, g0, be0)
        sems = [sem("mean_" + n) for n in MEAN_SEMS]
        layers = ((w1r, w1l, [b1l, g1, be1]), (w21, w22, [b21, b22]), (w31, w32, [b31, b32]))
        for layer, (w_x, w_m, vecs) in enumerate(layers, 1):
            if layer > 1:
                with nc.Block() as block:
                    @block.sync
                    def _(sp):
                        for s in sems:
                            sp.sem_clear(s)
            mean_layer(nc, sb, pb, sem, sems, layer, ident, eps_col, X, rdeg, nrdeg, has, slow, adjT_dram, w_x, w_m, vecs, out)


def edge_phase(nc, sb, pb, sem, ident, half_pi, relT, srcT, idx_all, base_f, base_i, npass,
               p_dram, q_dram, agg_dram, adj_dram, eaT, w0c, w02, b02):
    with ExitStack() as ctx:
        w_raw = sb("e_w_raw", [P, KD, D], F32, ctx)
        w2_hi, w2_lo = sb("w2_hi", [P, KD, D], F32R, ctx), sb("w2_lo", [P, KD, D], F32R, ctx)
        wc_raw = sb("wc_raw", [P, D], F32, ctx)
        wc_hi, wc_lo = sb("wc_hi", [P, D], F32R, ctx), sb("wc_lo", [P, D], F32R, ctx)
        b2 = sb("b2", [P, D], F32, ctx)
        iota_src = sb("iota_src", [P, NP], F16, ctx)
        ea_raw = sb("ea_raw", [P, 2, BE], F32, ctx)
        ea_parts = sb("ea_parts", [P, 2, BE], F32R, ctx)
        idx = sb("idx", [P, 2, 2 * TE], I32, ctx)
        G = sb("G", [P, 2, TE * D], F32, ctx)
        x1 = sb("x1", [P, 2, TE * D], F32, ctx)
        h1 = sb("h1", [P, 2, TE * D], F32, ctx)
        hT_hi = sb("hT_hi", [P, 2, D], F32R, ctx)
        hT_lo = sb("hT_lo", [P, 2, D], F32R, ctx)
        x2 = sb("x2", [P, 2, TE * D], F32, ctx)
        m2 = sb("m2", [P, TE * D], F32, ctx)
        m_hi, m_lo = sb("m_hi", [P, TE * D], F32R, ctx), sb("m_lo", [P, TE * D], F32R, ctx)
        oh_src = sb("oh_src", [P, 2, TE, NP], F16, ctx)
        oh_win = sb("oh_win", [P, 2, TE, P], F16, ctx)
        oh_winr = sb("oh_winr", [P, 2, TE, P], F32R, ctx)
        agg_sb = sb("agg_sb", [P, 2, D], F32, ctx)
        adj_sb = sb("adj_sb", [P, 2, NP], F32, ctx)
        ps_pre, ps_tr, ps_x2 = ([pb(f"{n}{i}", [P, D], ctx) for i in range(2)] for n in ("ps_pre", "ps_tr", "ps_x2"))
        ps_adj, ps_agg = pb("ps_adj", [P, D], ctx), pb("ps_agg", [P, D], ctx)

        (w_in, iota_ready, x2_evac, w_split, dve, pre_ready, x1_ready, sig1, atan1, t1_ready, h1_ready, tr_ready,
         hi_ready, hT_ready, x2_ready, sig2, atan2, t2_ready, m2_ready, mhi_ready, m_ready, oh_ready, adj_ready,
         adj_evac, agg_ready, agg_evac, summed, ea_hi, ea_ready, idx_ready, shifted, turn) = [
            sem("edge_" + n) for n in (
                "w_in", "iota_ready", "x2_evac", "w_split", "dve", "pre_ready", "x1_ready", "sig1", "atan1", "t1_ready",
                "h1_ready", "tr_ready", "hi_ready", "hT_ready", "x2_ready", "sig2", "atan2", "t2_ready", "m2_ready",
                "mhi_ready", "m_ready", "oh_ready", "adj_ready", "adj_evac", "agg_ready", "agg_evac", "summed",
                "ea_hi", "ea_ready", "idx_ready", "shifted", "turn")]
        ea_in = [sem(f"edge_ea_in{i}") for i in range(2)]
        p_in = [sem(f"edge_p_in{i}") for i in range(2)]
        q_in = [sem(f"edge_q_in{i}") for i in range(2)]

        def passes(eng, body):
            n = eng.value_load(npass[0:1, 0:1], min_val=1, max_val=MAXPASS)
            with eng.Fori(0, n) as p:
                body(p)
                eng.wait_ge(summed, p * (NB * 32) + NB * 32)
                eng.sem_inc(turn, 1)

        with nc.Block() as block:
            @block.sync
            def _(sp):
                sp.dma_start(w_raw[:, :, :], w02.rearrange("(k p) d -> p k d", p=P)).then_inc(w_in, 16)
                for half in range(2):
                    sp.dma_start(wc_raw[half * ED:(half + 1) * ED, :], w0c).then_inc(w_in, 16)

                sp.dma_start(b2[:, :], bcast(b02)).then_inc(w_in, 16)

                def step(s):
                    b = s.at(3)
                    if b.real():
                        if b.at(-2).real():
                            sp.wait_ge(ea_ready, b.at(-2).count(1))
                        for half in range(2):
                            sp.dma_start(ea_raw[half * ED:(half + 1) * ED, b.slot, :],
                                         eaT[:, bass.ds(b.number() * BE, BE)]).then_inc(ea_in[b.slot], 16)

                def one_pass(p):
                    steps(sp, p, step)
                passes(sp, one_pass)

            @block.gpsimd
            def _(pool):
                g = nc.gpsimd
                g.iota(iota_src[:, :], pattern=[[1, NP]], base=0, channel_multiplier=0,
                       allow_small_or_imprecise_dtypes=True).then_inc(iota_ready, 1)

                def wait(s, v):
                    pool.wait_ge(s, v)
                    pool.sem_inc(turn, 1)

                def step(s):
                    b = s.at(3)
                    if b.real():
                        if b.at(-2).real():
                            wait(x1_ready, b.at(-2).count(TE))
                        g.tensor_copy(idx[:, b.slot, :], idx_all[:, bass.ds(b.number() * (2 * TE), 2 * TE)]).then_inc(idx_ready, 1)
                        wait(idx_ready, b.count(1))
                        for c in range(TE):
                            g.indirect_dma_start(G[:, b.slot, c * D:(c + 1) * D], None, p_dram,
                                                 bass.IndirectOffsetOnAxis(ap=idx[:, b.slot, c:c + 1], axis=0)).then_inc(p_in[b.slot], 16)
                        wait(p_in[b.slot], b.slot_count(16 * TE))
                        for c in range(TE):
                            g.indirect_dma_start(G[:, b.slot, c * D:(c + 1) * D], None, q_dram,
                                                 bass.IndirectOffsetOnAxis(ap=idx[:, b.slot, TE + c:TE + c + 1], axis=0),
                                                 compute_op=ALU.add).then_inc(q_in[b.slot], 16)
                    b = s.at(-1)
                    if b.real():
                        for half in range(2):
                            c = slice(half * 2 * D, (half + 1) * 2 * D)
                            if half == 0 and b.at(-1).real():
                                wait(agg_ready, b.at(-1).count(1))
                            wait(m2_ready, b.count(TE, 2 * half + 2))
                            g.tensor_scalar(m_hi[:, c], m2[:, c], 1.0, 0.0, ALU.mult, ALU.add).then_inc(mhi_ready, 1)
                            pool.wait_ge(mhi_ready, b.count(2, half + 1))
                            g.tensor_tensor(m_lo[:, c], m2[:, c], m_hi[:, c].bitcast(F32), ALU.subtract).then_inc(m_ready, 1)
                    b = s.at(-2)
                    if b.real():
                        if b.at(-1).real():
                            wait(summed, b.at(-1).count(32))
                        wait(adj_evac, b.count(len(SRC_CHUNKS)))
                        wait(agg_evac, b.count(1))
                        row = g.value_load(base_i[0:1, bass.ds(b.number(), 1)], min_val=0, max_val=NP)
                        g.dma_start(adj_dram[bass.ds(row, P), :], adj_sb[:, b.slot, :], accum_op=ALU.add).then_inc(summed, 16)
                        g.dma_start(agg_dram[bass.ds(row, P), :], agg_sb[:, b.slot, :], accum_op=ALU.add).then_inc(summed, 16)

                def one_pass(p):
                    wait(shifted, p + 1)
                    steps(pool, p, step)
                passes(pool, one_pass)

            def passes_dve(dve_, body):
                v = nc.vector
                n = dve_.value_load(npass[0:1, 0:1], min_val=1, max_val=MAXPASS)
                with dve_.Fori(0, n) as p:
                    body(p)
                    dve_.wait_ge(summed, p * (NB * 32) + NB * 32)
                    v.tensor_scalar(relT[:, :, :], relT[:, :, :], float(P), None, ALU.subtract)
                    v.tensor_scalar(base_f[:, :], base_f[:, :], float(P), float(NP), ALU.add, ALU.min).then_inc(dve, 1)
                    dve_.wait_ge(dve, p + 1)
                    v.tensor_copy(base_i[:, :], base_f[:, :]).then_inc(shifted, 1)

            @block.vector
            def _(dve_):
                v = nc.vector
                dve_.wait_ge(w_in, 16 * 4)
                dve_.wait_ge(w_split, 2)
                v.tensor_tensor(w2_lo[:, :, :], w_raw[:, :, :], w2_hi[:, :, :].bitcast(F32), ALU.subtract)
                v.tensor_tensor(wc_lo[:, :], wc_raw[:, :], wc_hi[:, :].bitcast(F32), ALU.subtract).then_inc(w_split, 1)
                dve_.wait_ge(iota_ready, 1)

                def step(s):
                    b = s.at(3)
                    if b.real():
                        dve_.wait_ge(ea_in[b.slot], b.slot_count(32))
                        if b.at(-2).real():
                            dve_.wait_ge(pre_ready, b.at(-2).count(TE))
                        v.tensor_copy(ea_parts[:, b.slot, :], ea_raw[:, b.slot, :]).then_inc(ea_hi, 1)
                        dve_.wait_ge(ea_hi, b.count(1))
                        v.tensor_tensor(ea_parts[ED:P, b.slot, :], ea_raw[ED:P, b.slot, :],
                                        ea_parts[ED:P, b.slot, :].bitcast(F32), ALU.subtract).then_inc(ea_ready, 1)
                    for c in range(TE):
                        b, e = (s, c - 1) if c > 0 else (s.at(-1), TE - 1)
                        if b.real():
                            dve_.wait_ge(x2_ready, b.count(TE, e + 1))
                            v.tensor_tensor(x2[:, b.slot, cols(e)], ps_x2[e % 2][:, :], b2[:, :], ALU.add).then_inc(x2_evac, 1)
                        b = s.at(2)
                        if b.real():
                            if c == 0:
                                dve_.wait_ge(q_in[b.slot], b.slot_count(16 * TE))
                            dve_.wait_ge(pre_ready, b.count(TE, c + 1))
                            v.tensor_tensor(x1[:, b.slot, cols(c)], ps_pre[c % 2][:, :], G[:, b.slot, cols(c)], ALU.add).then_inc(x1_ready, 1)
                        b, e = (s, c + 1) if c < TE - 1 else (s.at(1), 0)
                        if b.real():
                            dve_.wait_ge(hi_ready, b.count(TE, e + 1))
                            v.tensor_tensor(hT_lo[:, e % 2, :], ps_tr[e % 2][:, :], hT_hi[:, e % 2, :].bitcast(F32), ALU.subtract).then_inc(hT_ready, 1)
                        b = s.at(-1)
                        if b.real():
                            if c == 0 and b.at(-2).real():
                                dve_.wait_ge(adj_ready, b.at(-2).count(len(SRC_CHUNKS)))
                                dve_.sem_inc(turn, 1)
                            i = bass.ds(b.number(), 1)
                            v.tensor_scalar(oh_src[:, b.slot, c, :], iota_src[:, :], srcT[:, c, i], None, ALU.is_equal)
                            v.tensor_scalar(oh_win[:, b.slot, c, :], iota_src[:, 0:P], relT[:, c, i], None, ALU.is_equal)
                            v.tensor_scalar(oh_winr[:, b.slot, c, :], iota_src[:, 0:P], relT[:, c, i], None, ALU.is_equal).then_inc(oh_ready, 1)
                        b = s.at(-2)
                        if b.real() and c == 1:
                            if b.at(-2).real():
                                dve_.wait_ge(summed, b.at(-2).count(32))
                            dve_.wait_ge(agg_ready, b.count(1))
                            v.tensor_copy(agg_sb[:, b.slot, :], ps_agg[:, :]).then_inc(agg_evac, 1)
                        b = s.at(-1)
                        if b.real() and c in (1, 2):
                            dve_.wait_ge(t2_ready, b.count(2, c))
                            for e in (2 * c - 2, 2 * c - 1):
                                v.tensor_tensor(m2[:, cols(e)], x2[:, b.slot, cols(e)], m2[:, cols(e)], ALU.mult).then_inc(m2_ready, 1)
                        b = s.at(1)
                        if b.real() and c == 2:
                            for e in range(TE):
                                if e % 2 == 0:
                                    dve_.wait_ge(t1_ready, b.count(2, e // 2 + 1))
                                v.tensor_tensor(h1[:, b.slot, cols(e)], x1[:, b.slot, cols(e)], h1[:, b.slot, cols(e)],
                                                ALU.mult).then_inc(h1_ready, 1)

                dve_.sem_inc(shifted, 1)

                def one_pass(p):
                    steps(dve_, p, step)
                passes_dve(dve_, one_pass)

            @block.scalar
            def _(act):
                a = nc.scalar
                act.wait_ge(w_in, 16 * 4)
                a.copy(w2_hi[:, :, :], w_raw[:, :, :]).then_inc(w_split, 1)
                a.copy(wc_hi[:, :], wc_raw[:, :]).then_inc(w_split, 1)

                def evac_adj(b, j):
                    if b.real():
                        if j == 0 and b.at(-2).real():
                            act.wait_ge(summed, b.at(-2).count(32))
                        o, n = SRC_CHUNKS[j]
                        act.wait_ge(adj_ready, b.count(len(SRC_CHUNKS), j + 1))
                        a.copy(adj_sb[:, b.slot, o:o + n], ps_adj[:, 0:n]).then_inc(adj_evac, 1)

                def high(b, e):
                    if b.real():
                        act.wait_ge(tr_ready, b.count(TE, e + 1))
                        a.copy(hT_hi[:, e % 2, :], ps_tr[e % 2][:, :]).then_inc(hi_ready, 1)

                def arctan(b, half, x_, ready, free, t_, sig, atan):
                    if b.real():
                        c = slice(half * 2 * D, (half + 1) * 2 * D)
                        act.wait_ge(ready, b.count(TE, 2 * half + 2))
                        free(b, half)
                        a.activation(t_(b)[:, c], x_[:, b.slot, c], ACT.Sigmoid, scale=-1.0).then_inc(sig, 1)
                        act.wait_ge(sig, b.count(2, half + 1))
                        a.activation(t_(b)[:, c], t_(b)[:, c], ACT.Arctan).then_inc(atan, 1)

                def sine(b, half, t_, atan, ready):
                    if b.real():
                        c = slice(half * 2 * D, (half + 1) * 2 * D)
                        act.wait_ge(atan, b.count(2, half + 1))
                        a.activation(t_(b)[:, c], t_(b)[:, c], ACT.Sin, scale=-2.0, bias=half_pi[:, :]).then_inc(ready, 1)

                def h1_free(b, half):
                    if b.at(-2).real():
                        act.wait_ge(tr_ready, b.at(-2).count(TE))

                def m2_free(b, half):
                    if b.at(-1).real():
                        act.wait_ge(m_ready, b.at(-1).count(2, half + 1))

                def arctan1(b, half):
                    arctan(b, half, x1, x1_ready, h1_free, lambda b: h1[:, b.slot, :], sig1, atan1)

                def arctan2(b, half):
                    arctan(b, half, x2, x2_evac, m2_free, lambda b: m2, sig2, atan2)

                def sine1(b, half):
                    sine(b, half, lambda b: h1[:, b.slot, :], atan1, t1_ready)

                def sine2(b, half):
                    sine(b, half, lambda b: m2, atan2, t2_ready)

                def step(s):
                    arctan2(s.at(-1), 1)
                    high(s, 1)
                    sine2(s.at(-1), 0)
                    sine2(s.at(-1), 1)
                    evac_adj(s.at(-2), 0)
                    high(s, 2)
                    sine1(s.at(1), 0)
                    sine1(s.at(1), 1)
                    evac_adj(s.at(-2), 1)
                    high(s, 3)
                    arctan1(s.at(2), 0)
                    arctan2(s, 0)
                    evac_adj(s.at(-2), 2)
                    high(s.at(1), 0)
                    arctan1(s.at(2), 1)

                def one_pass(p):
                    steps(act, p, step)
                passes(act, one_pass)

            @block.tensor
            def _(pe):
                t = nc.tensor
                pe.wait_ge(w_split, 3)

                def bank_free(sem, b, c):
                    if c >= 2:
                        pe.wait_ge(sem, b.count(TE, c - 1))
                    elif b.at(-1).real():
                        pe.wait_ge(sem, b.at(-1).count(TE, c + 3))

                def rest_of_first(b, c):
                    if c == 0:
                        pe.wait_ge(ea_ready, b.count(1))
                    bank_free(x1_ready, b, c)
                    for i, w in enumerate((wc_hi, wc_lo)):
                        last = t.matmul(ps_pre[c % 2][:, :], ea_parts[:, b.slot, c * P:(c + 1) * P], w[:, :], start=(i == 0), stop=(i == 1))
                    last.then_inc(pre_ready, 1)

                def adjacency(b, j):
                    chunks = len(SRC_CHUNKS)
                    if j > 0:
                        pe.wait_ge(adj_evac, b.count(chunks, j))
                    elif b.at(-1).real():
                        pe.wait_ge(adj_evac, b.at(-1).count(chunks))
                    o, n = SRC_CHUNKS[j]
                    for k in range(TE):
                        last = t.matmul(ps_adj[:, 0:n], oh_win[:, b.slot, k, :], oh_src[:, b.slot, k, o:o + n], start=(k == 0), stop=(k == TE - 1))
                    last.then_inc(adj_ready, 1)

                def sums(b):
                    pe.wait_ge(oh_ready, b.count(TE))
                    pe.wait_ge(m_ready, b.count(2))
                    if b.at(-1).real():
                        pe.wait_ge(agg_evac, b.at(-1).count(1))
                    for k in range(TE):
                        for i, m in enumerate((m_hi, m_lo)):
                            last = t.matmul(ps_agg[:, :], oh_winr[:, b.slot, k, :], m[:, cols(k)], start=(k == 0 and i == 0),
                                            stop=(k == TE - 1 and i == 1))
                    last.then_inc(agg_ready, 1)

                def turn_h(b, c):
                    pe.wait_ge(h1_ready, b.count(TE, c + 1))
                    bank_free(hT_ready, b, c)
                    for k in range(KD):
                        last = t.transpose(ps_tr[c % 2][:, k * P:(k + 1) * P], h1[:, b.slot, c * D + k * P:c * D + (k + 1) * P], ident[:, :])
                    last.then_inc(tr_ready, 1)

                def second(b, c):
                    pe.wait_ge(hT_ready, b.count(TE, c + 1))
                    bank_free(x2_evac, b, c)
                    three_products(nc, ps_x2[c % 2], hT_hi[:, c % 2, :], hT_lo[:, c % 2, :], w2_hi, w2_lo, True, True).then_inc(x2_ready, 1)

                def step(s):
                    for c in range(TE):
                        if s.at(2).real():
                            rest_of_first(s.at(2), c)
                        if s.at(-2).real():
                            if c == 0:
                                sums(s.at(-2))
                            else:
                                adjacency(s.at(-2), c - 1)
                        b = s if c < TE - 1 else s.at(1)
                        if b.real():
                            turn_h(b, (c + 1) % TE)
                        if s.real():
                            second(s, c)

                def one_pass(p):
                    steps(pe, p, step)
                passes(pe, one_pass)


def row_steps(eng, first, last, lo, hi, body):
    for k in range(first, lo):
        body(Blk(k, 0, 0, total=R))
    with eng.Fori(0, hi - lo + 1) as it:
        body(Blk(lo, it, it, it, total=R))
    for k in range(hi + 1, last + 1):
        body(Blk(k, 0, 0, total=R))


def three_products(nc, ps, a_hi, a_lo, w_hi, w_lo, first, last):
    for k in range(KD):
        for i, (a, w) in enumerate(((a_hi, w_hi), (a_hi, w_lo), (a_lo, w_hi))):
            ins = nc.tensor.matmul(ps[:, :], a[:, k * P:(k + 1) * P], w[:, k, :], start=(first and k == 0 and i == 0),
                                   stop=(last and k == KD - 1 and i == 2))
    return ins


def bcast(vec):
    return vec.rearrange("(a d) -> a d", a=1).to_broadcast([P, D])


def first_layer(nc, sb, pb, sem, ident, half_pi, eps_col, X, x, deg, rdeg, nrdeg, has, slow, agg_dram,
                adj_dram, adjT_dram, w03, b03, w04, b04, g0, be0):
    with ExitStack() as ctx:
        w_raw = sb("n0_w_raw", [P, 3 * KD, D], F32, ctx)
        w_hi, w_lo = sb("n0_w_hi", [P, 3 * KD, D], F32R, ctx), sb("n0_w_lo", [P, 3 * KD, D], F32R, ctx)
        b3, b4 = sb("b3", [P, D], F32, ctx), sb("b4", [P, D], F32, ctx)
        gam, bet = sb("n0_gam", [P, D], F32, ctx), sb("n0_bet", [P, D], F32, ctx)
        xs, ag = sb("n0_xs", [P, D], F32, ctx), sb("n0_ag", [P, D], F32, ctx)
        T_hi = [sb(f"n0_T_hi{i}", [P, D], F32R, ctx) for i in range(2)]
        T_lo = [sb(f"n0_T_lo{i}", [P, D], F32R, ctx) for i in range(2)]
        adj_in, adjT_sb = sb("adj_in", [P, NP], F32, ctx), sb("adjT_sb", [P, NP], F32, ctx)
        Z, TH = sb("Z", [P, R * D], F32, ctx), sb("TH", [P, R * D], F32, ctx)
        us, y = sb("n0_us", [P, D], F32, ctx), sb("n0_y", [P, D], F32, ctx)
        st, mv = sb("n0_st", [P, 6], F32, ctx), sb("n0_mv", [P, 2], F32, ctx)
        sd, rs = sb("n0_sd", [P, 1], F32, ctx), sb("n0_rs", [P, 1], F32, ctx)
        mdeg, mdeg1, gt = sb("mdeg", [P, 1], F32, ctx), sb("mdeg1", [1, 1], F32, ctx), sb("gt", [1, 1], F32, ctx)
        ps_T = [pb(f"n0_ps_T{i}", [P, D], ctx) for i in range(2)]
        ps_adj = pb("n0_ps_adj", [P, NP], ctx)
        ps_out, ps_deg = pb("n0_ps_out", [P, D], ctx), pb("n0_ps_deg", [1, P], ctx)
        x_in = sem("n0_x_in")
        (w_in, c_in, w_split, xs_ready, T_ready, hi_ready, lo_ready, z_out, z_ready, sig, atan, t_ready, a_in, aT_ready,
         aT_evac, aT_out, d_ready, dve, deg_tr, us_ready, u_T, u_hi, u_lo, y_ready, y_used, sd_ready, turn, ag_in,
         c_dve, mv_ready) = [
            sem("n0_" + n) for n in (
                "w_in", "c_in", "w_split", "xs_ready", "T_ready", "hi_ready", "lo_ready", "z_out", "z_ready", "sig", "atan",
                "t_ready", "a_in", "aT_ready", "aT_evac", "aT_out", "d_ready", "dve", "deg_tr", "us_ready", "u_T", "u_hi",
                "u_lo", "y_ready", "y_used", "sd_ready", "turn", "ag_in", "c_dve", "mv_ready")]

        with nc.Block() as block:
            @block.sync
            def _(sp):
                sp.wait_ge(x_in, 1)
                sp.dma_start(X[:, 0:(R - 1) * D].rearrange("p (r d) -> p r d", d=D), x[0:(R - 1) * P, :].rearrange("(r p) d -> p r d", p=P)).then_inc(x_in, 16)
                sp.dma_start(X[0:LASTR, (R - 1) * D:], x[(R - 1) * P:N, :]).then_inc(x_in, 16)
                sp.dma_start(w_raw[:, 0:2 * KD, :], w03.rearrange("(k p) d -> p k d", p=P)).then_inc(w_in, 16)
                sp.dma_start(w_raw[:, 2 * KD:, :], w04.rearrange("(k p) d -> p k d", p=P)).then_inc(w_in, 16)
                for t, b in ((b3, b03), (b4, b04), (gam, g0), (bet, be0)):
                    sp.dma_start(t[:, :], bcast(b)).then_inc(c_in, 16)

                def step(s):
                    b = s.at(1)
                    if b.real():
                        if b.k > 0 or b.it2 is not None:
                            sp.wait_ge(T_ready, b.at(-1).count(1))
                        sp.dma_start(ag[:, :], agg_dram[bass.ds(b.number() * P, P), :]).then_inc(ag_in, 16)
                        if b.k > 0 or b.it2 is not None:
                            sp.wait_ge(aT_ready, b.at(-1).count(1))
                            sp.wait_ge(d_ready, b.at(-1).count(1))
                        sp.dma_start(adj_in[:, :], adj_dram[bass.ds(b.number() * P, P), :]).then_inc(a_in, 16)
                    if s.real():
                        sp.wait_ge(aT_evac, s.count(1))
                        sp.dma_start(adjT_dram[bass.ds(s.number() * P, P), :], adjT_sb[:, :]).then_inc(aT_out, 16)
                row_steps(sp, -1, R - 1, 0, R - 2, step)
                sp.wait_ge(aT_out, 16 * R)

            @block.scalar
            def _(act):
                a = nc.scalar
                act.wait_ge(w_in, 32)
                a.copy(w_hi[:, :, :], w_raw[:, :, :]).then_inc(w_split, 1)
                act.wait_ge(x_in, 33)

                def step(s):
                    b = s.at(1)
                    if b.real():
                        if b.k > 0 or b.it2 is not None:
                            act.wait_ge(T_ready, b.at(-1).count(1))
                            act.sem_inc(turn, 1)
                        a.copy(xs[:, :], X[:, cols(b.number())]).then_inc(xs_ready, 1)
                    if s.real():
                        act.wait_ge(aT_ready, s.count(1))
                        if s.k > 0 or s.it2 is not None:
                            act.wait_ge(aT_out, s.at(-1).count(16))
                        a.copy(adjT_sb[:, :], ps_adj[:, :]).then_inc(aT_evac, 1)
                row_steps(act, -1, R - 1, 1, R - 2, step)
                act.wait_ge(z_ready, R)
                for h in range(2):
                    c = slice(h * (R // 2) * D, (h + 1) * (R // 2) * D)
                    a.activation(TH[:, c], Z[:, c], ACT.Sigmoid, scale=-1.0).then_inc(sig, 1)
                    act.wait_ge(sig, h + 1)
                    a.activation(TH[:, c], TH[:, c], ACT.Arctan).then_inc(atan, 1)
                for h in range(2):
                    c = slice(h * (R // 2) * D, (h + 1) * (R // 2) * D)
                    act.wait_ge(atan, h + 1)
                    a.activation(TH[:, c], TH[:, c], ACT.Sin, scale=-2.0, bias=half_pi[:, :]).then_inc(t_ready, 1)

                def step2(s):
                    act.wait_ge(u_T, s.count(1))
                    a.copy(T_hi[0][:, :], ps_T[0][:, :]).then_inc(u_hi, 1)
                    for j in range(2):
                        act.wait_ge(mv_ready, s.count(2, j + 1))
                        a.activation(sd[:, :], mv[:, 1:2], ACT.Sqrt, bias=eps_col[:, :]).then_inc(sd_ready, 1)
                row_steps(act, 0, R - 1, 0, R - 1, step2)

            @block.vector
            def _(dve_):
                v = nc.vector
                v.memset(X[:, (R - 1) * D:], 0.0).then_inc(x_in, 1)
                dve_.wait_ge(w_split, 1)
                v.tensor_tensor(w_lo[:, :, :], w_raw[:, :, :], w_hi[:, :, :].bitcast(F32), ALU.subtract).then_inc(w_split, 1)
                dve_.wait_ge(c_in, 64)

                def z_of(b):
                    dve_.wait_ge(z_out, b.count(1))
                    v.tensor_tensor(Z[:, cols(b.number())], ps_out[:, :], b3[:, :], ALU.add).then_inc(z_ready, 1)

                def step(s):
                    if s.real():
                        dve_.wait_ge(T_ready, s.count(1))
                        for i in range(2):
                            v.tensor_copy(T_hi[i][:, :], ps_T[i][:, :]).then_inc(hi_ready, 1)
                            dve_.wait_ge(hi_ready, s.count(2, i + 1))
                            v.tensor_tensor(T_lo[i][:, :], ps_T[i][:, :], T_hi[i][:, :].bitcast(F32), ALU.subtract).then_inc(lo_ready, 1)
                        dve_.wait_ge(a_in, s.count(16))
                        dve_.sem_inc(turn, 1)
                        v.tensor_reduce(deg[:, bass.ds(s.number(), 1)], adj_in[:, :], AX.X, ALU.add).then_inc(d_ready, 1)
                    if s.k >= 1 or s.it2 is not None:
                        z_of(s.at(-1))
                row_steps(dve_, 0, R, 1, R - 1, step)
                v.wait_ge(d_ready, R)
                v.tensor_reduce(mdeg[:, :], deg[:, :], AX.X, ALU.max).then_inc(deg_tr, 1)
                v.tensor_scalar(has[:, :], deg[:, :], 0.0, None, ALU.is_gt)
                v.tensor_scalar(rdeg[:, :], deg[:, :], 1.0, None, ALU.max).then_inc(c_dve, 1)
                dve_.wait_ge(c_dve, 1)
                v.reciprocal(rdeg[:, :], rdeg[:, :]).then_inc(c_dve, 1)
                dve_.wait_ge(c_dve, 2)
                v.tensor_scalar(nrdeg[:, :], rdeg[:, :], -1.0, None, ALU.mult)
                dve_.wait_ge(deg_tr, 2)
                v.tensor_reduce(mdeg1[:, :], ps_deg[:, :], AX.X, ALU.max).then_inc(c_dve, 1)
                dve_.wait_ge(c_dve, 3)
                v.tensor_scalar(gt[:, :], mdeg1[:, :], float(EXACT), None, ALU.is_gt).then_inc(c_dve, 1)
                dve_.wait_ge(c_dve, 4)
                v.tensor_copy(slow[:, :], gt[:, :]).then_inc(c_dve, 1)

                def u_of(b):
                    if b.k > 0 or b.it2 is not None:
                        dve_.wait_ge(u_T, b.at(-1).count(1))
                        dve_.sem_inc(turn, 1)
                    v.tensor_tensor(us[:, :], Z[:, cols(b.number())], TH[:, cols(b.number())], ALU.mult).then_inc(us_ready, 1)
                n = 9

                def step2(s):
                    i = [0]

                    def then(ins):
                        i[0] += 1
                        ins.then_inc(dve, 1)
                        dve_.wait_ge(dve, s.count(n, i[0]))
                    if s.k >= 0:
                        if s.real():
                            dve_.wait_ge(u_hi, s.count(1))
                            v.tensor_tensor(T_lo[0][:, :], ps_T[0][:, :], T_hi[0][:, :].bitcast(F32), ALU.subtract).then_inc(u_lo, 1)
                    if s.at(1).real():
                        u_of(s.at(1))
                    if s.real():
                        dve_.wait_ge(y_ready, s.count(1))
                        v.tensor_tensor(y[:, :], ps_out[:, :], b4[:, :], ALU.add).then_inc(y_used, 1)
                        dve_.wait_ge(y_used, s.count(1))
                        then(v.tensor_tensor(y[:, :], y[:, :], X[:, cols(s.number())], ALU.add))
                        for j in range(2):
                            then(v.bn_stats(st[:, :], y[:, :]))
                            dve_.sem_inc(turn, 1)
                            v.bn_aggr(mv[:, :], st[:, :]).then_inc(mv_ready, 1)
                            dve_.wait_ge(sd_ready, s.count(2, j + 1))
                            then(v.reciprocal(rs[:, :], sd[:, :]))
                            if j == 0:
                                then(v.tensor_scalar(y[:, :], y[:, :], mv[:, 0:1], rs[:, 0:1], ALU.subtract, ALU.mult))
                                then(v.tensor_tensor(y[:, :], y[:, :], gam[:, :], ALU.mult))
                                then(v.tensor_tensor(y[:, :], y[:, :], bet[:, :], ALU.add))
                                then(v.tensor_tensor(y[:, :], y[:, :], X[:, cols(s.number())], ALU.add))
                            else:
                                v.tensor_scalar(X[:, cols(s.number())], y[:, :], mv[:, 0:1], rs[:, 0:1], ALU.subtract, ALU.mult)
                        assert i[0] == n, i[0]
                dve_.wait_ge(t_ready, 2)
                row_steps(dve_, -1, R - 1, 0, R - 2, step2)

            @block.tensor
            def _(pe):
                t = nc.tensor

                def step(s):
                    pe.wait_ge(xs_ready, s.count(1))
                    pe.wait_ge(ag_in, s.count(16))
                    for ps, src_ in ((ps_T[0], xs), (ps_T[1], ag)):
                        for k in range(KD):
                            last = t.transpose(ps[:, k * P:(k + 1) * P], src_[:, k * P:(k + 1) * P], ident[:, :])
                    last.then_inc(T_ready, 1)
                    pe.wait_ge(a_in, s.count(16))
                    if s.k > 0 or s.it2 is not None:
                        pe.wait_ge(aT_evac, s.at(-1).count(1))
                    for k in range(R):
                        last = t.transpose(ps_adj[:, k * P:(k + 1) * P], adj_in[:, k * P:(k + 1) * P], ident[:, :])
                    last.then_inc(aT_ready, 1)
                    if s.k > 0 or s.it2 is not None:
                        pe.wait_ge(z_ready, s.at(-1).count(1))
                    pe.wait_ge(lo_ready, s.count(2))
                    three_products(nc, ps_out, T_hi[0], T_lo[0], w_hi[:, 0:KD, :], w_lo[:, 0:KD, :], True, False)
                    three_products(nc, ps_out, T_hi[1], T_lo[1], w_hi[:, KD:2 * KD, :], w_lo[:, KD:2 * KD, :], False, True).then_inc(z_out, 1)
                pe.wait_ge(w_split, 2)
                row_steps(pe, 0, R - 1, 1, R - 1, step)
                pe.wait_ge(deg_tr, 1)
                t.transpose(ps_deg[:, :], mdeg[:, :], ident[:, :]).then_inc(deg_tr, 1)

                def step2(s):
                    pe.wait_ge(us_ready, s.count(1))
                    for k in range(KD):
                        last = t.transpose(ps_T[0][:, k * P:(k + 1) * P], us[:, k * P:(k + 1) * P], ident[:, :])
                    last.then_inc(u_T, 1)
                    if s.k > 0 or s.it2 is not None:
                        pe.wait_ge(y_used, s.at(-1).count(1))
                    pe.wait_ge(u_lo, s.count(1))
                    three_products(nc, ps_out, T_hi[0], T_lo[0], w_hi[:, 2 * KD:, :], w_lo[:, 2 * KD:, :], True, True).then_inc(y_ready, 1)
                row_steps(pe, 0, R - 1, 1, R - 1, step2)


MEAN_SEMS = ("w_in", "v_in", "w_split", "x_split", "a_in", "xs_ready", "m_out", "ms_ready", "T_ready", "hi_ready",
             "lo_ready", "o_out", "o_used", "mv_ready", "sd_ready", "dve", "x_new", "turn", "stored")


def mean_layer(nc, sb, pb, sem, sems, layer, ident, eps_col, X, rdeg, nrdeg, has, slow, adjT_dram, w_x, w_m, vecs, out):
    n_ = f"n{layer}_"
    with ExitStack() as ctx:
        w_raw = sb(n_ + "w_raw", [P, 2 * KD, D], F32, ctx)
        w_hi, w_lo = sb(n_ + "w_hi", [P, 2 * KD, D], F32R, ctx), sb(n_ + "w_lo", [P, 2 * KD, D], F32R, ctx)
        vec = [sb(f"{n_}vec{i}", [P, D], F32, ctx) for i in range(len(vecs))]
        X_hi, X_lo = sb(n_ + "X_hi", [P, R * D], F32R, ctx), sb(n_ + "X_lo", [P, R * D], F32R, ctx)
        adjT = sb(n_ + "adjT", [P, NP], F32, ctx)
        xs, ms = sb(n_ + "xs", [P, D], F32, ctx), sb(n_ + "ms", [P, D], F32, ctx)
        T_hi = [sb(f"{n_}T_hi{i}", [P, D], F32R, ctx) for i in range(2)]
        T_lo = [sb(f"{n_}T_lo{i}", [P, D], F32R, ctx) for i in range(2)]
        y = sb(n_ + "y", [P, D], F32, ctx)
        st, mv = sb(n_ + "st", [P, 6], F32, ctx), sb(n_ + "mv", [P, 2], F32, ctx)
        sd, rs = sb(n_ + "sd", [P, 1], F32, ctx), sb(n_ + "rs", [P, 1], F32, ctx)
        keep = sb(n_ + "keep", [P, R], F32, ctx)
        ps_T = [pb(f"{n_}ps_T{i}", [P, D], ctx) for i in range(2)]
        ps_m, ps_out = pb(n_ + "ps_m", [P, D], ctx), pb(n_ + "ps_out", [P, D], ctx)
        (w_in, v_in, w_split, x_split, a_in, xs_ready, m_out, ms_ready, T_ready, hi_ready, lo_ready, o_out, o_used,
         mv_ready, sd_ready, dve, x_new, turn, stored) = sems
        if layer == 1:
            Y = sb("Y", [P, R * D], F32, ctx)
            sq = sb("sq", [P, 2, D], F32, ctx)
            ones, valid = sb("ones", [P, P], F32, ctx), sb("valid", [P, P], F32, ctx)
            mean, scale = sb("mean", [P, D], F32, ctx), sb("scale", [P, D], F32, ctx)
            ps_s, ps_v = pb("ps_s", [P, D], ctx), pb("ps_v", [P, D], ctx)
            (ones_ready, valid_ready, s_out, c_ready, sq_ready, v_part, v_out, var_ready, y_ready) = [
                sem("bn_" + n) for n in ("ones_ready", "valid_ready", "s_out", "c_ready", "sq_ready", "v_part", "v_out",
                                         "var_ready", "y_ready")]

        def past(b):
            return b.it2 is not None or b.k >= 0

        with nc.Block() as block:
            @block.sync
            def _(sp):
                for i, w in enumerate((w_x, w_m)):
                    sp.dma_start(w_raw[:, i * KD:(i + 1) * KD, :], w.rearrange("(k p) d -> p k d", p=P)).then_inc(w_in, 16)
                for t, b in zip(vec, vecs):
                    sp.dma_start(t[:, :], bcast(b)).then_inc(v_in, 16)

                def step(s):
                    if past(s.at(-1)):
                        sp.wait_ge(m_out, s.at(-1).count(1))
                    sp.dma_start(adjT[:, :], adjT_dram[bass.ds(s.number() * P, P), :]).then_inc(a_in, 16)
                row_steps(sp, 0, R - 1, 1, R - 1, step)
                if layer == 3:
                    with sp.Fori(0, R - 1) as r:
                        sp.wait_ge(x_new, r + 1)
                        sp.dma_start(out[bass.ds(r * P, P), :], X[:, cols(r)]).then_inc(stored, 16)
                    sp.wait_ge(x_new, R)
                    sp.dma_start(out[(R - 1) * P:N, :], X[0:LASTR, (R - 1) * D:]).then_inc(stored, 16)
                    sp.wait_ge(stored, 16 * R)

            @block.scalar
            def _(act):
                a = nc.scalar
                a.copy(X_hi[:, :], X[:, :]).then_inc(x_split, 1)
                act.wait_ge(w_in, 32)
                a.copy(w_hi[:, :, :], w_raw[:, :, :]).then_inc(w_split, 1)

                def deviation(b):
                    act.wait_ge(mv_ready, b.count(1))
                    a.activation(sd[:, :], mv[:, 1:2], ACT.Sqrt, bias=eps_col[:, :]).then_inc(sd_ready, 1)

                def step(s):
                    if s.real():
                        for i in range(2):
                            if i == 0:
                                act.wait_ge(T_ready, s.count(1))
                            a.copy(T_hi[i][:, :], ps_T[i][:, :]).then_inc(hi_ready, 1)
                    b = s.at(1)
                    if b.real():
                        if past(b.at(-1)):
                            act.wait_ge(T_ready, b.at(-1).count(1))
                            act.sem_inc(turn, 1)
                        a.copy(xs[:, :], X[:, cols(b.number())]).then_inc(xs_ready, 1)
                    if layer != 1 and past(s.at(-1)):
                        deviation(s.at(-1))
                row_steps(act, -1, R, 1, R - 2, step)
                if layer == 1:
                    def square(b, u):
                        act.wait_ge(c_ready, b.count(2, u + 1))
                        if past(b.at(-1)):
                            act.wait_ge(v_part, b.at(-1).count(2, u + 1))
                        act.sem_inc(turn, 1)
                        a.activation(sq[:, u, :], Y[:, cols(b.number() * 2 + u)], ACT.Square).then_inc(sq_ready, 1)

                    def step_sq(s):
                        square(s, 0)
                        square(s, 1)
                    row_steps(act, 0, R // 2 - 1, 1, R // 2 - 1, step_sq)
                    act.wait_ge(v_out, 1)
                    a.activation(scale[:, :], ps_v[:, :], ACT.Sqrt, scale=1.0 / N, bias=eps_col[:, :]).then_inc(var_ready, 1)
                    row_steps(act, 0, R - 1, 0, R - 1, deviation)

            @block.gpsimd
            def _(pool):
                if layer == 1:
                    g = nc.gpsimd
                    g.memset(ones[:, :], 1.0).then_inc(ones_ready, 1)
                    pool.wait_ge(ones_ready, 1)
                    g.affine_select(out=valid[:, :], in_=ones[:, :], compare_op=ALU.is_ge, fill=0.0, base=LASTR - 1,
                                    pattern=[[0, P]], channel_multiplier=-1).then_inc(valid_ready, 1)

            @block.vector
            def _(dve_):
                v = nc.vector
                dve_.wait_ge(x_split, 1)
                v.tensor_tensor(X_lo[:, :], X[:, :], X_hi[:, :].bitcast(F32), ALU.subtract).then_inc(x_split, 1)
                v.tensor_scalar(keep[:, :], has[:, :], -1.0, 2.0, ALU.mult, ALU.add)
                dve_.wait_ge(w_split, 1)
                v.tensor_tensor(w_lo[:, :, :], w_raw[:, :, :], w_hi[:, :, :].bitcast(F32), ALU.subtract).then_inc(w_split, 1)
                dve_.wait_ge(v_in, 16 * len(vecs))
                chain = {1: 0, 2: 2 + (len(vecs) - 1), 3: 5}[layer]
                if layer == 2:
                    chain = 4
                if layer == 3:
                    chain = 5

                def mean_of(b):
                    dve_.wait_ge(m_out, b.count(1))
                    dve_.sem_inc(turn, 1)
                    if layer == 3:
                        v.scalar_tensor_tensor(ms[:, :], ps_m[:, :], nrdeg[:, bass.ds(b.number(), 1)], X[:, cols(b.number())],
                                               ALU.mult, ALU.add).then_inc(ms_ready, 1)
                    else:
                        v.tensor_scalar(ms[:, :], ps_m[:, :], rdeg[:, bass.ds(b.number(), 1)], None, ALU.mult).then_inc(ms_ready, 1)

                def low(b):
                    for i in range(2):
                        dve_.wait_ge(hi_ready, b.count(2, i + 1))
                        v.tensor_tensor(T_lo[i][:, :], ps_T[i][:, :], T_hi[i][:, :].bitcast(F32), ALU.subtract).then_inc(lo_ready, 1)

                def norm(b, then):
                    then(v.bn_stats(st[:, :], y[:, :]))
                    dve_.sem_inc(turn, 1)
                    v.bn_aggr(mv[:, :], st[:, :]).then_inc(mv_ready, 1)
                    dve_.wait_ge(sd_ready, b.count(1))
                    then(v.reciprocal(rs[:, :], sd[:, :]))
                    v.tensor_scalar(X[:, cols(b.number())], y[:, :], mv[:, 0:1], rs[:, 0:1], ALU.subtract, ALU.mult).then_inc(x_new, 1)

                def counter(b, n):
                    i = [0]

                    def then(ins):
                        i[0] += 1
                        assert i[0] <= n
                        ins.then_inc(dve, 1)
                        dve_.wait_ge(dve, b.count(n, i[0]))
                    return then

                def finish(b):
                    dve_.wait_ge(o_out, b.count(1))
                    if layer == 1:
                        v.tensor_tensor(Y[:, cols(b.number())], ps_out[:, :], vec[0][:, :], ALU.add).then_inc(o_used, 1)
                        return
                    then = counter(b, 4 if layer == 2 else 5)
                    if past(b.at(-1)):
                        dve_.wait_ge(x_new, b.at(-1).count(1))
                    v.tensor_tensor(y[:, :], ps_out[:, :], vec[0][:, :], ALU.add).then_inc(o_used, 1)
                    dve_.wait_ge(o_used, b.count(1))
                    then(v.tensor_tensor(y[:, :], y[:, :], vec[1][:, :], ALU.add))
                    if layer == 2:
                        then(v.tensor_tensor(y[:, :], y[:, :], X[:, cols(b.number())], ALU.add))
                    else:
                        dve_.sem_inc(turn, 1)
                        then(v.tensor_scalar(y[:, :], y[:, :], has[:, bass.ds(b.number(), 1)], None, ALU.mult))
                        dve_.sem_inc(turn, 1)
                        then(v.scalar_tensor_tensor(y[:, :], X[:, cols(b.number())], keep[:, bass.ds(b.number(), 1)], y[:, :],
                                                    ALU.mult, ALU.add))
                    norm(b, then)

                def step(s):
                    if s.real():
                        low(s)
                    if past(s.at(-1)) and s.at(-1).real():
                        finish(s.at(-1))
                    if s.at(1).real():
                        mean_of(s.at(1))
                row_steps(dve_, -1, R, 1, R - 2, step)
                if layer == 1:
                    dve_.wait_ge(s_out, 1)
                    v.tensor_scalar(mean[:, :], ps_s[:, :], 1.0 / N, None, ALU.mult).then_inc(y_ready, 1)
                    dve_.wait_ge(y_ready, 1)
                    with dve_.Fori(0, R) as r:
                        v.tensor_tensor(Y[:, cols(r)], Y[:, cols(r)], mean[:, :], ALU.subtract).then_inc(c_ready, 1)
                    dve_.wait_ge(var_ready, 1)
                    v.reciprocal(mean[:, :], scale[:, :]).then_inc(y_ready, 1)
                    dve_.wait_ge(y_ready, 2)
                    v.tensor_tensor(scale[:, :], mean[:, :], vec[1][:, :], ALU.mult).then_inc(y_ready, 1)
                    dve_.wait_ge(y_ready, 3)

                    def activate(b):
                        then = counter(b, 6)
                        if past(b.at(-1)):
                            dve_.wait_ge(x_new, b.at(-1).count(1))
                        then(v.tensor_tensor(y[:, :], Y[:, cols(b.number())], scale[:, :], ALU.mult))
                        then(v.tensor_tensor(y[:, :], y[:, :], vec[2][:, :], ALU.add))
                        then(v.scalar_tensor_tensor(y[:, :], y[:, :], 0.01, y[:, :], ALU.mult, ALU.max))
                        then(v.scalar_tensor_tensor(y[:, :], X[:, cols(b.number())], 2.0, y[:, :], ALU.mult, ALU.add))
                        norm(b, then)
                    row_steps(dve_, 0, R - 1, 0, R - 1, activate)

            @block.tensor
            def _(pe):
                t = nc.tensor
                is_slow = pe.value_load(slow[0:1, 0:1], min_val=0, max_val=1)

                def sums(b):
                    pe.wait_ge(a_in, b.count(16))
                    if past(b.at(-1)):
                        pe.wait_ge(ms_ready, b.at(-1).count(1))
                    pe.sem_inc(turn, 1)
                    with pe.If(is_slow):
                        products_of(b, F32)
                    with pe.Else():
                        products_of(b, F32R)

                def products_of(b, dt):
                    for k in range(R):
                        for i, xx in enumerate((X_hi, X_lo)):
                            last = t.matmul(ps_m[:, :], adjT[:, k * P:(k + 1) * P].bitcast(dt), xx[:, cols(k)].bitcast(dt),
                                            start=(k == 0 and i == 0), stop=(k == R - 1 and i == 1))
                    last.then_inc(m_out, 1)

                def turn_both(b):
                    pe.wait_ge(xs_ready, b.count(1))
                    pe.wait_ge(ms_ready, b.count(1))
                    for ps, src_ in ((ps_T[0], xs), (ps_T[1], ms)):
                        for k in range(KD):
                            last = t.transpose(ps[:, k * P:(k + 1) * P], src_[:, k * P:(k + 1) * P], ident[:, :])
                    last.then_inc(T_ready, 1)

                def products(b):
                    if past(b.at(-1)):
                        pe.wait_ge(o_used, b.at(-1).count(1))
                    pe.wait_ge(lo_ready, b.count(2))
                    three_products(nc, ps_out, T_hi[0], T_lo[0], w_hi[:, 0:KD, :], w_lo[:, 0:KD, :], True, False)
                    three_products(nc, ps_out, T_hi[1], T_lo[1], w_hi[:, KD:, :], w_lo[:, KD:, :], False, True).then_inc(o_out, 1)

                def step(s):
                    if s.real():
                        turn_both(s)
                    if s.at(1).real():
                        sums(s.at(1))
                    if s.real():
                        products(s)
                pe.wait_ge(x_split, 2)
                pe.wait_ge(w_split, 2)
                row_steps(pe, -1, R - 1, 1, R - 2, step)
                if layer == 1:
                    pe.wait_ge(valid_ready, 1)
                    pe.wait_ge(o_used, R)
                    t.matmul(ps_s[:, :], ones[:, :], Y[:, cols(0)], start=True, stop=False)
                    with pe.Fori(1, R - 1) as r:
                        t.matmul(ps_s[:, :], ones[:, :], Y[:, cols(r)], start=False, stop=False)
                    t.matmul(ps_s[:, :], valid[:, :], Y[:, cols(R - 1)], start=False, stop=True).then_inc(s_out, 1)
                    pe.wait_ge(sq_ready, 1)
                    t.matmul(ps_v[:, :], ones[:, :], sq[:, 0, :], start=True, stop=False).then_inc(v_part, 1)
                    with pe.Fori(0, R // 2 - 1) as h:
                        pe.wait_ge(sq_ready, h * 2 + 2)
                        t.matmul(ps_v[:, :], ones[:, :], sq[:, 1, :], start=False, stop=False).then_inc(v_part, 1)
                        pe.wait_ge(sq_ready, h * 2 + 3)
                        t.matmul(ps_v[:, :], ones[:, :], sq[:, 0, :], start=False, stop=False).then_inc(v_part, 1)
                    pe.wait_ge(sq_ready, R)
                    t.matmul(ps_v[:, :], valid[:, :], sq[:, 1, :], start=False, stop=True).then_inc(v_out, 1)


def kernel(**inputs):
    import numpy as np
    import concourse.bacc as bacc
    from concourse.bass_utils import run_bass_kernel_spmd as run

    nc = bacc.Bacc("TRN2", target_bir_lowering=False, num_devices=1)
    a = {k: np.ascontiguousarray(v) for k, v in inputs.items()}
    edges = np.zeros((ED, NB * BE), a["edge_attr_64"].dtype)
    edges[:, :E] = a["edge_attr_64"].T
    w1 = a["L0_gnn_W1"]
    arrays = {
        "x": a["x"], "src": a["src"], "dst": a["dst"], "eaT": edges,
        "w0a": w1[0:D], "w0b": w1[D:2 * D], "w0c": w1[2 * D:], "b01": a["L0_gnn_b1"],
        "w02": a["L0_gnn_W2"], "b02": a["L0_gnn_b2"], "w03": a["L0_gnn_W3"], "b03": a["L0_gnn_b3"],
        "w04": a["L0_gnn_W4"], "b04": a["L0_gnn_b4"], "g0": a["L0_gnn_gamma"], "be0": a["L0_gnn_beta"],
        "w1l": a["L1_gnn_W_l"], "b1l": a["L1_gnn_b_l"], "w1r": a["L1_gnn_W_r"], "g1": a["L1_gnn_gamma"],
        "be1": a["L1_gnn_beta"], "w21": a["L2_gnn_W1"].T, "b21": a["L2_gnn_b1"], "w22": a["L2_gnn_W2"].T,
        "b22": a["L2_gnn_b2"], "w31": a["L3_gnn_W1"], "b31": a["L3_gnn_b1"], "w32": a["L3_gnn_W2"],
        "b32": a["L3_gnn_b2"],
    }
    arrays = {"in_" + k: np.ascontiguousarray(v) for k, v in arrays.items()}
    args = [nc.dram_tensor(k, v.shape, mybir.dt.from_np(v.dtype), kind="ExternalInput").ap() for k, v in arrays.items()]
    out = nc.dram_tensor("out_x", [N, D], F32, kind="ExternalOutput").ap()
    gnn(nc, *args, out)
    return run(nc, [arrays], core_ids=[0]).results[0]["out_x"]
```

```python
import concourse.bass as bass
from concourse import mybir
from contextlib import ExitStack

F32 = mybir.dt.float32
F32R = mybir.dt.float32r
F16 = mybir.dt.float16
I32 = mybir.dt.int32
ACT = mybir.ActivationFunctionType
ALU = mybir.AluOpType
AX = mybir.AxisListType

P = 128
N = 1250
D = 512
KD = D // P
E = 21250
ED = 64
R = -(-N // P)
NP = R * P
LASTR = N - (R - 1) * P
TE = 4
BE = TE * P
NB = -(-E // BE)
NB += NB % 2
LASTE = E - (NB - 1) * BE
PADE = 1 << 20
DROWS = NP + P
MAXPASS = -(-N // P)
SRC_CHUNKS = [(0, 427), (427, 427), (854, NP - 854)]
EXACT = 4096
SIN_TILES = (2, 6)
EPS = 1e-5
HALF_PI = 1.5707963267948966


class Blk:

    def __init__(self, k, lead, half, it2=None, total=NB):
        self.k, self.it2, self.total = k, it2, total
        self.lead, self.half = lead, half

    def at(self, off):
        return Blk(self.k + off, self.lead, self.half, self.it2, self.total)

    def real(self):
        assert self.it2 is None or self.k >= 0
        return self.it2 is not None or 0 <= self.k < self.total

    def count(self, per, part=None):
        return self.lead * per + (self.k * per + (per if part is None else part))

    def slot_count(self, per):
        return self.half * per + (self.k // 2 + 1) * per

    @property
    def slot(self):
        return self.k % 2

    def number(self):
        return self.k if self.it2 is None else self.it2 + self.k


FIRST_STEP, LOOP_FROM, LOOP_TO, LAST_STEP = -3, 4, NB - 5, NB + 1
assert (LOOP_TO - LOOP_FROM + 1) % 2 == 0


def steps(eng, p, body):
    lead, half = eng.snap(p * NB), eng.snap(p * (NB // 2))
    for k in range(FIRST_STEP, LOOP_FROM):
        body(Blk(k, lead, half))
    with eng.Fori(0, (LOOP_TO - LOOP_FROM + 1) // 2) as it:
        it2 = eng.snap(it * 2)
        lead2, half2 = eng.snap(lead + it2), eng.snap(half + it)
        for u in range(2):
            body(Blk(LOOP_FROM + u, lead2, half2, it2))
    for k in range(LOOP_TO + 1, LAST_STEP + 1):
        body(Blk(k, lead, half))


def cols(r, n=D):
    return bass.ds(r * n, n)


def gnn(nc, x, src, dst, eaT, w0a, w0b, w0c, b01, w02, b02, w03, b03, w04, b04, g0, be0,
        w1l, b1l, w1r, g1, be1, w21, b21, w22, b22, w31, b31, w32, b32, out):
    top = ExitStack()
    with top:
        def sb(name, shape, dt=F32, ctx=top):
            return ctx.enter_context(nc.sbuf_tensor(name, shape, dt))

        def pb(name, shape, ctx):
            return ctx.enter_context(nc.psum_tensor(name, shape, F32))

        def sem(name):
            return top.enter_context(nc.semaphore(name))

        def dram(name, shape):
            return nc.dram_tensor(name, shape, F32, kind="Internal").ap()

        p_dram = dram("p_dram", [NP, D])
        q_dram = dram("q_dram", [NP, D])
        agg_dram = dram("agg_dram", [DROWS, D])
        adj_dram = dram("adj_dram", [DROWS, NP])
        adjT_dram = dram("adjT_dram", [R * P, NP])

        ident = sb("ident", [P, P])
        deg = sb("deg", [P, R])
        rdeg = sb("rdeg", [P, R])
        nrdeg = sb("nrdeg", [P, R])
        has = sb("has", [P, R])
        eps_col = sb("eps_col", [P, 1])
        half_pi = sb("half_pi", [P, 1])
        relT = sb("relT", [P, TE, NB])
        srcT = sb("srcT", [P, TE, NB])
        idx_all = sb("idx_all", [P, NB * 2 * TE], I32)
        base_f = sb("base_f", [1, NB])
        base_i = sb("base_i", [1, NB], I32)
        npass = sb("npass", [1, 1], I32)
        slow = sb("slow", [1, 1], I32)

        with ExitStack() as ctx:
            X = sb("X0", [P, R * D], F32, ctx)
            dst_i = sb("dst_i", [NB, BE], I32, ctx)
            src_i = sb("src_i", [NB, BE], I32, ctx)
            dst_f = sb("dst_f", [NB, BE], F32, ctx)
            src_f = sb("src_f", [NB, BE], F32, ctx)
            rel_f = sb("rel_f", [NB, BE], F32, ctx)
            dstc_f = sb("dstc_f", [NB, BE], F32, ctx)
            real_f = sb("real_f", [NB, BE], F32, ctx)
            bounds = sb("bounds", [NB, 2], F32, ctx)
            span = sb("span", [1, NB], F32, ctx)
            mspan = sb("mspan", [1, 1], F32, ctx)
            mspan_i = sb("mspan_i", [1, 1], I32, ctx)
            w_raw = sb("w_raw", [P, 2 * KD, D], F32, ctx)
            w_hi = sb("w_hi", [P, 2 * KD, D], F32R, ctx)
            w_lo = sb("w_lo", [P, 2 * KD, D], F32R, ctx)
            b1_bc = sb("b1_bc", [P, D], F32, ctx)
            zeros = sb("zeros", [P, NP], F32, ctx)
            xs = sb("xs", [P, 2, D], F32, ctx)
            xT_hi = sb("xT_hi", [P, 2, D], F32R, ctx)
            xT_lo = sb("xT_lo", [P, 2, D], F32R, ctx)
            p_sb = sb("p_sb", [P, 2, D], F32, ctx)
            q_sb = sb("q_sb", [P, 2, D], F32, ctx)
            ps_idx = pb("ps_idx", [P, 3, TE, NB], ctx)
            ps_row = pb("ps_row", [P, 2, 64], ctx)
            ps_t = [pb(f"ps_t{i}", [P, D], ctx) for i in range(2)]
            ps_p, ps_q = pb("ps_p", [P, D], ctx), pb("ps_q", [P, D], ctx)
            (z_ready, ident_ready, x_in, w_in, b_in, idx_in, pad_set, dve, w_split, idx_tr, xs_ready, t_ready,
             hi_ready, lo_ready, p_ready, q_ready, p_evac, q_evac, tab_out, zero_out, act_turn) = [
                sem("prep_" + n) for n in (
                    "z_ready", "ident_ready", "x_in", "w_in", "b_in", "idx_in", "pad_set", "dve", "w_split", "idx_tr",
                    "xs_ready", "t_ready", "hi_ready", "lo_ready", "p_ready", "q_ready", "p_evac", "q_evac",
                    "tab_out", "zero_out", "act_turn")]
            p_out = [sem(f"prep_p_out{i}") for i in range(2)]
            q_out = [sem(f"prep_q_out{i}") for i in range(2)]

            with nc.Block() as block:
                @block.sync
                def _(sp):
                    sp.wait_ge(pad_set, 1)
                    sp.dma_start(X[:, 0:(R - 1) * D].rearrange("p (r d) -> p r d", d=D), x[0:(R - 1) * P, :].rearrange("(r p) d -> p r d", p=P)).then_inc(x_in, 16)
                    sp.dma_start(X[0:LASTR, (R - 1) * D:], x[(R - 1) * P:N, :]).then_inc(x_in, 16)
                    sp.dma_start(w_raw[:, 0:KD, :], w0a.rearrange("(k p) d -> p k d", p=P)).then_inc(w_in, 16)
                    sp.dma_start(w_raw[:, KD:2 * KD, :], w0b.rearrange("(k p) d -> p k d", p=P)).then_inc(w_in, 16)
                    sp.dma_start(b1_bc[:, :], b01.rearrange("(a d) -> a d", a=1).to_broadcast([P, D])).then_inc(b_in, 16)
                    sp.wait_ge(z_ready, 1)
                    for r in range(DROWS // P):
                        sp.dma_start(adj_dram[r * P:(r + 1) * P, :], zeros[:, :]).then_inc(zero_out, 16)
                        sp.dma_start(agg_dram[r * P:(r + 1) * P, :], zeros[:, 0:D]).then_inc(zero_out, 16)

                    def store(half, u):
                        row = half * 2 * P + u * P
                        sp.wait_ge(p_evac, half * 2 + (u + 1))
                        sp.dma_start(p_dram[bass.ds(row, P), :], p_sb[:, u, :]).then_inc(p_out[u], 16)
                        sp.wait_ge(q_evac, half * 2 + (u + 1))
                        sp.dma_start(q_dram[bass.ds(row, P), :], q_sb[:, u, :]).then_inc(q_out[u], 16)
                    with sp.Fori(0, R // 2) as half:
                        store(half, 0)
                        store(half, 1)
                    for u in range(2):
                        sp.wait_ge(p_out[u], 16 * (R // 2))
                        sp.wait_ge(q_out[u], 16 * (R // 2))
                    sp.wait_ge(zero_out, 32 * (DROWS // P))

                @block.gpsimd
                def _(pool):
                    nc.gpsimd.memset(zeros[:, :], 0.0).then_inc(z_ready, 1)
                    nc.gpsimd.memset(ident[:, :], 0.0).then_inc(ident_ready, 1)
                    pool.wait_ge(ident_ready, 1)
                    nc.gpsimd.affine_select(out=ident[:, :], in_=ident[:, :], compare_op=ALU.not_equal, fill=1.0, base=0,
                                            pattern=[[-1, P]], channel_multiplier=1).then_inc(ident_ready, 1)

                @block.vector
                def _(dve_):
                    v = nc.vector
                    n = [0]

                    def then(ins):
                        n[0] += 1
                        ins.then_inc(dve, 1)
                        dve_.wait_ge(dve, n[0])

                    v.memset(X[:, (R - 1) * D:], 0.0).then_inc(pad_set, 1)
                    v.memset(dst_i[:, :], PADE).then_inc(pad_set, 1)
                    v.memset(src_i[:, :], 0).then_inc(pad_set, 1)
                    v.memset(eps_col[:, :], EPS)
                    v.memset(half_pi[:, :], HALF_PI)
                    dve_.wait_ge(idx_in, 64)
                    v.tensor_copy(src_f[:, :], src_i[:, :])
                    then(v.tensor_copy(dst_f[:, :], dst_i[:, :]))
                    v.tensor_reduce(bounds[:, 0:1], dst_f[:, :], AX.X, ALU.min)
                    then(v.scalar_tensor_tensor(real_f[:, :], dst_f[:, :], float(PADE), dst_f[:, :], ALU.is_lt, ALU.mult))
                    v.tensor_scalar(dstc_f[:, :], dst_f[:, :], float(N - 1), None, ALU.min)
                    then(v.tensor_reduce(bounds[:, 1:2], real_f[:, :], AX.X, ALU.max))
                    v.tensor_scalar(rel_f[:, :], dst_f[:, :], bounds[:, 0:1], None, ALU.subtract).then_inc(idx_tr, 1)
                    dve_.wait_ge(idx_tr, 2)
                    v.tensor_copy(idx_all[:, :].rearrange("p (b c) -> p c b", c=2 * TE)[:, 0:TE, :], ps_idx[:, 1, :, :])
                    v.tensor_copy(idx_all[:, :].rearrange("p (b c) -> p c b", c=2 * TE)[:, TE:, :], ps_idx[:, 2, :, :])
                    v.tensor_copy(srcT[:, :, :], ps_idx[:, 1, :, :])
                    v.tensor_copy(relT[:, :, :], ps_idx[:, 0, :, :])
                    then(v.tensor_copy(base_f[:, :], ps_row[0:1, 0, 0:NB]))
                    v.tensor_copy(base_i[:, :], base_f[:, :])
                    then(v.tensor_tensor(span[:, :], ps_row[0:1, 1, 0:NB], base_f[:, :], ALU.subtract))
                    then(v.tensor_reduce(mspan[:, :], span[:, :], AX.X, ALU.max))
                    then(v.tensor_copy(mspan_i[:, :], mspan[:, :]))
                    then(v.tensor_scalar(mspan_i[:, :], mspan_i[:, :], 7, None, ALU.arith_shift_right))
                    then(v.tensor_scalar(npass[:, :], mspan_i[:, :], 1.0, None, ALU.add))
                    dve_.wait_ge(w_split, 1)
                    v.tensor_tensor(w_lo[:, :, :], w_raw[:, :, :], w_hi[:, :, :].bitcast(F32), ALU.subtract).then_inc(w_split, 1)
                    dve_.wait_ge(b_in, 16)

                    def low(cnt, u):
                        dve_.wait_ge(hi_ready, cnt)
                        v.tensor_tensor(xT_lo[:, u, :], ps_t[u][:, :], xT_hi[:, u, :].bitcast(F32), ALU.subtract).then_inc(lo_ready, 1)

                    def bias(cnt, u, reuse):
                        if reuse is not None:
                            dve_.wait_ge(q_out[u], reuse)
                        dve_.wait_ge(q_ready, cnt)
                        v.tensor_tensor(q_sb[:, u, :], ps_q[:, :], b1_bc[:, :], ALU.add).then_inc(q_evac, 1)
                    low(1, 0)
                    low(2, 1)
                    bias(1, 0, None)
                    low(3, 0)
                    bias(2, 1, None)
                    with dve_.Fori(1, R // 2 - 1) as h:
                        low(h * 2 + 2, 1)
                        bias(h * 2 + 1, 0, h * 16)
                        low(h * 2 + 3, 0)
                        bias(h * 2 + 2, 1, h * 16)
                    low(R, 1)
                    bias(R - 1, 0, 16 * (R // 2 - 1))
                    bias(R, 1, 16 * (R // 2 - 1))

                @block.scalar
                def _(act):
                    act.wait_ge(pad_set, 3)
                    for t, (raw, dram_idx) in enumerate(((dst_i, dst), (src_i, src))):
                        act.dma_start(raw[0:NB - 1, :], dram_idx[0:(NB - 1) * BE].rearrange("(b e) -> b e", e=BE)).then_inc(idx_in, 16)
                        act.dma_start(raw[NB - 1:NB, 0:LASTE], dram_idx[(NB - 1) * BE:E].rearrange("(b e) -> b e", b=1)).then_inc(idx_in, 16)
                    act.wait_ge(w_in, 32)
                    nc.scalar.copy(w_hi[:, :, :], w_raw[:, :, :]).then_inc(w_split, 1)
                    act.wait_ge(x_in, 32)

                    def fetch(r, reuse, u):
                        if reuse is not None:
                            act.wait_ge(t_ready, reuse)
                            act.sem_inc(act_turn, 1)
                        nc.scalar.copy(xs[:, u, :], X[:, cols(r)]).then_inc(xs_ready, 1)

                    def high(cnt, u):
                        act.wait_ge(t_ready, cnt)
                        nc.scalar.copy(xT_hi[:, u, :], ps_t[u][:, :]).then_inc(hi_ready, 1)

                    def p_store(cnt, u, reuse):
                        if reuse is not None:
                            act.wait_ge(p_out[u], reuse)
                        act.wait_ge(p_ready, cnt)
                        nc.scalar.copy(p_sb[:, u, :], ps_p[:, :]).then_inc(p_evac, 1)
                    fetch(0, None, 0)
                    fetch(1, None, 1)
                    high(1, 0)
                    high(2, 1)
                    fetch(2, 1, 0)
                    p_store(1, 0, None)
                    high(3, 0)
                    fetch(3, 2, 1)
                    p_store(2, 1, None)
                    with act.Fori(1, R // 2 - 1) as h:
                        high(h * 2 + 2, 1)
                        fetch(h * 2 + 2, h * 2 + 1, 0)
                        p_store(h * 2 + 1, 0, h * 16)
                        high(h * 2 + 3, 0)
                        fetch(h * 2 + 3, h * 2 + 2, 1)
                        p_store(h * 2 + 2, 1, h * 16)
                    high(R, 1)
                    p_store(R - 1, 0, 16 * (R // 2 - 1))
                    p_store(R, 1, 16 * (R // 2 - 1))

                @block.tensor
                def _(pe):
                    pe.wait_ge(ident_ready, 2)
                    pe.wait_ge(idx_tr, 1)
                    for q, t in enumerate((rel_f, src_f, dstc_f)):
                        for c in range(TE):
                            nc.tensor.transpose(ps_idx[:, q, c, :], t[:, c * P:(c + 1) * P], ident[0:NB, 0:NB])
                    nc.tensor.transpose(ps_row[0:1, 0, 0:NB], bounds[:, 0:1], ident[0:NB, 0:NB])
                    nc.tensor.transpose(ps_row[0:1, 1, 0:NB], bounds[:, 1:2], ident[0:NB, 0:NB]).then_inc(idx_tr, 1)

                    def turn(cnt, u):
                        pe.wait_ge(xs_ready, cnt)
                        for k in range(KD):
                            last = nc.tensor.transpose(ps_t[u][:, k * P:(k + 1) * P], xs[:, u, k * P:(k + 1) * P], ident[:, :])
                        last.then_inc(t_ready, 1)

                    def products(cnt, u, reuse):
                        pe.wait_ge(lo_ready, cnt)
                        for j, (ps, ready, evac) in enumerate(((ps_p, p_ready, p_evac), (ps_q, q_ready, q_evac))):
                            if reuse is not None:
                                pe.wait_ge(evac, reuse)
                            for k in range(KD):
                                for i, (a, w) in enumerate(((xT_hi, w_hi), (xT_hi, w_lo), (xT_lo, w_hi))):
                                    last = nc.tensor.matmul(ps[:, :], a[:, u, k * P:(k + 1) * P], w[:, j * KD + k, :],
                                                            start=(k == 0 and i == 0), stop=(k == KD - 1 and i == 2))
                            last.then_inc(ready, 1)
                    turn(1, 0)
                    turn(2, 1)
                    pe.wait_ge(w_split, 2)
                    products(1, 0, None)
                    turn(3, 0)
                    products(2, 1, 1)
                    with pe.Fori(1, R // 2 - 1) as h:
                        turn(h * 2 + 2, 1)
                        products(h * 2 + 1, 0, h * 2)
                        turn(h * 2 + 3, 0)
                        products(h * 2 + 2, 1, h * 2 + 1)
                    turn(R, 1)
                    products(R - 1, 0, R - 2)
                    products(R, 1, R - 1)

        edge_phase(nc, sb, pb, sem, ident, half_pi, relT, srcT, idx_all, base_f, base_i, npass,
                   p_dram, q_dram, agg_dram, adj_dram, eaT, w0c, w02, b02)
        X = sb("X", [P, R * D])
        parts = [[sb(f"X_{n}0", [P, R * D], F32R) for n in ("hi", "lo")]]
        w_raw = sb("w_raw_n", [P, 2 * KD, D])
        w_hi, w_lo = sb("w_hi_n", [P, 2 * KD, D], F32R), sb("w_lo_n", [P, 2 * KD, D], F32R)
        w_in = [[sem(f"w_in{layer}{i}") for i in range(2)] for layer in (1, 2, 3)]
        layers = ((w1r, w1l, [b1l, g1, be1]), (w21, w22, [b21, b22]), (w31, w32, [b31, b32]))
        first_layer(nc, sb, pb, sem, ident, half_pi, eps_col, X, *parts[0], w_raw, w_hi, w_lo, x, deg, rdeg, nrdeg, has, slow,
                    agg_dram, adj_dram, adjT_dram, w03, b03, w04, b04, g0, be0, layers[0][:2], w_in[0])
        sems = [sem("mean_" + n) for n in MEAN_SEMS]
        for layer in (1, 2, 3):
            if layer == 2:
                parts.append([sb(f"X_{n}1", [P, R * D], F32R) for n in ("hi", "lo")])
            if layer > 1:
                with nc.Block() as block:
                    @block.sync
                    def _(sp):
                        for s in sems:
                            sp.sem_clear(s)
            used, made = parts[layer // 3], parts[layer // 2 % 2]
            mean_layer(nc, sb, pb, sem, sems, layer, ident, eps_col, X, *used, *made, w_raw, w_hi, w_lo,
                       rdeg, nrdeg, has, slow, adjT_dram, w_in[layer - 1], layers[layer][:2] if layer < 3 else None,
                       w_in[layer] if layer < 3 else None, layers[layer - 1][2], out)


def edge_phase(nc, sb, pb, sem, ident, half_pi, relT, srcT, idx_all, base_f, base_i, npass,
               p_dram, q_dram, agg_dram, adj_dram, eaT, w0c, w02, b02):
    with ExitStack() as ctx:
        w_raw = sb("e_w_raw", [P, KD, D], F32, ctx)
        w2_hi, w2_lo = sb("w2_hi", [P, KD, D], F32R, ctx), sb("w2_lo", [P, KD, D], F32R, ctx)
        wc_raw = sb("wc_raw", [P, D], F32, ctx)
        wc_hi, wc_lo = sb("wc_hi", [P, D], F32R, ctx), sb("wc_lo", [P, D], F32R, ctx)
        b2 = sb("b2", [P, D], F32, ctx)
        iota_src = sb("iota_src", [P, NP], F16, ctx)
        ea_raw = sb("ea_raw", [P, 2, BE], F32, ctx)
        ea_parts = sb("ea_parts", [P, 2, BE], F32R, ctx)
        idx = sb("idx", [P, 2, 2 * TE], I32, ctx)
        G = sb("G", [P, 2, TE * D], F32, ctx)
        x1 = sb("x1", [P, 2, TE * D], F32, ctx)
        h1 = sb("h1", [P, 2, TE * D], F32, ctx)
        hT_hi = sb("hT_hi", [P, 2, D], F32R, ctx)
        hT_lo = sb("hT_lo", [P, 2, D], F32R, ctx)
        x2 = sb("x2", [P, 2, TE * D], F32, ctx)
        m2 = sb("m2", [P, TE * D], F32, ctx)
        m_hi, m_lo = sb("m_hi", [P, TE * D], F32R, ctx), sb("m_lo", [P, TE * D], F32R, ctx)
        oh_src = sb("oh_src", [P, 2, TE, NP], F16, ctx)
        oh_win = sb("oh_win", [P, 2, TE, P], F16, ctx)
        oh_winr = sb("oh_winr", [P, 2, TE, P], F32R, ctx)
        agg_sb = sb("agg_sb", [P, 2, D], F32, ctx)
        adj_sb = sb("adj_sb", [P, 2, NP], F32, ctx)
        ps_pre, ps_tr, ps_x2 = ([pb(f"{n}{i}", [P, D], ctx) for i in range(2)] for n in ("ps_pre", "ps_tr", "ps_x2"))
        ps_adj, ps_agg = pb("ps_adj", [P, D], ctx), pb("ps_agg", [P, D], ctx)

        (w_in, iota_ready, x2_evac, w_split, dve, pre_ready, x1_ready, sig1, atan1, t1_ready, h1_ready, tr_ready,
         hi_ready, hT_ready, x2_ready, sig2, atan2, t2_ready, m2_ready, mhi_ready, m_ready, oh_ready, adj_ready,
         adj_evac, agg_ready, agg_evac, summed, ea_hi, ea_ready, idx_ready, shifted, turn) = [
            sem("edge_" + n) for n in (
                "w_in", "iota_ready", "x2_evac", "w_split", "dve", "pre_ready", "x1_ready", "sig1", "atan1", "t1_ready",
                "h1_ready", "tr_ready", "hi_ready", "hT_ready", "x2_ready", "sig2", "atan2", "t2_ready", "m2_ready",
                "mhi_ready", "m_ready", "oh_ready", "adj_ready", "adj_evac", "agg_ready", "agg_evac", "summed",
                "ea_hi", "ea_ready", "idx_ready", "shifted", "turn")]
        ea_in = [sem(f"edge_ea_in{i}") for i in range(2)]
        p_in = [sem(f"edge_p_in{i}") for i in range(2)]
        q_in = [sem(f"edge_q_in{i}") for i in range(2)]

        def passes(eng, body):
            n = eng.value_load(npass[0:1, 0:1], min_val=1, max_val=MAXPASS)
            with eng.Fori(0, n) as p:
                body(p)
                eng.wait_ge(summed, p * (NB * 32) + NB * 32)
                eng.sem_inc(turn, 1)

        with nc.Block() as block:
            @block.sync
            def _(sp):
                sp.dma_start(w_raw[:, :, :], w02.rearrange("(k p) d -> p k d", p=P)).then_inc(w_in, 16)
                for half in range(2):
                    sp.dma_start(wc_raw[half * ED:(half + 1) * ED, :], w0c).then_inc(w_in, 16)

                sp.dma_start(b2[:, :], bcast(b02)).then_inc(w_in, 16)

                def step(s):
                    b = s.at(3)
                    if b.real():
                        if b.at(-2).real():
                            sp.wait_ge(ea_ready, b.at(-2).count(1))
                        for half in range(2):
                            sp.dma_start(ea_raw[half * ED:(half + 1) * ED, b.slot, :],
                                         eaT[:, bass.ds(b.number() * BE, BE)]).then_inc(ea_in[b.slot], 16)

                def one_pass(p):
                    steps(sp, p, step)
                passes(sp, one_pass)

            @block.gpsimd
            def _(pool):
                g = nc.gpsimd
                g.iota(iota_src[:, :], pattern=[[1, NP]], base=0, channel_multiplier=0,
                       allow_small_or_imprecise_dtypes=True).then_inc(iota_ready, 1)

                def wait(s, v):
                    pool.wait_ge(s, v)
                    pool.sem_inc(turn, 1)

                def step(s):
                    b = s.at(3)
                    if b.real():
                        if b.at(-2).real():
                            wait(x1_ready, b.at(-2).count(TE))
                        g.tensor_copy(idx[:, b.slot, :], idx_all[:, bass.ds(b.number() * (2 * TE), 2 * TE)]).then_inc(idx_ready, 1)
                        wait(idx_ready, b.count(1))
                        for c in range(TE):
                            g.indirect_dma_start(G[:, b.slot, c * D:(c + 1) * D], None, p_dram,
                                                 bass.IndirectOffsetOnAxis(ap=idx[:, b.slot, c:c + 1], axis=0)).then_inc(p_in[b.slot], 16)
                        wait(p_in[b.slot], b.slot_count(16 * TE))
                        for c in range(TE):
                            g.indirect_dma_start(G[:, b.slot, c * D:(c + 1) * D], None, q_dram,
                                                 bass.IndirectOffsetOnAxis(ap=idx[:, b.slot, TE + c:TE + c + 1], axis=0),
                                                 compute_op=ALU.add).then_inc(q_in[b.slot], 16)
                    b = s.at(-1)
                    if b.real():
                        for half in range(2):
                            c = slice(half * 2 * D, (half + 1) * 2 * D)
                            if half == 0 and b.at(-1).real():
                                wait(agg_ready, b.at(-1).count(1))
                            wait(m2_ready, b.count(TE, 2 * half + 2))
                            g.tensor_scalar(m_hi[:, c], m2[:, c], 1.0, 0.0, ALU.mult, ALU.add).then_inc(mhi_ready, 1)
                            pool.wait_ge(mhi_ready, b.count(2, half + 1))
                            g.tensor_tensor(m_lo[:, c], m2[:, c], m_hi[:, c].bitcast(F32), ALU.subtract).then_inc(m_ready, 1)
                    b = s.at(-2)
                    if b.real():
                        if b.at(-1).real():
                            wait(summed, b.at(-1).count(32))
                        wait(adj_evac, b.count(len(SRC_CHUNKS)))
                        wait(agg_evac, b.count(1))
                        row = g.value_load(base_i[0:1, bass.ds(b.number(), 1)], min_val=0, max_val=NP)
                        g.dma_start(adj_dram[bass.ds(row, P), :], adj_sb[:, b.slot, :], accum_op=ALU.add).then_inc(summed, 16)
                        g.dma_start(agg_dram[bass.ds(row, P), :], agg_sb[:, b.slot, :], accum_op=ALU.add).then_inc(summed, 16)

                def one_pass(p):
                    wait(shifted, p + 1)
                    steps(pool, p, step)
                passes(pool, one_pass)

            def passes_dve(dve_, body):
                v = nc.vector
                n = dve_.value_load(npass[0:1, 0:1], min_val=1, max_val=MAXPASS)
                with dve_.Fori(0, n) as p:
                    body(p)
                    dve_.wait_ge(summed, p * (NB * 32) + NB * 32)
                    v.tensor_scalar(relT[:, :, :], relT[:, :, :], float(P), None, ALU.subtract)
                    v.tensor_scalar(base_f[:, :], base_f[:, :], float(P), float(NP), ALU.add, ALU.min).then_inc(dve, 1)
                    dve_.wait_ge(dve, p + 1)
                    v.tensor_copy(base_i[:, :], base_f[:, :]).then_inc(shifted, 1)

            @block.vector
            def _(dve_):
                v = nc.vector
                dve_.wait_ge(w_in, 16 * 4)
                dve_.wait_ge(w_split, 2)
                v.tensor_tensor(w2_lo[:, :, :], w_raw[:, :, :], w2_hi[:, :, :].bitcast(F32), ALU.subtract)
                v.tensor_tensor(wc_lo[:, :], wc_raw[:, :], wc_hi[:, :].bitcast(F32), ALU.subtract).then_inc(w_split, 1)
                dve_.wait_ge(iota_ready, 1)

                def step(s):
                    b = s.at(3)
                    if b.real():
                        dve_.wait_ge(ea_in[b.slot], b.slot_count(32))
                        if b.at(-2).real():
                            dve_.wait_ge(pre_ready, b.at(-2).count(TE))
                        v.tensor_copy(ea_parts[:, b.slot, :], ea_raw[:, b.slot, :]).then_inc(ea_hi, 1)
                        dve_.wait_ge(ea_hi, b.count(1))
                        v.tensor_tensor(ea_parts[ED:P, b.slot, :], ea_raw[ED:P, b.slot, :],
                                        ea_parts[ED:P, b.slot, :].bitcast(F32), ALU.subtract).then_inc(ea_ready, 1)
                    for c in range(TE):
                        b, e = (s, c - 1) if c > 0 else (s.at(-1), TE - 1)
                        if b.real():
                            dve_.wait_ge(x2_ready, b.count(TE, e + 1))
                            v.tensor_tensor(x2[:, b.slot, cols(e)], ps_x2[e % 2][:, :], b2[:, :], ALU.add).then_inc(x2_evac, 1)
                        b = s.at(2)
                        if b.real():
                            if c == 0:
                                dve_.wait_ge(q_in[b.slot], b.slot_count(16 * TE))
                            dve_.wait_ge(pre_ready, b.count(TE, c + 1))
                            v.tensor_tensor(x1[:, b.slot, cols(c)], ps_pre[c % 2][:, :], G[:, b.slot, cols(c)], ALU.add).then_inc(x1_ready, 1)
                        b, e = (s, c + 1) if c < TE - 1 else (s.at(1), 0)
                        if b.real():
                            dve_.wait_ge(hi_ready, b.count(TE, e + 1))
                            v.tensor_tensor(hT_lo[:, e % 2, :], ps_tr[e % 2][:, :], hT_hi[:, e % 2, :].bitcast(F32), ALU.subtract).then_inc(hT_ready, 1)
                        b = s.at(-1)
                        if b.real():
                            if c == 0 and b.at(-2).real():
                                dve_.wait_ge(adj_ready, b.at(-2).count(len(SRC_CHUNKS)))
                                dve_.sem_inc(turn, 1)
                            i = bass.ds(b.number(), 1)
                            v.tensor_scalar(oh_src[:, b.slot, c, :], iota_src[:, :], srcT[:, c, i], None, ALU.is_equal)
                            v.tensor_scalar(oh_win[:, b.slot, c, :], iota_src[:, 0:P], relT[:, c, i], None, ALU.is_equal)
                            v.tensor_scalar(oh_winr[:, b.slot, c, :], iota_src[:, 0:P], relT[:, c, i], None, ALU.is_equal).then_inc(oh_ready, 1)
                        b = s.at(-2)
                        if b.real() and c == 1:
                            if b.at(-2).real():
                                dve_.wait_ge(summed, b.at(-2).count(32))
                            dve_.wait_ge(agg_ready, b.count(1))
                            v.tensor_copy(agg_sb[:, b.slot, :], ps_agg[:, :]).then_inc(agg_evac, 1)
                        b = s.at(-1)
                        if b.real() and c in (1, 2):
                            dve_.wait_ge(t2_ready, b.count(2, c))
                            for e in (2 * c - 2, 2 * c - 1):
                                v.tensor_tensor(m2[:, cols(e)], x2[:, b.slot, cols(e)], m2[:, cols(e)], ALU.mult).then_inc(m2_ready, 1)
                        b = s.at(1)
                        if b.real() and c == 2:
                            for e in range(TE):
                                if e % 2 == 0:
                                    dve_.wait_ge(t1_ready, b.count(2, e // 2 + 1))
                                v.tensor_tensor(h1[:, b.slot, cols(e)], x1[:, b.slot, cols(e)], h1[:, b.slot, cols(e)],
                                                ALU.mult).then_inc(h1_ready, 1)

                dve_.sem_inc(shifted, 1)

                def one_pass(p):
                    steps(dve_, p, step)
                passes_dve(dve_, one_pass)

            @block.scalar
            def _(act):
                a = nc.scalar
                act.wait_ge(w_in, 16 * 4)
                a.copy(w2_hi[:, :, :], w_raw[:, :, :]).then_inc(w_split, 1)
                a.copy(wc_hi[:, :], wc_raw[:, :]).then_inc(w_split, 1)

                def evac_adj(b, j):
                    if b.real():
                        if j == 0 and b.at(-2).real():
                            act.wait_ge(summed, b.at(-2).count(32))
                        o, n = SRC_CHUNKS[j]
                        act.wait_ge(adj_ready, b.count(len(SRC_CHUNKS), j + 1))
                        a.copy(adj_sb[:, b.slot, o:o + n], ps_adj[:, 0:n]).then_inc(adj_evac, 1)

                def high(b, e):
                    if b.real():
                        act.wait_ge(tr_ready, b.count(TE, e + 1))
                        a.copy(hT_hi[:, e % 2, :], ps_tr[e % 2][:, :]).then_inc(hi_ready, 1)

                def arctan(b, half, x_, ready, free, t_, sig, atan):
                    if b.real():
                        c = slice(half * 2 * D, (half + 1) * 2 * D)
                        act.wait_ge(ready, b.count(TE, 2 * half + 2))
                        free(b, half)
                        a.activation(t_(b)[:, c], x_[:, b.slot, c], ACT.Sigmoid, scale=-1.0).then_inc(sig, 1)
                        act.wait_ge(sig, b.count(2, half + 1))
                        a.activation(t_(b)[:, c], t_(b)[:, c], ACT.Arctan).then_inc(atan, 1)

                def sine(b, half, t_, atan, ready):
                    if b.real():
                        c = slice(half * 2 * D, (half + 1) * 2 * D)
                        act.wait_ge(atan, b.count(2, half + 1))
                        a.activation(t_(b)[:, c], t_(b)[:, c], ACT.Sin, scale=-2.0, bias=half_pi[:, :]).then_inc(ready, 1)

                def h1_free(b, half):
                    if b.at(-2).real():
                        act.wait_ge(tr_ready, b.at(-2).count(TE))

                def m2_free(b, half):
                    if b.at(-1).real():
                        act.wait_ge(m_ready, b.at(-1).count(2, half + 1))

                def arctan1(b, half):
                    arctan(b, half, x1, x1_ready, h1_free, lambda b: h1[:, b.slot, :], sig1, atan1)

                def arctan2(b, half):
                    arctan(b, half, x2, x2_evac, m2_free, lambda b: m2, sig2, atan2)

                def sine1(b, half):
                    sine(b, half, lambda b: h1[:, b.slot, :], atan1, t1_ready)

                def sine2(b, half):
                    sine(b, half, lambda b: m2, atan2, t2_ready)

                def step(s):
                    arctan2(s.at(-1), 1)
                    high(s, 1)
                    sine2(s.at(-1), 0)
                    sine2(s.at(-1), 1)
                    evac_adj(s.at(-2), 0)
                    high(s, 2)
                    sine1(s.at(1), 0)
                    sine1(s.at(1), 1)
                    evac_adj(s.at(-2), 1)
                    high(s, 3)
                    arctan1(s.at(2), 0)
                    arctan2(s, 0)
                    evac_adj(s.at(-2), 2)
                    high(s.at(1), 0)
                    arctan1(s.at(2), 1)

                def one_pass(p):
                    steps(act, p, step)
                passes(act, one_pass)

            @block.tensor
            def _(pe):
                t = nc.tensor
                pe.wait_ge(w_split, 3)

                def bank_free(sem, b, c):
                    if c >= 2:
                        pe.wait_ge(sem, b.count(TE, c - 1))
                    elif b.at(-1).real():
                        pe.wait_ge(sem, b.at(-1).count(TE, c + 3))

                def rest_of_first(b, c):
                    if c == 0:
                        pe.wait_ge(ea_ready, b.count(1))
                    bank_free(x1_ready, b, c)
                    for i, w in enumerate((wc_hi, wc_lo)):
                        last = t.matmul(ps_pre[c % 2][:, :], ea_parts[:, b.slot, c * P:(c + 1) * P], w[:, :], start=(i == 0), stop=(i == 1))
                    last.then_inc(pre_ready, 1)

                def adjacency(b, j):
                    chunks = len(SRC_CHUNKS)
                    if j > 0:
                        pe.wait_ge(adj_evac, b.count(chunks, j))
                    elif b.at(-1).real():
                        pe.wait_ge(adj_evac, b.at(-1).count(chunks))
                    o, n = SRC_CHUNKS[j]
                    for k in range(TE):
                        last = t.matmul(ps_adj[:, 0:n], oh_win[:, b.slot, k, :], oh_src[:, b.slot, k, o:o + n], start=(k == 0), stop=(k == TE - 1))
                    last.then_inc(adj_ready, 1)

                def sums(b):
                    pe.wait_ge(oh_ready, b.count(TE))
                    pe.wait_ge(m_ready, b.count(2))
                    if b.at(-1).real():
                        pe.wait_ge(agg_evac, b.at(-1).count(1))
                    for k in range(TE):
                        for i, m in enumerate((m_hi, m_lo)):
                            last = t.matmul(ps_agg[:, :], oh_winr[:, b.slot, k, :], m[:, cols(k)], start=(k == 0 and i == 0),
                                            stop=(k == TE - 1 and i == 1))
                    last.then_inc(agg_ready, 1)

                def turn_h(b, c):
                    pe.wait_ge(h1_ready, b.count(TE, c + 1))
                    bank_free(hT_ready, b, c)
                    for k in range(KD):
                        last = t.transpose(ps_tr[c % 2][:, k * P:(k + 1) * P], h1[:, b.slot, c * D + k * P:c * D + (k + 1) * P], ident[:, :])
                    last.then_inc(tr_ready, 1)

                def second(b, c):
                    pe.wait_ge(hT_ready, b.count(TE, c + 1))
                    bank_free(x2_evac, b, c)
                    three_products(nc, ps_x2[c % 2], hT_hi[:, c % 2, :], hT_lo[:, c % 2, :], w2_hi, w2_lo, True, True).then_inc(x2_ready, 1)

                def step(s):
                    for c in range(TE):
                        if s.at(2).real():
                            rest_of_first(s.at(2), c)
                        if s.at(-2).real():
                            if c == 0:
                                sums(s.at(-2))
                            else:
                                adjacency(s.at(-2), c - 1)
                        b = s if c < TE - 1 else s.at(1)
                        if b.real():
                            turn_h(b, (c + 1) % TE)
                        if s.real():
                            second(s, c)

                def one_pass(p):
                    steps(pe, p, step)
                passes(pe, one_pass)


def tile_steps(eng, first, last, body, lo=2):
    hi = R - 3
    for k in range(first, lo):
        body(Blk(k, 0, 0, total=R))
    with eng.Fori(0, (hi - lo + 1) // 2) as it:
        it2 = eng.snap(it * 2)
        for u in range(2):
            body(Blk(lo + u, it2, it, it2, total=R))
    for k in range(hi + 1, last + 1):
        body(Blk(k, 0, 0, total=R))


assert R % 2 == 0 and R >= 6


def three_products(nc, ps, a_hi, a_lo, w_hi, w_lo, first, last):
    for k in range(KD):
        for i, (a, w) in enumerate(((a_hi, w_hi), (a_hi, w_lo), (a_lo, w_hi))):
            ins = nc.tensor.matmul(ps[:, :], a[:, k * P:(k + 1) * P], w[:, k, :], start=(first and k == 0 and i == 0),
                                   stop=(last and k == KD - 1 and i == 2))
    return ins


def bcast(vec):
    return vec.rearrange("(a d) -> a d", a=1).to_broadcast([P, D])


def by_slices(w):
    return w.rearrange("(k p) d -> p k d", p=P)


def split_weights_hi(a, act, w_in, w_raw, w_hi, w_hi_ready):
    for i in range(2):
        act.wait_ge(w_in[i], 16)
        a.copy(w_hi[:, i * KD:(i + 1) * KD, :], w_raw[:, i * KD:(i + 1) * KD, :]).then_inc(w_hi_ready, 1)


def split_weights_lo(v, dve_, w_raw, w_hi, w_lo, w_hi_ready, w_lo_ready):
    for i in range(2):
        c = slice(i * KD, (i + 1) * KD)
        dve_.wait_ge(w_hi_ready, i + 1)
        v.tensor_tensor(w_lo[:, c, :], w_raw[:, c, :], w_hi[:, c, :].bitcast(F32), ALU.subtract).then_inc(w_lo_ready, 1)


def first_layer(nc, sb, pb, sem, ident, half_pi, eps_col, X, X_hi, X_lo, w_raw, w_hi, w_lo, x, deg, rdeg, nrdeg, has, slow,
                agg_dram, adj_dram, adjT_dram, w03, b03, w04, b04, g0, be0, w_next, w_next_in):
    with ExitStack() as ctx:
        b3, b4 = sb("b3", [P, D], F32, ctx), sb("b4", [P, D], F32, ctx)
        gam, bet = sb("n0_gam", [P, D], F32, ctx), sb("n0_bet", [P, D], F32, ctx)
        rows = [sb(f"n0_{n}", [P, 2, D], F32, ctx) for n in ("xs", "ag")]
        T_hi = [sb(f"n0_T_hi{i}", [P, 2, D], F32R, ctx) for i in range(2)]
        T_lo = [sb(f"n0_T_lo{i}", [P, 2, D], F32R, ctx) for i in range(2)]
        adj_in, adjT_sb = sb("adj_in", [P, 2, NP], F32, ctx), sb("adjT_sb", [P, 2, NP], F32, ctx)
        Z, TH = sb("Z", [P, R * D], F32, ctx), sb("TH", [P, R * D], F32, ctx)
        us = rows[0]
        xb4, xbet = adj_in[:, :, 0:D], adj_in[:, :, D:2 * D]
        y_out, y_in, y_sc = adjT_sb[:, :, 0:D], adjT_sb[:, 0, D:2 * D], adjT_sb[:, 1, D:2 * D]
        st = [sb(f"n0_st{i}", [P, 6], F32, ctx) for i in range(2)]
        mv = [sb(f"n0_mv{i}", [P, 2], F32, ctx) for i in range(2)]
        sd = [sb(f"n0_sd{i}", [P, 1], F32, ctx) for i in range(2)]
        rs = [sb(f"n0_rs{i}", [P, 1], F32, ctx) for i in range(2)]
        nmr = sb("n0_nmr", [P, 1], F32, ctx)
        mdeg, mdeg1, gt = sb("mdeg", [P, 1], F32, ctx), sb("mdeg1", [1, 1], F32, ctx), sb("gt", [1, 1], F32, ctx)
        ps_T = [[pb(f"n0_ps_T{i}{u}", [P, D], ctx) for u in range(2)] for i in range(2)]
        ps_adj, ps_out = pb("n0_ps_adj", [P, NP], ctx), pb("n0_ps_out", [P, D], ctx)
        ps_y = [ps_out, ps_T[1][0]]
        row_in = [sem(f"n0_row_in{u}") for u in range(2)]
        a_in = [sem(f"n0_a_in{u}") for u in range(2)]
        aT_out = [sem(f"n0_aT_out{u}") for u in range(2)]
        st_ready, mv_ready, sd_ready, rs_ready = ([sem(f"n0_{n}{i}") for i in range(2)] for n in (
            "st_ready", "mv_ready", "sd_ready", "rs_ready"))
        w_in = [sem(f"n0_w_in{i}") for i in range(2)]
        (x_in, w4_in, c_in, w_hi_ready, w_lo_ready, T_ready, hi_ready, lo_ready, z_out, z_ready, sig, atan, t_ready,
         aT_ready, aT_evac, d_ready, c_dve, deg_tr, us_ready, xb_ready, xe_ready, u_T, u_hi, u_lo, y_ready, y_used, sc_ready,
         res_ready, co_ready, x_new, xlo_ready, turn) = [
            sem("n0_" + n) for n in (
                "x_in", "w4_in", "c_in", "w_hi_ready", "w_lo_ready", "T_ready", "hi_ready", "lo_ready", "z_out", "z_ready",
                "sig", "atan", "t_ready", "aT_ready", "aT_evac", "d_ready", "c_dve", "deg_tr", "us_ready", "xb_ready",
                "xe_ready", "u_T", "u_hi", "u_lo", "y_ready", "y_used", "sc_ready", "res_ready", "co_ready", "x_new",
                "xlo_ready", "turn")]

        with nc.Block() as block:
            @block.sync
            def _(sp):
                def step(s):
                    if s.it2 is None and s.k == 0:
                        sp.wait_ge(x_in, 1)
                        sp.dma_start(X[:, 0:(R - 1) * D].rearrange("p (r d) -> p r d", d=D),
                                     x[0:(R - 1) * P, :].rearrange("(r p) d -> p r d", p=P)).then_inc(x_in, 16)
                        sp.dma_start(X[0:LASTR, (R - 1) * D:], x[(R - 1) * P:N, :]).then_inc(x_in, 16)
                    b = s.at(2)
                    if b.real():
                        if b.at(-2).real():
                            sp.wait_ge(T_ready, b.at(-2).count(2))
                        if b.it2 is None and b.k < 4:
                            sp.dma_start(rows[0][:, b.slot, :], x[b.k * P:(b.k + 1) * P, :]).then_inc(row_in[b.slot], 16)
                        else:
                            sp.wait_ge(x_in, 33)
                            sp.dma_start(rows[0][:, b.slot, :], X[:, cols(b.number())]).then_inc(row_in[b.slot], 16)
                        sp.dma_start(rows[1][:, b.slot, :], agg_dram[bass.ds(b.number() * P, P), :]).then_inc(row_in[b.slot], 16)
                        if b.at(-2).real():
                            sp.wait_ge(aT_ready, b.at(-2).count(1))
                            sp.wait_ge(d_ready, b.at(-2).count(1))
                        sp.dma_start(adj_in[:, b.slot, :], adj_dram[bass.ds(b.number() * P, P), :]).then_inc(a_in[b.slot], 16)
                    if s.real():
                        sp.wait_ge(aT_evac, s.count(1))
                        sp.dma_start(adjT_dram[bass.ds(s.number() * P, P), :], adjT_sb[:, s.slot, :]).then_inc(aT_out[s.slot], 16)
                tile_steps(sp, -2, R - 1, step)
                for u in range(2):
                    sp.wait_ge(aT_out[u], 16 * (R // 2))

            @block.scalar
            def _(act):
                a = nc.scalar
                for i in range(2):
                    act.dma_start(w_raw[:, i * KD:(i + 1) * KD, :], by_slices(w03[i * D:(i + 1) * D, :])).then_inc(w_in[i], 16)
                for t, b in ((b3, b03), (b4, b04), (gam, g0), (bet, be0)):
                    act.dma_start(t[:, :], bcast(b)).then_inc(c_in, 16)
                split_weights_hi(a, act, w_in, w_raw, w_hi, w_hi_ready)

                def step(s):
                    b = s.at(1)
                    if b.real():
                        if b.at(-2).real():
                            act.wait_ge(z_out, b.at(-2).count(1))
                        for i in range(2):
                            act.wait_ge(T_ready, b.count(2, i + 1))
                            a.copy(T_hi[i][:, b.slot, :], ps_T[i][b.slot][:, :]).then_inc(hi_ready, 1)
                    b = s.at(-1)
                    if b.real():
                        act.wait_ge(z_ready, b.count(1))
                        act.sem_inc(turn, 1)
                        a.activation(TH[:, cols(b.number())], Z[:, cols(b.number())], ACT.Sigmoid, scale=-1.0).then_inc(sig, 1)
                        act.wait_ge(sig, b.count(1))
                        act.sem_inc(turn, 1)
                        a.activation(TH[:, cols(b.number())], TH[:, cols(b.number())], ACT.Arctan).then_inc(atan, 1)
                    if s.real():
                        if s.at(-2).real():
                            act.wait_ge(aT_out[s.slot], s.at(-2).slot_count(16))
                        act.wait_ge(aT_ready, s.count(1))
                        a.copy(adjT_sb[:, s.slot, :], ps_adj[:, :]).then_inc(aT_evac, 1)
                tile_steps(act, -1, R, step)
                act.wait_ge(atan, R)
                for r0, r1 in zip((0, *SIN_TILES), (*SIN_TILES, R)):
                    c = slice(r0 * D, r1 * D)
                    a.activation(TH[:, c], TH[:, c], ACT.Sin, scale=-2.0, bias=half_pi[:, :]).then_inc(t_ready, 1)

                def step2(s):
                    b = s.at(1)
                    if b.real():
                        if b.at(-2).real():
                            act.wait_ge(y_ready, b.at(-2).count(1))
                        act.wait_ge(u_T, b.count(1))
                        a.copy(T_hi[0][:, b.slot, :], ps_T[0][b.slot][:, :]).then_inc(u_hi, 1)
                    b = s.at(-3)
                    if b.real():
                        act.wait_ge(co_ready, b.count(1))
                        act.sem_inc(turn, 1)
                        for t in (X[:, cols(b.number())], X_hi[:, cols(b.number())]):
                            a.activation(t, y_out[:, b.slot, :], ACT.Identity, scale=rs[1][:, :], bias=nmr[:, :]).then_inc(x_new, 1)
                    for j, b in enumerate((s.at(-1), s.at(-2))):
                        if b.real():
                            act.wait_ge(mv_ready[j], b.count(1))
                            a.activation(sd[j][:, :], mv[j][:, 1:2], ACT.Sqrt, bias=eps_col[:, :]).then_inc(sd_ready[j], 1)
                tile_steps(act, -1, R + 2, step2, 4)

            @block.gpsimd
            def _(pool):
                g = nc.gpsimd

                def wait(s, v):
                    pool.wait_ge(s, v)
                    pool.sem_inc(turn, 1)

                wait(w_lo_ready, 2)
                g.dma_start(w_raw[:, 0:KD, :], by_slices(w04)).then_inc(w4_in, 16)
                wait(c_in, 64)
                wait(x_in, 33)
                wait(T_ready, 2 * R)
                wait(aT_ready, R)
                wait(d_ready, R)

                def step2(s):
                    if s.it2 is None and s.k == 0:
                        wait(w_lo_ready, 3)
                        for i, w in enumerate(w_next):
                            g.dma_start(w_raw[:, i * KD:(i + 1) * KD, :], by_slices(w)).then_inc(w_next_in[i], 16)
                    b = s.at(2)
                    if b.real():
                        if b.at(-2).real():
                            wait(u_T, b.at(-2).count(1))
                        if b.k in (0, *SIN_TILES):
                            wait(t_ready, (0, *SIN_TILES).index(b.k) + 1)
                        g.tensor_tensor(us[:, b.slot, :], Z[:, cols(b.number())], TH[:, cols(b.number())], ALU.mult).then_inc(us_ready, 1)
                    b = s.at(1)
                    if b.real():
                        if b.at(-2).real():
                            wait(y_used, b.at(-2).count(1))
                        g.tensor_tensor(xb4[:, b.slot, :], X[:, cols(b.number())], b4[:, :], ALU.add).then_inc(xb_ready, 1)
                    b = s
                    if b.real():
                        if b.at(-2).real():
                            wait(res_ready, b.at(-2).count(1))
                        g.tensor_tensor(xbet[:, b.slot, :], X[:, cols(b.number())], bet[:, :], ALU.add).then_inc(xe_ready, 1)
                    b = s.at(-3)
                    if b.real():
                        wait(x_new, b.count(2))
                        g.tensor_tensor(X_lo[:, cols(b.number())], X[:, cols(b.number())], X_hi[:, cols(b.number())].bitcast(F32),
                                        ALU.subtract).then_inc(xlo_ready, 1)
                tile_steps(pool, -2, R + 2, step2, 4)

            @block.vector
            def _(dve_):
                v = nc.vector
                v.memset(X[:, (R - 1) * D:], 0.0).then_inc(x_in, 1)
                split_weights_lo(v, dve_, w_raw, w_hi, w_lo, w_hi_ready, w_lo_ready)
                dve_.wait_ge(c_in, 64)

                def step(s):
                    b = s.at(-1)
                    if b.real():
                        dve_.wait_ge(z_out, b.count(1))
                        v.tensor_tensor(Z[:, cols(b.number())], ps_out[:, :], b3[:, :], ALU.add).then_inc(z_ready, 1)
                    b = s.at(1)
                    if b.real():
                        for i in range(2):
                            dve_.wait_ge(hi_ready, b.count(2, i + 1))
                            v.tensor_tensor(T_lo[i][:, b.slot, :], ps_T[i][b.slot][:, :], T_hi[i][:, b.slot, :].bitcast(F32),
                                            ALU.subtract).then_inc(lo_ready, 1)
                    if s.real():
                        dve_.wait_ge(a_in[s.slot], s.slot_count(16))
                        dve_.sem_inc(turn, 1)
                        v.tensor_reduce(deg[:, bass.ds(s.number(), 1)], adj_in[:, s.slot, :], AX.X, ALU.add).then_inc(d_ready, 1)
                tile_steps(dve_, -1, R, step)
                dve_.wait_ge(z_out, R)
                for u in range(2):
                    dve_.wait_ge(aT_out[u], 16 * (R // 2))
                dve_.wait_ge(w4_in, 16)
                v.tensor_copy(w_hi[:, 0:KD, :], w_raw[:, 0:KD, :]).then_inc(w_hi_ready, 1)
                v.wait_ge(d_ready, R)
                v.tensor_reduce(mdeg[:, :], deg[:, :], AX.X, ALU.max).then_inc(deg_tr, 1)
                v.tensor_scalar(has[:, :], deg[:, :], 0.0, None, ALU.is_gt)
                v.tensor_scalar(rdeg[:, :], deg[:, :], 1.0, None, ALU.max).then_inc(c_dve, 1)
                dve_.wait_ge(w_hi_ready, 3)
                v.tensor_tensor(w_lo[:, 0:KD, :], w_raw[:, 0:KD, :], w_hi[:, 0:KD, :].bitcast(F32), ALU.subtract).then_inc(w_lo_ready, 1)
                dve_.wait_ge(c_dve, 1)
                v.reciprocal(rdeg[:, :], rdeg[:, :]).then_inc(c_dve, 1)
                dve_.wait_ge(c_dve, 2)
                v.tensor_scalar(nrdeg[:, :], rdeg[:, :], -1.0, None, ALU.mult)
                dve_.wait_ge(deg_tr, 2)
                v.tensor_reduce(mdeg1[:, :], ps_adj[0:1, 0:P], AX.X, ALU.max).then_inc(c_dve, 1)
                dve_.wait_ge(c_dve, 3)
                v.tensor_scalar(gt[:, :], mdeg1[:, :], float(EXACT), None, ALU.is_gt).then_inc(c_dve, 1)
                dve_.wait_ge(c_dve, 4)
                v.tensor_copy(slow[:, :], gt[:, :]).then_inc(c_dve, 1)

                def step2(s):
                    nxt, inner, scaled, res = s.at(1), s.at(-1), s.at(-2), s.at(-3)
                    if nxt.real():
                        dve_.wait_ge(u_hi, nxt.count(1))
                        v.tensor_tensor(T_lo[0][:, nxt.slot, :], ps_T[0][nxt.slot][:, :], T_hi[0][:, nxt.slot, :].bitcast(F32),
                                        ALU.subtract).then_inc(u_lo, 1)
                    if res.real():
                        dve_.wait_ge(sd_ready[1], res.count(1))
                        if res.at(-1).real():
                            dve_.wait_ge(x_new, res.at(-1).count(2))
                        v.reciprocal(rs[1][:, :], sd[1][:, :]).then_inc(rs_ready[1], 1)
                    if scaled.real():
                        dve_.wait_ge(sd_ready[0], scaled.count(1))
                        v.reciprocal(rs[0][:, :], sd[0][:, :]).then_inc(rs_ready[0], 1)
                        if scaled.at(-1).real():
                            dve_.wait_ge(res_ready, scaled.at(-1).count(1))
                        v.scalar_tensor_tensor(y_sc[:, :], y_in[:, :], mv[0][:, 0:1], gam[:, :], ALU.subtract, ALU.mult).then_inc(sc_ready, 1)
                    if res.real():
                        dve_.wait_ge(rs_ready[1], res.count(1))
                        v.scalar_tensor_tensor(nmr[:, :], mv[1][:, 0:1], -1.0, rs[1][:, :], ALU.mult, ALU.mult).then_inc(co_ready, 1)
                    if inner.real():
                        dve_.wait_ge(y_ready, inner.count(1))
                        dve_.wait_ge(xb_ready, inner.count(1))
                        if inner.at(-1).real():
                            dve_.wait_ge(sc_ready, inner.at(-1).count(1))
                        v.tensor_tensor(y_in[:, :], ps_y[inner.slot][:, :], xb4[:, inner.slot, :], ALU.add).then_inc(y_used, 1)
                    if scaled.real():
                        dve_.wait_ge(rs_ready[0], scaled.count(1))
                        dve_.wait_ge(sc_ready, scaled.count(1))
                        dve_.wait_ge(xe_ready, scaled.count(1))
                        v.scalar_tensor_tensor(y_out[:, scaled.slot, :], y_sc[:, :], rs[0][:, :], xbet[:, scaled.slot, :],
                                               ALU.mult, ALU.add).then_inc(res_ready, 1)
                    if inner.real():
                        dve_.wait_ge(y_used, inner.count(1))
                        v.bn_stats(st[0][:, :], y_in[:, :]).then_inc(st_ready[0], 1)
                    if scaled.real():
                        dve_.wait_ge(res_ready, scaled.count(1))
                        v.bn_stats(st[1][:, :], y_out[:, scaled.slot, :]).then_inc(st_ready[1], 1)
                    if inner.real():
                        dve_.wait_ge(st_ready[0], inner.count(1))
                        dve_.sem_inc(turn, 1)
                        v.bn_aggr(mv[0][:, :], st[0][:, :]).then_inc(mv_ready[0], 1)
                    if scaled.real():
                        dve_.wait_ge(st_ready[1], scaled.count(1))
                        if res.real():
                            dve_.wait_ge(co_ready, res.count(1))
                        dve_.sem_inc(turn, 1)
                        v.bn_aggr(mv[1][:, :], st[1][:, :]).then_inc(mv_ready[1], 1)
                tile_steps(dve_, -1, R + 2, step2, 4)

            @block.tensor
            def _(pe):
                t = nc.tensor

                def step(s):
                    b = s.at(1)
                    if b.real():
                        pe.wait_ge(row_in[b.slot], b.slot_count(32))
                        for i in range(2):
                            for k in range(KD):
                                last = t.transpose(ps_T[i][b.slot][:, k * P:(k + 1) * P], rows[i][:, b.slot, k * P:(k + 1) * P], ident[:, :])
                            last.then_inc(T_ready, 1)
                    if s.real():
                        pe.wait_ge(a_in[s.slot], s.slot_count(16))
                        if s.at(-1).real():
                            pe.wait_ge(aT_evac, s.at(-1).count(1))
                        for k in range(R):
                            last = t.transpose(ps_adj[:, k * P:(k + 1) * P], adj_in[:, s.slot, k * P:(k + 1) * P], ident[:, :])
                        last.then_inc(aT_ready, 1)
                        if s.at(-1).real():
                            pe.wait_ge(z_ready, s.at(-1).count(1))
                        for i in range(2):
                            if s.it2 is None and s.k == 0:
                                pe.wait_ge(w_lo_ready, i + 1)
                            pe.wait_ge(lo_ready, s.count(2, i + 1))
                            last = three_products(nc, ps_out, T_hi[i][:, s.slot, :], T_lo[i][:, s.slot, :], w_hi[:, i * KD:(i + 1) * KD, :],
                                                  w_lo[:, i * KD:(i + 1) * KD, :], i == 0, i == 1)
                        last.then_inc(z_out, 1)
                tile_steps(pe, -1, R - 1, step)
                pe.wait_ge(deg_tr, 1)
                pe.wait_ge(aT_evac, R)
                t.transpose(ps_adj[0:1, 0:P], mdeg[:, :], ident[:, :]).then_inc(deg_tr, 1)
                pe.wait_ge(z_ready, R)

                def step2(s):
                    b = s.at(1)
                    if b.real():
                        pe.wait_ge(us_ready, b.count(1))
                        for k in range(KD):
                            last = t.transpose(ps_T[0][b.slot][:, k * P:(k + 1) * P], us[:, b.slot, k * P:(k + 1) * P], ident[:, :])
                        last.then_inc(u_T, 1)
                    if s.real():
                        if s.it2 is None and s.k == 0:
                            pe.wait_ge(w_lo_ready, 3)
                        if s.at(-2).real():
                            pe.wait_ge(y_used, s.at(-2).count(1))
                        pe.wait_ge(u_lo, s.count(1))
                        three_products(nc, ps_y[s.slot], T_hi[0][:, s.slot, :], T_lo[0][:, s.slot, :], w_hi[:, 0:KD, :], w_lo[:, 0:KD, :],
                                       True, True).then_inc(y_ready, 1)
                tile_steps(pe, -1, R - 1, step2)


MEAN_SEMS = ("v_in", "w_hi_ready", "w_lo_ready", "m_out", "ms_ready", "T_ready", "hi_ready", "lo_ready", "o_out", "o_used",
             "y_ready", "st_ready", "mv_ready", "sd_ready", "rs_ready", "co_ready", "x_new", "xlo_ready", "turn", "stored",
             "xk_ready", "a_in0", "a_in1", "xs_in0", "xs_in1")


def mean_layer(nc, sb, pb, sem, sems, layer, ident, eps_col, X, X_hi, X_lo, new_hi, new_lo, w_raw, w_hi, w_lo,
               rdeg, nrdeg, has, slow, adjT_dram, w_in, w_next, w_next_in, vecs, out):
    n_ = f"n{layer}_"
    with ExitStack() as ctx:
        vec = [sb(f"{n_}vec{i}", [P, D], F32, ctx) for i in range(len(vecs))]
        adjT = sb(n_ + "adjT", [P, 2, NP], F32, ctx)
        rows = [sb(n_ + n, [P, 2, D], F32, ctx) for n in ("xs", "ms")]
        T_hi = [sb(f"{n_}T_hi{i}", [P, 2, D], F32R, ctx) for i in range(2)]
        T_lo = [sb(f"{n_}T_lo{i}", [P, 2, D], F32R, ctx) for i in range(2)]
        y = sb(n_ + "y", [P, 2, D], F32, ctx)
        st, mv = sb(n_ + "st", [P, 6], F32, ctx), sb(n_ + "mv", [P, 2], F32, ctx)
        sd, rs, nmr = sb(n_ + "sd", [P, 1], F32, ctx), sb(n_ + "rs", [P, 1], F32, ctx), sb(n_ + "nmr", [P, 1], F32, ctx)
        ps_T = [[pb(f"{n_}ps_T{i}{u}", [P, D], ctx) for u in range(2)] for i in range(2)]
        ps_m, ps_out = ([pb(f"{n_}{n}{u}", [P, D], ctx) for u in range(2)] for n in ("ps_m", "ps_out"))
        (v_in, w_hi_ready, w_lo_ready, m_out, ms_ready, T_ready, hi_ready, lo_ready, o_out, o_used,
         y_ready, st_ready, mv_ready, sd_ready, rs_ready, co_ready, x_new, xlo_ready, turn, stored,
         xk_ready, a_in0, a_in1, xs_in0, xs_in1) = sems
        a_in, xs_in = (a_in0, a_in1), (xs_in0, xs_in1)
        if layer == 3:
            keep = sb("keep", [P, R], F32, ctx)
            xk = sb("xk", [P, D], F32, ctx)
        if layer == 1:
            Y = sb("Y", [P, R * D], F32, ctx)
            sq = sb("sq", [P, 2, D], F32, ctx)
            total = sb("total", [P, D], F32, ctx)
            ones, valid = sb("ones", [P, P], F32, ctx), sb("valid", [P, P], F32, ctx)
            mean, scale = sb("mean", [P, D], F32, ctx), sb("scale", [P, D], F32, ctx)
            t_sc, t_be, t_act = rows[0], rows[1], total
            ps_s, ps_v = ps_m
            (ones_ready, total_ready, s_out, c_ready, sq_ready, v_part, v_out, var_ready, scale_ready, tsc_ready, tbe_ready,
             tact_ready) = [
                sem("bn_" + n) for n in ("ones_ready", "total_ready", "s_out", "c_ready", "sq_ready", "v_part", "v_out",
                                         "var_ready", "scale_ready", "tsc_ready", "tbe_ready", "tact_ready")]

        with nc.Block() as block:
            @block.sync
            def _(sp):
                def adj_load(b):
                    if b.real():
                        if b.at(-2).real():
                            sp.wait_ge(m_out, b.at(-2).count(1))
                        sp.dma_start(adjT[:, b.slot, :], adjT_dram[bass.ds(b.number() * P, P), :]).then_inc(a_in[b.slot], 16)

                def x_load(b):
                    if b.real():
                        if b.at(-2).real():
                            sp.wait_ge(T_ready, b.at(-2).count(2))
                        sp.dma_start(rows[0][:, b.slot, :], X[:, cols(b.number())]).then_inc(xs_in[b.slot], 16)

                def vec_load():
                    for t, b in zip(vec, vecs):
                        sp.dma_start(t[:, :], bcast(b)).then_inc(v_in, 16)

                def step(s):
                    adj_load(s.at(2))
                    x_load(s.at(2))
                    if s.it2 is None and s.k == -1:
                        vec_load()
                    b = s.at(-2)
                    if layer == 3 and b.real():
                        sp.wait_ge(x_new, b.count(1))
                        if b.it2 is None and b.k == R - 1:
                            sp.dma_start(out[(R - 1) * P:N, :], X[0:LASTR, (R - 1) * D:]).then_inc(stored, 16)
                        else:
                            sp.dma_start(out[bass.ds(b.number() * P, P), :], X[:, cols(b.number())]).then_inc(stored, 16)
                tile_steps(sp, -2, R + 1, step)
                if layer == 3:
                    sp.wait_ge(stored, 16 * R)

            @block.scalar
            def _(act):
                a = nc.scalar
                split_weights_hi(a, act, w_in, w_raw, w_hi, w_hi_ready)

                def deviation(b):
                    if b.real():
                        act.wait_ge(mv_ready, b.count(1))
                        a.activation(sd[:, :], mv[:, 1:2], ACT.Sqrt, bias=eps_col[:, :]).then_inc(sd_ready, 1)

                def result(b):
                    if b.real():
                        act.wait_ge(co_ready, b.count(1))
                        act.sem_inc(turn, 1)
                        for t in [X[:, cols(b.number())]] + ([new_hi[:, cols(b.number())]] if layer < 3 else []):
                            a.activation(t, y[:, b.slot, :], ACT.Identity, scale=rs[:, :], bias=nmr[:, :]).then_inc(x_new, 1)

                def step(s):
                    b = s.at(1)
                    if b.real():
                        if b.at(-2).real():
                            act.wait_ge(o_out, b.at(-2).count(1))
                        for i in range(2):
                            act.wait_ge(T_ready, b.count(2, i + 1))
                            a.copy(T_hi[i][:, b.slot, :], ps_T[i][b.slot][:, :]).then_inc(hi_ready, 1)
                    if layer > 1:
                        result(s.at(-2))
                        deviation(s.at(-1))
                tile_steps(act, -1, R + 1, step)
                if layer == 1:
                    def square(s):
                        if s.at(-2).real():
                            act.wait_ge(v_part, s.at(-2).count(1))
                        act.wait_ge(c_ready, s.count(1))
                        act.sem_inc(turn, 1)
                        a.activation(sq[:, s.slot, :], Y[:, cols(s.number())], ACT.Square).then_inc(sq_ready, 1)
                    tile_steps(act, 0, R - 1, square)
                    act.wait_ge(v_out, 1)
                    a.activation(scale[:, :], ps_v[:, :], ACT.Sqrt, scale=1.0 / N, bias=eps_col[:, :]).then_inc(var_ready, 1)

                    def step_act(s):
                        result(s.at(-1))
                        deviation(s)
                    tile_steps(act, 0, R, step_act)

            @block.gpsimd
            def _(pool):
                g = nc.gpsimd

                def wait(s, v):
                    pool.wait_ge(s, v)
                    pool.sem_inc(turn, 1)

                def low(b):
                    if b.real():
                        wait(x_new, b.count(2))
                        g.tensor_tensor(new_lo[:, cols(b.number())], X[:, cols(b.number())], new_hi[:, cols(b.number())].bitcast(F32),
                                        ALU.subtract).then_inc(xlo_ready, 1)
                if layer < 3:
                    wait(w_lo_ready, 2)
                    for i, w in enumerate(w_next):
                        g.dma_start(w_raw[:, i * KD:(i + 1) * KD, :], by_slices(w)).then_inc(w_next_in[i], 16)
                if layer == 1:
                    g.memset(total[:, :], 0.0).then_inc(total_ready, 1)
                    g.memset(ones[:, :], 1.0).then_inc(ones_ready, 1)
                    pool.wait_ge(ones_ready, 1)
                    g.affine_select(out=valid[:, :], in_=ones[:, :], compare_op=ALU.is_ge, fill=0.0, base=LASTR - 1,
                                    pattern=[[0, P]], channel_multiplier=-1).then_inc(ones_ready, 1)
                    with pool.Fori(0, R - 1) as r:
                        wait(o_used, r + 1)
                        wait(total_ready, r + 1)
                        g.tensor_tensor(total[:, :], total[:, :], Y[:, cols(r)], ALU.add).then_inc(total_ready, 1)
                    wait(v_in, 16 * len(vecs))

                    def step_act(s):
                        b = s.at(1)
                        if b.real():
                            if b.at(-2).real():
                                wait(tact_ready, b.at(-2).count(1))
                            wait(tsc_ready, b.count(1))
                            g.tensor_tensor(t_be[:, b.slot, :], t_sc[:, b.slot, :], vec[2][:, :], ALU.add).then_inc(tbe_ready, 1)
                        low(s.at(-2))
                    tile_steps(pool, -1, R + 1, step_act)
                elif layer == 2:
                    tile_steps(pool, 0, R + 1, lambda s: low(s.at(-2)))

            @block.vector
            def _(dve_):
                v = nc.vector
                if layer == 3:
                    v.tensor_scalar(keep[:, :], has[:, :], -1.0, 2.0, ALU.mult, ALU.add)

                def mean_of(b):
                    if b.real():
                        if b.at(-2).real():
                            dve_.wait_ge(T_ready, b.at(-2).count(2))
                        dve_.wait_ge(m_out, b.count(1))
                        dve_.sem_inc(turn, 1)
                        if layer == 3:
                            v.scalar_tensor_tensor(rows[1][:, b.slot, :], ps_m[b.slot][:, :], nrdeg[:, bass.ds(b.number(), 1)],
                                                   X[:, cols(b.number())], ALU.mult, ALU.add).then_inc(ms_ready, 1)
                        else:
                            v.tensor_scalar(rows[1][:, b.slot, :], ps_m[b.slot][:, :], rdeg[:, bass.ds(b.number(), 1)], None,
                                            ALU.mult).then_inc(ms_ready, 1)

                def low(b, i):
                    if b.real():
                        dve_.wait_ge(hi_ready, b.count(2, i + 1))
                        v.tensor_tensor(T_lo[i][:, b.slot, :], ps_T[i][b.slot][:, :], T_hi[i][:, b.slot, :].bitcast(F32),
                                        ALU.subtract).then_inc(lo_ready, 1)

                def reciprocal(b):
                    if b.real():
                        if b.at(-1).real():
                            dve_.wait_ge(x_new, b.at(-1).count(1 if layer == 3 else 2))
                        dve_.wait_ge(sd_ready, b.count(1))
                        v.reciprocal(rs[:, :], sd[:, :]).then_inc(rs_ready, 1)

                def shift(b):
                    if b.real():
                        dve_.wait_ge(rs_ready, b.count(1))
                        v.scalar_tensor_tensor(nmr[:, :], mv[:, 0:1], -1.0, rs[:, :], ALU.mult, ALU.mult).then_inc(co_ready, 1)

                def moments(b):
                    if b.real():
                        dve_.wait_ge(y_ready, b.count(1))
                        v.bn_stats(st[:, :], y[:, b.slot, :]).then_inc(st_ready, 1)

                def variance(b):
                    if b.real():
                        if b.at(-1).real():
                            dve_.wait_ge(co_ready, b.at(-1).count(1))
                        dve_.wait_ge(st_ready, b.count(1))
                        dve_.sem_inc(turn, 1)
                        v.bn_aggr(mv[:, :], st[:, :]).then_inc(mv_ready, 1)

                def out_of(b):
                    if b.real():
                        dve_.wait_ge(o_out, b.count(1))
                        if layer == 1:
                            v.tensor_tensor(Y[:, cols(b.number())], ps_out[b.slot][:, :], vec[0][:, :], ALU.add).then_inc(o_used, 1)
                            return
                        if b.at(-2).real():
                            dve_.wait_ge(x_new, b.at(-2).count(1 if layer == 3 else 2))
                        v.tensor_tensor(y[:, b.slot, :], ps_out[b.slot][:, :], vec[0][:, :], ALU.add).then_inc(o_used, 1)

                def x_kept(b):
                    if layer == 3 and b.real():
                        if b.at(-1).real():
                            dve_.wait_ge(y_ready, b.at(-1).count(1))
                        dve_.sem_inc(turn, 1)
                        v.tensor_scalar(xk[:, :], X[:, cols(b.number())], keep[:, bass.ds(b.number(), 1)], None, ALU.mult).then_inc(xk_ready, 1)

                def y_of(b):
                    if layer > 1 and b.real():
                        dve_.wait_ge(o_used, b.count(1))
                        if layer == 2:
                            v.tensor_tensor(y[:, b.slot, :], y[:, b.slot, :], X[:, cols(b.number())], ALU.add).then_inc(y_ready, 1)
                        else:
                            dve_.wait_ge(xk_ready, b.count(1))
                            dve_.sem_inc(turn, 1)
                            v.scalar_tensor_tensor(y[:, b.slot, :], y[:, b.slot, :], has[:, bass.ds(b.number(), 1)], xk[:, :],
                                                   ALU.mult, ALU.add).then_inc(y_ready, 1)

                def step(s):
                    if s.it2 is None and s.k == -1:
                        split_weights_lo(v, dve_, w_raw, w_hi, w_lo, w_hi_ready, w_lo_ready)
                        dve_.wait_ge(v_in, 16 * len(vecs))
                        if layer > 1:
                            v.tensor_tensor(vec[0][:, :], vec[0][:, :], vec[1][:, :], ALU.add).then_inc(v_in, 1)
                            dve_.wait_ge(v_in, 16 * len(vecs) + 1)
                    out_of(s.at(-1))
                    x_kept(s.at(-1))
                    if layer > 1:
                        reciprocal(s.at(-2))
                    mean_of(s.at(2))
                    y_of(s.at(-1))
                    if layer > 1:
                        shift(s.at(-2))
                    low(s.at(1), 0)
                    if layer > 1:
                        moments(s.at(-1))
                    low(s.at(1), 1)
                    if layer > 1:
                        variance(s.at(-1))
                tile_steps(dve_, -2, R + 1, step, 4 if layer > 1 else 2)
                if layer == 1:
                    dve_.wait_ge(s_out, 1)
                    v.tensor_scalar(mean[:, :], ps_s[:, :], 1.0 / N, None, ALU.mult).then_inc(scale_ready, 1)
                    dve_.wait_ge(scale_ready, 1)
                    with dve_.Fori(0, R) as r:
                        v.tensor_tensor(Y[:, cols(r)], Y[:, cols(r)], mean[:, :], ALU.subtract).then_inc(c_ready, 1)
                    dve_.wait_ge(var_ready, 1)
                    v.reciprocal(mean[:, :], scale[:, :]).then_inc(scale_ready, 1)
                    dve_.wait_ge(scale_ready, 2)
                    v.tensor_tensor(scale[:, :], mean[:, :], vec[1][:, :], ALU.mult).then_inc(scale_ready, 1)
                    dve_.wait_ge(scale_ready, 3)

                    def step_act(s):
                        b = s.at(1)
                        if b.real():
                            if b.at(-2).real():
                                dve_.wait_ge(tbe_ready, b.at(-2).count(1))
                            v.tensor_tensor(t_sc[:, b.slot, :], Y[:, cols(b.number())], scale[:, :], ALU.mult).then_inc(tsc_ready, 1)
                        if s.real():
                            dve_.wait_ge(tbe_ready, s.count(1))
                            if s.at(-1).real():
                                dve_.wait_ge(y_ready, s.at(-1).count(1))
                            v.scalar_tensor_tensor(t_act[:, :], t_be[:, s.slot, :], 0.01, t_be[:, s.slot, :], ALU.mult, ALU.max).then_inc(tact_ready, 1)
                        reciprocal(s.at(-1))
                        if s.real():
                            if s.at(-2).real():
                                dve_.wait_ge(x_new, s.at(-2).count(2))
                            dve_.wait_ge(tact_ready, s.count(1))
                            v.scalar_tensor_tensor(y[:, s.slot, :], X[:, cols(s.number())], 2.0, t_act[:, :], ALU.mult, ALU.add).then_inc(y_ready, 1)
                        shift(s.at(-1))
                        moments(s)
                        variance(s)
                    tile_steps(dve_, -1, R, step_act)

            @block.tensor
            def _(pe):
                t = nc.tensor
                is_slow = pe.value_load(slow[0:1, 0:1], min_val=0, max_val=1)

                def sums(b):
                    if b.real():
                        pe.wait_ge(a_in[b.slot], b.slot_count(16))
                        if b.at(-2).real():
                            pe.wait_ge(ms_ready, b.at(-2).count(1))
                        pe.sem_inc(turn, 1)
                        with pe.If(is_slow):
                            sums_in(b, F32)
                        with pe.Else():
                            sums_in(b, F32R)

                def sums_in(b, dt):
                    for k in range(R):
                        for i, xx in enumerate((X_hi, X_lo)):
                            last = t.matmul(ps_m[b.slot][:, :], adjT[:, b.slot, k * P:(k + 1) * P].bitcast(dt), xx[:, cols(k)].bitcast(dt),
                                            start=(k == 0 and i == 0), stop=(k == R - 1 and i == 1))
                    last.then_inc(m_out, 1)

                def turn_both(b):
                    if b.real():
                        for i in range(2):
                            if i == 0:
                                pe.wait_ge(xs_in[b.slot], b.slot_count(16))
                            else:
                                pe.wait_ge(ms_ready, b.count(1))
                            for k in range(KD):
                                last = t.transpose(ps_T[i][b.slot][:, k * P:(k + 1) * P], rows[i][:, b.slot, k * P:(k + 1) * P], ident[:, :])
                            last.then_inc(T_ready, 1)

                def products(b):
                    if b.real():
                        if b.at(-2).real():
                            pe.wait_ge(o_used, b.at(-2).count(1))
                        for i in range(2):
                            if b.it2 is None and b.k == 0:
                                pe.wait_ge(w_lo_ready, i + 1)
                            pe.wait_ge(lo_ready, b.count(2, i + 1))
                            last = three_products(nc, ps_out[b.slot], T_hi[i][:, b.slot, :], T_lo[i][:, b.slot, :],
                                                  w_hi[:, i * KD:(i + 1) * KD, :], w_lo[:, i * KD:(i + 1) * KD, :], i == 0, i == 1)
                        last.then_inc(o_out, 1)

                def step(s):
                    sums(s.at(2))
                    turn_both(s.at(1))
                    products(s)
                tile_steps(pe, -2, R - 1, step)
                if layer == 1:
                    pe.wait_ge(ones_ready, 2)
                    pe.wait_ge(o_used, R)
                    t.matmul(ps_s[:, :], valid[:, :], Y[:, cols(R - 1)], start=True, stop=False)
                    pe.wait_ge(total_ready, R)
                    t.matmul(ps_s[:, :], ones[:, :], total[:, :], start=False, stop=True).then_inc(s_out, 1)

                    def square_sums(s):
                        pe.wait_ge(sq_ready, s.count(1))
                        final = s.it2 is None and s.k == R - 1
                        t.matmul(ps_v[:, :], (valid if final else ones)[:, :], sq[:, s.slot, :], start=(s.it2 is None and s.k == 0),
                                 stop=final).then_inc(v_out if final else v_part, 1)
                    tile_steps(pe, 0, R - 1, square_sums)


def kernel(**inputs):
    import numpy as np
    import concourse.bacc as bacc
    from concourse.bass_utils import run_bass_kernel_spmd as run

    nc = bacc.Bacc("TRN2", target_bir_lowering=False, num_devices=1)
    a = {k: np.ascontiguousarray(v) for k, v in inputs.items()}
    edges = np.zeros((ED, NB * BE), a["edge_attr_64"].dtype)
    edges[:, :E] = a["edge_attr_64"].T
    w1 = a["L0_gnn_W1"]
    arrays = {
        "x": a["x"], "src": a["src"], "dst": a["dst"], "eaT": edges,
        "w0a": w1[0:D], "w0b": w1[D:2 * D], "w0c": w1[2 * D:], "b01": a["L0_gnn_b1"],
        "w02": a["L0_gnn_W2"], "b02": a["L0_gnn_b2"], "w03": a["L0_gnn_W3"], "b03": a["L0_gnn_b3"],
        "w04": a["L0_gnn_W4"], "b04": a["L0_gnn_b4"], "g0": a["L0_gnn_gamma"], "be0": a["L0_gnn_beta"],
        "w1l": a["L1_gnn_W_l"], "b1l": a["L1_gnn_b_l"], "w1r": a["L1_gnn_W_r"], "g1": a["L1_gnn_gamma"],
        "be1": a["L1_gnn_beta"], "w21": a["L2_gnn_W1"].T, "b21": a["L2_gnn_b1"], "w22": a["L2_gnn_W2"].T,
        "b22": a["L2_gnn_b2"], "w31": a["L3_gnn_W1"], "b31": a["L3_gnn_b1"], "w32": a["L3_gnn_W2"],
        "b32": a["L3_gnn_b2"],
    }
    arrays = {"in_" + k: np.ascontiguousarray(v) for k, v in arrays.items()}
    args = [nc.dram_tensor(k, v.shape, mybir.dt.from_np(v.dtype), kind="ExternalInput").ap() for k, v in arrays.items()]
    out = nc.dram_tensor("out_x", [N, D], F32, kind="ExternalOutput").ap()
    gnn(nc, *args, out)
    return run(nc, [arrays], core_ids=[0]).results[0]["out_x"]
```

```python
import concourse.bass as bass
from concourse import mybir
from contextlib import ExitStack

F32 = mybir.dt.float32
F32R = mybir.dt.float32r
F16 = mybir.dt.float16
I32 = mybir.dt.int32
ACT = mybir.ActivationFunctionType
ALU = mybir.AluOpType
AX = mybir.AxisListType

P = 128
N = 1250
D = 512
KD = D // P
E = 21250
ED = 64
R = -(-N // P)
NP = R * P
LASTR = N - (R - 1) * P
TE = 4
BE = TE * P
NB = -(-E // BE)
NB += NB % 2
LASTE = E - (NB - 1) * BE
PADE = 1 << 20
DROWS = NP + P
MAXPASS = -(-N // P)
SRC_CHUNKS = [(0, 427), (427, 427), (854, NP - 854)]
EXACT = 4096
SIN_TILES = (2, 6)
EPS = 1e-5
HALF_PI = 1.5707963267948966


class Blk:

    def __init__(self, k, lead, half, it2=None, total=NB):
        self.k, self.it2, self.total = k, it2, total
        self.lead, self.half = lead, half

    def at(self, off):
        return Blk(self.k + off, self.lead, self.half, self.it2, self.total)

    def real(self):
        assert self.it2 is None or self.k >= 0
        return self.it2 is not None or 0 <= self.k < self.total

    def count(self, per, part=None):
        return self.lead * per + (self.k * per + (per if part is None else part))

    def slot_count(self, per):
        return self.half * per + (self.k // 2 + 1) * per

    @property
    def slot(self):
        return self.k % 2

    def number(self):
        return self.k if self.it2 is None else self.it2 + self.k


FIRST_STEP, LOOP_FROM, LOOP_TO, LAST_STEP = -3, 4, NB - 5, NB + 2
assert (LOOP_TO - LOOP_FROM + 1) % 2 == 0


def steps(eng, p, body):
    lead, half = eng.snap(p * NB), eng.snap(p * (NB // 2))
    for k in range(FIRST_STEP, LOOP_FROM):
        body(Blk(k, lead, half))
    with eng.Fori(0, (LOOP_TO - LOOP_FROM + 1) // 2) as it:
        it2 = eng.snap(it * 2)
        lead2, half2 = eng.snap(lead + it2), eng.snap(half + it)
        for u in range(2):
            body(Blk(LOOP_FROM + u, lead2, half2, it2))
    for k in range(LOOP_TO + 1, LAST_STEP + 1):
        body(Blk(k, lead, half))


def cols(r, n=D):
    return bass.ds(r * n, n)


def gnn(nc, x, src, dst, eaT, w0a, w0b, w0c, b01, w02, b02, w03, b03, w04, b04, g0, be0,
        w1l, b1l, w1r, g1, be1, w21, b21, w22, b22, w31, b31, w32, b32, out):
    top = ExitStack()
    with top:
        def sb(name, shape, dt=F32, ctx=top):
            return ctx.enter_context(nc.sbuf_tensor(name, shape, dt))

        def pb(name, shape, ctx):
            return ctx.enter_context(nc.psum_tensor(name, shape, F32))

        def sem(name):
            return top.enter_context(nc.semaphore(name))

        def dram(name, shape):
            return nc.dram_tensor(name, shape, F32, kind="Internal").ap()

        p_dram = dram("p_dram", [NP, D])
        q_dram = dram("q_dram", [NP, D])
        agg_dram = dram("agg_dram", [DROWS, D])
        adj_dram = dram("adj_dram", [DROWS, NP])
        adjT_dram = dram("adjT_dram", [R * P, NP])

        ident = sb("ident", [P, P])
        deg = sb("deg", [P, R])
        rdeg = sb("rdeg", [P, R])
        nrdeg = sb("nrdeg", [P, R])
        has = sb("has", [P, R])
        eps_col = sb("eps_col", [P, 1])
        half_pi = sb("half_pi", [P, 1])
        slow = sb("slow", [1, 1], I32)

        with ExitStack() as edges:
            relT = sb("relT", [P, TE, NB], F32, edges)
            srcT = sb("srcT", [P, TE, NB], F32, edges)
            idx_all = sb("idx_all", [P, NB * 2 * TE], I32, edges)
            base_f = sb("base_f", [1, NB], F32, edges)
            base_i = sb("base_i", [1, NB], I32, edges)
            npass = sb("npass", [1, 1], I32, edges)
            iota_src = sb("iota_src", [P, NP], F16, edges)
            w2_hi, w2_lo = sb("w2_hi", [P, KD, D], F32R, edges), sb("w2_lo", [P, KD, D], F32R, edges)
            wc_hi, wc_lo = sb("wc_hi", [P, D], F32R, edges), sb("wc_lo", [P, D], F32R, edges)
            b2 = sb("b2", [P, D], F32, edges)
            prepare(nc, sb, pb, sem, ident, eps_col, half_pi, relT, srcT, idx_all, base_f, base_i, npass, iota_src,
                    w2_hi, w2_lo, wc_hi, wc_lo, b2, x, src, dst, w0a, w0b, w0c, b01, w02, b02, p_dram, q_dram, agg_dram, adj_dram)
            edge_phase(nc, sb, pb, sem, ident, half_pi, relT, srcT, idx_all, base_f, base_i, npass, iota_src,
                       w2_hi, w2_lo, wc_hi, wc_lo, b2, p_dram, q_dram, agg_dram, adj_dram, eaT)
        X = sb("X", [P, R * D])
        parts = [[sb(f"X_{n}0", [P, R * D], F32R) for n in ("hi", "lo")]]
        w_raw = sb("w_raw_n", [P, 2 * KD, D])
        w_hi, w_lo = sb("w_hi_n", [P, 2 * KD, D], F32R), sb("w_lo_n", [P, 2 * KD, D], F32R)
        w_in = [sem(f"w_in{i}") for i in range(2)]
        adjT = sb("adjT", [P, 2, NP])
        adj_first = [sem(f"adj_first{u}") for u in range(2)]
        layers = ((w1r, w1l, [b1l, g1, be1]), (w21, w22, [b21, b22]), (w31, w32, [b31, b32]))
        Y = sb("Y", [P, R * D])
        first_layer(nc, sb, pb, sem, ident, half_pi, eps_col, X, *parts[0], Y, w_raw, w_hi, w_lo, x, deg, rdeg, nrdeg, has, slow,
                    agg_dram, adj_dram, adjT_dram, w03, b03, w04, b04, g0, be0, layers[0][:2], w_in, adjT, adj_first)
        sems = [sem("mean_" + n) for n in MEAN_SEMS]
        for layer in (1, 2, 3):
            if layer == 2:
                parts.append([sb(f"X_{n}1", [P, R * D], F32R) for n in ("hi", "lo")])
            if layer > 1:
                with nc.Block() as block:
                    @block.sync
                    def _(sp):
                        for s in sems:
                            sp.sem_clear(s)
            used, made = parts[layer // 3], parts[layer // 2 % 2]
            mean_layer(nc, sb, pb, sem, sems, layer, ident, eps_col, X, *used, *made, Y, w_raw, w_hi, w_lo,
                       rdeg, nrdeg, has, slow, adjT_dram, w_in, layers[layer][:2] if layer < 3 else None,
                       adjT, adj_first, layers[layer - 1][2], out)


def prepare(nc, sb, pb, sem, ident, eps_col, half_pi, relT, srcT, idx_all, base_f, base_i, npass, iota_src,
            w2_hi, w2_lo, wc_hi, wc_lo, b2, x, src, dst, w0a, w0b, w0c, b01, w02, b02, p_dram, q_dram, agg_dram, adj_dram):
    with ExitStack() as ctx:
        dst_i, src_i = sb("dst_i", [NB, BE], I32, ctx), sb("src_i", [NB, BE], I32, ctx)
        dst_f, src_f = sb("dst_f", [NB, BE], F32, ctx), sb("src_f", [NB, BE], F32, ctx)
        rel_f = sb("rel_f", [NB, BE], F32, ctx)
        dstc_f = sb("dstc_f", [NB, BE], F32, ctx)
        real_f = sb("real_f", [NB, BE], F32, ctx)
        bounds = sb("bounds", [NB, 2], F32, ctx)
        span, mspan, mspan_i = sb("span", [1, NB], F32, ctx), sb("mspan", [1, 1], F32, ctx), sb("mspan_i", [1, 1], I32, ctx)
        w_raw, w2_raw = sb("w_raw", [P, 2 * KD, D], F32, ctx), sb("w2_raw", [P, KD, D], F32, ctx)
        wc_raw = sb("wc_raw", [P, D], F32, ctx)
        w_hi, w_lo = sb("w_hi", [P, 2 * KD, D], F32R, ctx), sb("w_lo", [P, 2 * KD, D], F32R, ctx)
        b1 = sb("b1", [P, D], F32, ctx)
        zeros = sb("zeros", [P, NP], F32, ctx)
        xs = sb("xs", [P, 2, D], F32, ctx)
        xT_hi, xT_lo = sb("xT_hi", [P, 2, D], F32R, ctx), sb("xT_lo", [P, 2, D], F32R, ctx)
        p_sb, q_sb = sb("p_sb", [P, 2, D], F32, ctx), sb("q_sb", [P, 2, D], F32, ctx)
        ps_idx, ps_row = pb("ps_idx", [P, 3, TE, NB], ctx), pb("ps_row", [P, 2, 64], ctx)
        ps_t = [pb(f"ps_t{i}", [P, D], ctx) for i in range(2)]
        ps_p, ps_q = pb("ps_p", [P, D], ctx), pb("ps_q", [P, D], ctx)
        (z_ready, ident_ready, b_in, idx_in, pad_set, dve, w_hi_ready, w_lo_ready, idx_tr, t_ready, hi_ready, lo_ready,
         p_ready, q_ready, p_evac, q_evac, zero_out, w2_in, w2_split) = [
            sem("prep_" + n) for n in (
                "z_ready", "ident_ready", "b_in", "idx_in", "pad_set", "dve", "w_hi_ready", "w_lo_ready", "idx_tr", "t_ready",
                "hi_ready", "lo_ready", "p_ready", "q_ready", "p_evac", "q_evac", "zero_out", "w2_in", "w2_split")]
        w_in, x_in, p_out, q_out = ([sem(f"prep_{n}{i}") for i in range(2)] for n in ("w_in", "x_in", "p_out", "q_out"))

        with nc.Block() as block:
            @block.sync
            def _(sp):
                def clear(r):
                    sp.dma_start(adj_dram[bass.ds(r * P, P), :], zeros[:, :]).then_inc(zero_out, 16)
                    sp.dma_start(agg_dram[bass.ds(r * P, P), :], zeros[:, 0:D]).then_inc(zero_out, 16)

                def step(s):
                    b = s.at(2)
                    if b.real():
                        if b.at(-2).real():
                            sp.wait_ge(t_ready, b.at(-2).count(1))
                        sp.dma_start(xs[:, b.slot, :], x[bass.ds(b.number() * P, P), :]).then_inc(x_in[b.slot], 16)
                    if s.it2 is None and s.k == -1:
                        sp.dma_start(b1[:, :], bcast(b01)).then_inc(b_in, 16)
                        sp.dma_start(w2_raw[:, :, :], by_slices(w02)).then_inc(w2_in, 16)
                        for half in range(2):
                            sp.dma_start(wc_raw[half * ED:(half + 1) * ED, :], w0c).then_inc(w2_in, 16)
                        sp.dma_start(b2[:, :], bcast(b02)).then_inc(w2_in, 16)
                        sp.wait_ge(z_ready, 1)
                        clear(R)
                    if s.real():
                        clear(s.number())
                        sp.wait_ge(p_evac, s.count(1))
                        sp.dma_start(p_dram[bass.ds(s.number() * P, P), :], p_sb[:, s.slot, :]).then_inc(p_out[s.slot], 16)
                        sp.wait_ge(q_evac, s.count(1))
                        sp.dma_start(q_dram[bass.ds(s.number() * P, P), :], q_sb[:, s.slot, :]).then_inc(q_out[s.slot], 16)
                tile_steps(sp, -2, R - 1, step)
                for u in range(2):
                    sp.wait_ge(p_out[u], 16 * (R // 2))
                    sp.wait_ge(q_out[u], 16 * (R // 2))
                sp.wait_ge(zero_out, 32 * (DROWS // P))

            @block.gpsimd
            def _(pool):
                g = nc.gpsimd
                g.memset(ident[:, :], 0.0).then_inc(ident_ready, 1)
                pool.wait_ge(ident_ready, 1)
                g.affine_select(out=ident[:, :], in_=ident[:, :], compare_op=ALU.not_equal, fill=1.0, base=0,
                                pattern=[[-1, P]], channel_multiplier=1).then_inc(ident_ready, 1)
                g.memset(zeros[:, :], 0.0).then_inc(z_ready, 1)
                g.iota(iota_src[:, :], pattern=[[1, NP]], base=0, channel_multiplier=0, allow_small_or_imprecise_dtypes=True)

            @block.vector
            def _(dve_):
                v = nc.vector
                n = [0]

                def then(ins):
                    n[0] += 1
                    ins.then_inc(dve, 1)
                    dve_.wait_ge(dve, n[0])

                v.memset(dst_i[:, :], PADE).then_inc(pad_set, 1)
                v.memset(src_i[:, :], 0).then_inc(pad_set, 1)
                v.memset(eps_col[:, :], EPS)
                v.memset(half_pi[:, :], HALF_PI)
                dve_.wait_ge(idx_in, 64)
                v.tensor_copy(src_f[:, :], src_i[:, :])
                then(v.tensor_copy(dst_f[:, :], dst_i[:, :]))
                v.tensor_reduce(bounds[:, 0:1], dst_f[:, :], AX.X, ALU.min)
                then(v.scalar_tensor_tensor(real_f[:, :], dst_f[:, :], float(PADE), dst_f[:, :], ALU.is_lt, ALU.mult))
                v.tensor_scalar(dstc_f[:, :], dst_f[:, :], float(N - 1), None, ALU.min)
                then(v.tensor_reduce(bounds[:, 1:2], real_f[:, :], AX.X, ALU.max))
                v.tensor_scalar(rel_f[:, :], dst_f[:, :], bounds[:, 0:1], None, ALU.subtract).then_inc(idx_tr, 1)
                split_weights_lo(v, dve_, w_raw, w_hi, w_lo, w_hi_ready, w_lo_ready, (0,))
                dve_.wait_ge(b_in, 16)

                def indices():
                    dve_.wait_ge(idx_tr, 2)
                    v.tensor_copy(idx_all[:, :].rearrange("p (b c) -> p c b", c=2 * TE)[:, 0:TE, :], ps_idx[:, 1, :, :])
                    v.tensor_copy(idx_all[:, :].rearrange("p (b c) -> p c b", c=2 * TE)[:, TE:, :], ps_idx[:, 2, :, :])
                    v.tensor_copy(srcT[:, :, :], ps_idx[:, 1, :, :])
                    v.tensor_copy(relT[:, :, :], ps_idx[:, 0, :, :])
                    then(v.tensor_copy(base_f[:, :], ps_row[0:1, 0, 0:NB]))
                    v.tensor_copy(base_i[:, :], base_f[:, :])
                    then(v.tensor_tensor(span[:, :], ps_row[0:1, 1, 0:NB], base_f[:, :], ALU.subtract))
                    then(v.tensor_reduce(mspan[:, :], span[:, :], AX.X, ALU.max))
                    then(v.tensor_copy(mspan_i[:, :], mspan[:, :]))
                    then(v.tensor_scalar(mspan_i[:, :], mspan_i[:, :], 7, None, ALU.arith_shift_right))
                    then(v.tensor_scalar(npass[:, :], mspan_i[:, :], 1.0, None, ALU.add))

                def step(s):
                    if s.it2 is None and s.k == 0:
                        split_weights_lo(v, dve_, w_raw, w_hi, w_lo, w_hi_ready, w_lo_ready, (1,), 1)
                    b = s.at(1)
                    if b.real():
                        dve_.wait_ge(hi_ready, b.count(1))
                        v.tensor_tensor(xT_lo[:, b.slot, :], ps_t[b.slot][:, :], xT_hi[:, b.slot, :].bitcast(F32), ALU.subtract).then_inc(lo_ready, 1)
                    if s.it2 is None and s.k == 0:
                        indices()
                    if s.it2 is None and s.k == R - 1:
                        dve_.wait_ge(w2_split, 2)
                        v.tensor_tensor(w2_lo[:, :, :], w2_raw[:, :, :], w2_hi[:, :, :].bitcast(F32), ALU.subtract)
                        v.tensor_tensor(wc_lo[:, :], wc_raw[:, :], wc_hi[:, :].bitcast(F32), ALU.subtract)
                    if s.real():
                        if s.at(-2).real():
                            dve_.wait_ge(q_out[s.slot], s.at(-2).slot_count(16))
                        dve_.wait_ge(q_ready, s.count(1))
                        v.tensor_tensor(q_sb[:, s.slot, :], ps_q[:, :], b1[:, :], ALU.add).then_inc(q_evac, 1)
                tile_steps(dve_, -1, R - 1, step)

            @block.scalar
            def _(act):
                a = nc.scalar
                act.dma_start(w_raw[:, 0:KD, :], by_slices(w0a)).then_inc(w_in[0], 16)
                act.wait_ge(pad_set, 2)
                for raw, dram_idx in ((dst_i, dst), (src_i, src)):
                    act.dma_start(raw[0:NB - 1, :], dram_idx[0:(NB - 1) * BE].rearrange("(b e) -> b e", e=BE)).then_inc(idx_in, 16)
                    act.dma_start(raw[NB - 1:NB, 0:LASTE], dram_idx[(NB - 1) * BE:E].rearrange("(b e) -> b e", b=1)).then_inc(idx_in, 16)
                act.dma_start(w_raw[:, KD:, :], by_slices(w0b)).then_inc(w_in[1], 16)
                split_weights_hi(a, act, w_in, w_raw, w_hi, w_hi_ready, halves=(0,))

                def step(s):
                    if s.it2 is None and s.k == 0:
                        split_weights_hi(a, act, w_in, w_raw, w_hi, w_hi_ready, halves=(1,))
                    b = s.at(1)
                    if b.real():
                        if b.at(-2).real():
                            act.wait_ge(q_ready, b.at(-2).count(1))
                        act.wait_ge(t_ready, b.count(1))
                        a.copy(xT_hi[:, b.slot, :], ps_t[b.slot][:, :]).then_inc(hi_ready, 1)
                    if s.it2 is None and s.k == R - 1:
                        act.wait_ge(w2_in, 64)
                        a.copy(w2_hi[:, :, :], w2_raw[:, :, :]).then_inc(w2_split, 1)
                        a.copy(wc_hi[:, :], wc_raw[:, :]).then_inc(w2_split, 1)
                    if s.real():
                        if s.at(-2).real():
                            act.wait_ge(p_out[s.slot], s.at(-2).slot_count(16))
                        act.wait_ge(p_ready, s.count(1))
                        a.copy(p_sb[:, s.slot, :], ps_p[:, :]).then_inc(p_evac, 1)
                tile_steps(act, -1, R - 1, step)

            @block.tensor
            def _(pe):
                t = nc.tensor

                def turn(b):
                    pe.wait_ge(x_in[b.slot], b.slot_count(16))
                    for k in range(KD):
                        last = t.transpose(ps_t[b.slot][:, k * P:(k + 1) * P], xs[:, b.slot, k * P:(k + 1) * P], ident[:, :])
                    last.then_inc(t_ready, 1)

                def step(s):
                    if s.at(1).real():
                        turn(s.at(1))
                    if s.it2 is None and s.k == -1:
                        pe.wait_ge(idx_tr, 1)
                        for q, rows in enumerate((rel_f, src_f, dstc_f)):
                            for c in range(TE):
                                t.transpose(ps_idx[:, q, c, :], rows[:, c * P:(c + 1) * P], ident[0:NB, 0:NB])
                        t.transpose(ps_row[0:1, 0, 0:NB], bounds[:, 0:1], ident[0:NB, 0:NB])
                        t.transpose(ps_row[0:1, 1, 0:NB], bounds[:, 1:2], ident[0:NB, 0:NB]).then_inc(idx_tr, 1)
                    if s.real():
                        pe.wait_ge(lo_ready, s.count(1))
                        for i, (ps, ready, evac) in enumerate(((ps_p, p_ready, p_evac), (ps_q, q_ready, q_evac))):
                            if s.it2 is None and s.k == 0:
                                pe.wait_ge(w_lo_ready, i + 1)
                            if s.at(-1).real():
                                pe.wait_ge(evac, s.at(-1).count(1))
                            three_products(nc, ps, xT_hi[:, s.slot, :], xT_lo[:, s.slot, :], w_hi[:, i * KD:(i + 1) * KD, :],
                                           w_lo[:, i * KD:(i + 1) * KD, :], True, True).then_inc(ready, 1)
                pe.wait_ge(ident_ready, 2)
                tile_steps(pe, -1, R - 1, step)


def edge_phase(nc, sb, pb, sem, ident, half_pi, relT, srcT, idx_all, base_f, base_i, npass, iota_src,
               w2_hi, w2_lo, wc_hi, wc_lo, b2, p_dram, q_dram, agg_dram, adj_dram, eaT):
    with ExitStack() as ctx:
        ea_raw = sb("ea_raw", [P, 2, BE], F32, ctx)
        ea_parts = sb("ea_parts", [P, 2, BE], F32R, ctx)
        idx = sb("idx", [P, 2, 2 * TE], I32, ctx)
        G = sb("G", [P, 2, TE * D], F32, ctx)
        x1 = sb("x1", [P, 2, TE * D], F32, ctx)
        h1 = sb("h1", [P, 2, TE * D], F32, ctx)
        hT_hi = sb("hT_hi", [P, 2, D], F32R, ctx)
        hT_lo = sb("hT_lo", [P, 2, D], F32R, ctx)
        x2 = sb("x2", [P, 2, TE * D], F32, ctx)
        m2 = sb("m2", [P, 2, TE * D], F32, ctx)
        m_hi, m_lo = sb("m_hi", [P, TE * D], F32R, ctx), sb("m_lo", [P, TE * D], F32R, ctx)
        oh_src = sb("oh_src", [P, 2, TE, NP], F16, ctx)
        oh_win = sb("oh_win", [P, 2, TE, P], F16, ctx)
        oh_winr = sb("oh_winr", [P, 2, TE, P], F32R, ctx)
        agg_sb = sb("agg_sb", [P, 2, D], F32, ctx)
        adj_sb = sb("adj_sb", [P, 2, NP], F32, ctx)
        ps_pre, ps_tr, ps_x2 = ([pb(f"{n}{i}", [P, D], ctx) for i in range(2)] for n in ("ps_pre", "ps_tr", "ps_x2"))
        ps_adj, ps_agg = pb("ps_adj", [P, D], ctx), pb("ps_agg", [P, D], ctx)

        (x2_evac, dve, pre_ready, x1_ready, sig1, atan1, t1_ready, h1_ready, tr_ready,
         hi_ready, hT_ready, x2_ready, sig2, atan2, t2_ready, m2_ready, mhi_ready, m_ready, oh_ready, adj_ready,
         adj_evac, agg_ready, agg_evac, summed, ea_hi, ea_ready, idx_ready, shifted, turn) = [
            sem("edge_" + n) for n in (
                "x2_evac", "dve", "pre_ready", "x1_ready", "sig1", "atan1", "t1_ready",
                "h1_ready", "tr_ready", "hi_ready", "hT_ready", "x2_ready", "sig2", "atan2", "t2_ready", "m2_ready",
                "mhi_ready", "m_ready", "oh_ready", "adj_ready", "adj_evac", "agg_ready", "agg_evac", "summed",
                "ea_hi", "ea_ready", "idx_ready", "shifted", "turn")]
        ea_in = [sem(f"edge_ea_in{i}") for i in range(2)]
        p_in = [sem(f"edge_p_in{i}") for i in range(2)]
        q_in = [sem(f"edge_q_in{i}") for i in range(2)]

        def passes(eng, body):
            n = eng.value_load(npass[0:1, 0:1], min_val=1, max_val=MAXPASS)
            with eng.Fori(0, n) as p:
                body(p)
                eng.wait_ge(summed, p * (NB * 32) + NB * 32)
                eng.sem_inc(turn, 1)

        with nc.Block() as block:
            @block.sync
            def _(sp):
                def step(s):
                    b = s.at(3)
                    if b.real():
                        if b.at(-2).real():
                            sp.wait_ge(ea_ready, b.at(-2).count(1))
                        for half in range(2):
                            sp.dma_start(ea_raw[half * ED:(half + 1) * ED, b.slot, :],
                                         eaT[:, bass.ds(b.number() * BE, BE)]).then_inc(ea_in[b.slot], 16)

                def one_pass(p):
                    steps(sp, p, step)
                passes(sp, one_pass)

            @block.gpsimd
            def _(pool):
                g = nc.gpsimd

                def wait(s, v):
                    pool.wait_ge(s, v)
                    pool.sem_inc(turn, 1)

                def gather_p(b):
                    if b.at(-2).real():
                        wait(x1_ready, b.at(-2).count(TE))
                    g.tensor_copy(idx[:, b.slot, :], idx_all[:, bass.ds(b.number() * (2 * TE), 2 * TE)]).then_inc(idx_ready, 1)
                    wait(idx_ready, b.count(1))
                    for c in range(TE):
                        g.indirect_dma_start(G[:, b.slot, c * D:(c + 1) * D], None, p_dram,
                                             bass.IndirectOffsetOnAxis(ap=idx[:, b.slot, c:c + 1], axis=0)).then_inc(p_in[b.slot], 16)

                def gather_q(b):
                    wait(p_in[b.slot], b.slot_count(16 * TE))
                    for c in range(TE):
                        g.indirect_dma_start(G[:, b.slot, c * D:(c + 1) * D], None, q_dram,
                                             bass.IndirectOffsetOnAxis(ap=idx[:, b.slot, TE + c:TE + c + 1], axis=0),
                                             compute_op=ALU.add).then_inc(q_in[b.slot], 16)

                def window(b):
                    if b.real():
                        if b.at(-1).real():
                            wait(summed, b.at(-1).count(32))
                        wait(adj_evac, b.count(len(SRC_CHUNKS)))
                        wait(agg_evac, b.count(1))
                        row = g.value_load(base_i[0:1, bass.ds(b.number(), 1)], min_val=0, max_val=NP)
                        g.dma_start(adj_dram[bass.ds(row, P), :], adj_sb[:, b.slot, :], accum_op=ALU.add).then_inc(summed, 16)
                        g.dma_start(agg_dram[bass.ds(row, P), :], agg_sb[:, b.slot, :], accum_op=ALU.add).then_inc(summed, 16)

                def step(s):
                    b = s.at(3)
                    if b.k == 0 and b.it2 is None:
                        gather_p(b)
                        gather_q(b)
                        gather_p(b.at(1))
                        gather_q(b.at(1))
                    elif b.real() and (b.k > 1 or b.it2 is not None):
                        gather_p(b)
                        window(s.at(-3))
                        gather_q(b)
                    else:
                        window(s.at(-3))
                    b = s.at(-1)
                    if b.real():
                        for half in range(2):
                            c = slice(half * 2 * D, (half + 1) * 2 * D)
                            if half == 0 and b.at(-1).real():
                                wait(agg_ready, b.at(-1).count(1))
                            wait(m2_ready, b.count(TE, 2 * half + 2))
                            g.tensor_scalar(m_hi[:, c], m2[:, b.slot, c], 1.0, 0.0, ALU.mult, ALU.add).then_inc(mhi_ready, 1)
                            pool.wait_ge(mhi_ready, b.count(2, half + 1))
                            g.tensor_tensor(m_lo[:, c], m2[:, b.slot, c], m_hi[:, c].bitcast(F32), ALU.subtract).then_inc(m_ready, 1)

                def one_pass(p):
                    wait(shifted, p + 1)
                    steps(pool, p, step)
                passes(pool, one_pass)

            def passes_dve(dve_, body):
                v = nc.vector
                n = dve_.value_load(npass[0:1, 0:1], min_val=1, max_val=MAXPASS)
                with dve_.Fori(0, n) as p:
                    body(p)
                    dve_.wait_ge(summed, p * (NB * 32) + NB * 32)
                    v.tensor_scalar(relT[:, :, :], relT[:, :, :], float(P), None, ALU.subtract)
                    v.tensor_scalar(base_f[:, :], base_f[:, :], float(P), float(NP), ALU.add, ALU.min).then_inc(dve, 1)
                    dve_.wait_ge(dve, p + 1)
                    v.tensor_copy(base_i[:, :], base_f[:, :]).then_inc(shifted, 1)

            @block.vector
            def _(dve_):
                v = nc.vector

                def split_edge_attr(b):
                    if b.real():
                        dve_.wait_ge(ea_in[b.slot], b.slot_count(32))
                        if b.at(-2).real():
                            dve_.wait_ge(pre_ready, b.at(-2).count(TE))
                        v.tensor_copy(ea_parts[:, b.slot, :], ea_raw[:, b.slot, :]).then_inc(ea_hi, 1)
                        dve_.wait_ge(ea_hi, b.count(1))
                        v.tensor_tensor(ea_parts[ED:P, b.slot, :], ea_raw[ED:P, b.slot, :],
                                        ea_parts[ED:P, b.slot, :].bitcast(F32), ALU.subtract).then_inc(ea_ready, 1)

                def x2_of(b, e):
                    if b.real():
                        dve_.wait_ge(x2_ready, b.count(TE, e + 1))
                        v.tensor_tensor(x2[:, b.slot, cols(e)], ps_x2[e % 2][:, :], b2[:, :], ALU.add).then_inc(x2_evac, 1)

                def x1_of(b, e):
                    if b.real():
                        if e == 0:
                            dve_.wait_ge(q_in[b.slot], b.slot_count(16 * TE))
                        dve_.wait_ge(pre_ready, b.count(TE, e + 1))
                        v.tensor_tensor(x1[:, b.slot, cols(e)], ps_pre[e % 2][:, :], G[:, b.slot, cols(e)], ALU.add).then_inc(x1_ready, 1)

                def low(b, e):
                    if b.real():
                        dve_.wait_ge(hi_ready, b.count(TE, e + 1))
                        v.tensor_tensor(hT_lo[:, e % 2, :], ps_tr[e % 2][:, :], hT_hi[:, e % 2, :].bitcast(F32), ALU.subtract).then_inc(hT_ready, 1)

                def one_hots(b, e):
                    if b.real():
                        if e == 0 and b.at(-2).real():
                            dve_.wait_ge(adj_ready, b.at(-2).count(len(SRC_CHUNKS)))
                            dve_.sem_inc(turn, 1)
                        i = bass.ds(b.number(), 1)
                        v.tensor_scalar(oh_src[:, b.slot, e, :], iota_src[:, :], srcT[:, e, i], None, ALU.is_equal)
                        v.tensor_scalar(oh_win[:, b.slot, e, :], iota_src[:, 0:P], relT[:, e, i], None, ALU.is_equal)
                        v.tensor_scalar(oh_winr[:, b.slot, e, :], iota_src[:, 0:P], relT[:, e, i], None, ALU.is_equal).then_inc(oh_ready, 1)

                def window_sums(b):
                    if b.real():
                        if b.at(-2).real():
                            dve_.wait_ge(summed, b.at(-2).count(32))
                        dve_.wait_ge(agg_ready, b.count(1))
                        v.tensor_copy(agg_sb[:, b.slot, :], ps_agg[:, :]).then_inc(agg_evac, 1)

                def messages(b, half):
                    if b.real():
                        dve_.wait_ge(t2_ready, b.count(2, half + 1))
                        for e in (2 * half, 2 * half + 1):
                            v.tensor_tensor(m2[:, b.slot, cols(e)], x2[:, b.slot, cols(e)], m2[:, b.slot, cols(e)], ALU.mult).then_inc(m2_ready, 1)

                def h1_of(b, half):
                    if b.real():
                        dve_.wait_ge(t1_ready, b.count(2, half + 1))
                        for e in (2 * half, 2 * half + 1):
                            v.tensor_tensor(h1[:, b.slot, cols(e)], x1[:, b.slot, cols(e)], h1[:, b.slot, cols(e)],
                                            ALU.mult).then_inc(h1_ready, 1)

                def step(s):
                    x2_of(s.at(-1), 3)
                    x1_of(s.at(2), 0)
                    one_hots(s.at(-1), 0)
                    one_hots(s.at(-1), 1)
                    low(s, 1)
                    split_edge_attr(s.at(3))

                    x2_of(s, 0)
                    x1_of(s.at(2), 1)
                    one_hots(s.at(-1), 2)
                    one_hots(s.at(-1), 3)
                    low(s, 2)
                    messages(s.at(-1), 0)

                    x2_of(s, 1)
                    x1_of(s.at(2), 2)
                    low(s, 3)
                    h1_of(s.at(1), 0)
                    messages(s.at(-1), 1)
                    h1_of(s.at(1), 1)
                    window_sums(s.at(-2))

                    x2_of(s, 2)
                    x1_of(s.at(2), 3)
                    low(s.at(1), 0)

                dve_.sem_inc(shifted, 1)

                def one_pass(p):
                    steps(dve_, p, step)
                passes_dve(dve_, one_pass)

            @block.scalar
            def _(act):
                a = nc.scalar

                def evac_adj(b, j):
                    if b.real():
                        if j == 0 and b.at(-2).real():
                            act.wait_ge(summed, b.at(-2).count(32))
                        o, n = SRC_CHUNKS[j]
                        act.wait_ge(adj_ready, b.count(len(SRC_CHUNKS), j + 1))
                        a.copy(adj_sb[:, b.slot, o:o + n], ps_adj[:, 0:n]).then_inc(adj_evac, 1)

                def high(b, e):
                    if b.real():
                        act.wait_ge(tr_ready, b.count(TE, e + 1))
                        a.copy(hT_hi[:, e % 2, :], ps_tr[e % 2][:, :]).then_inc(hi_ready, 1)

                def arctan(b, half, x_, ready, free, t_, sig, atan):
                    if b.real():
                        c = slice(half * 2 * D, (half + 1) * 2 * D)
                        act.wait_ge(ready, b.count(TE, 2 * half + 2))
                        free(b, half)
                        a.activation(t_(b)[:, c], x_[:, b.slot, c], ACT.Sigmoid, scale=-1.0).then_inc(sig, 1)
                        act.wait_ge(sig, b.count(2, half + 1))
                        a.activation(t_(b)[:, c], t_(b)[:, c], ACT.Arctan).then_inc(atan, 1)

                def sine(b, half, t_, atan, ready):
                    if b.real():
                        c = slice(half * 2 * D, (half + 1) * 2 * D)
                        act.wait_ge(atan, b.count(2, half + 1))
                        a.activation(t_(b)[:, c], t_(b)[:, c], ACT.Sin, scale=-2.0, bias=half_pi[:, :]).then_inc(ready, 1)

                def h1_free(b, half):
                    if b.at(-2).real():
                        act.wait_ge(tr_ready, b.at(-2).count(TE))

                def m2_free(b, half):
                    if b.at(-2).real():
                        act.wait_ge(m_ready, b.at(-2).count(2, half + 1))

                def arctan1(b, half):
                    arctan(b, half, x1, x1_ready, h1_free, lambda b: h1[:, b.slot, :], sig1, atan1)

                def arctan2(b, half):
                    arctan(b, half, x2, x2_evac, m2_free, lambda b: m2[:, b.slot, :], sig2, atan2)

                def sine1(b, half):
                    sine(b, half, lambda b: h1[:, b.slot, :], atan1, t1_ready)

                def sine2(b, half):
                    sine(b, half, lambda b: m2[:, b.slot, :], atan2, t2_ready)

                def step(s):
                    arctan2(s.at(-1), 1)
                    high(s, 1)
                    sine2(s.at(-1), 0)
                    sine2(s.at(-1), 1)
                    evac_adj(s.at(-2), 0)
                    high(s, 2)
                    sine1(s.at(1), 0)
                    sine1(s.at(1), 1)
                    evac_adj(s.at(-2), 1)
                    high(s, 3)
                    arctan1(s.at(2), 0)
                    high(s.at(1), 0)
                    evac_adj(s.at(-2), 2)
                    arctan2(s, 0)
                    arctan1(s.at(2), 1)

                def one_pass(p):
                    steps(act, p, step)
                passes(act, one_pass)

            @block.tensor
            def _(pe):
                t = nc.tensor

                def bank_free(sem, b, c):
                    if c >= 2:
                        pe.wait_ge(sem, b.count(TE, c - 1))
                    elif b.at(-1).real():
                        pe.wait_ge(sem, b.at(-1).count(TE, c + 3))

                def rest_of_first(b, c):
                    if c == 0:
                        pe.wait_ge(ea_ready, b.count(1))
                    bank_free(x1_ready, b, c)
                    for i, w in enumerate((wc_hi, wc_lo)):
                        last = t.matmul(ps_pre[c % 2][:, :], ea_parts[:, b.slot, c * P:(c + 1) * P], w[:, :], start=(i == 0), stop=(i == 1))
                    last.then_inc(pre_ready, 1)

                def adjacency(b, j):
                    chunks = len(SRC_CHUNKS)
                    if j == 0:
                        pe.wait_ge(oh_ready, b.count(TE))
                    if j > 0:
                        pe.wait_ge(adj_evac, b.count(chunks, j))
                    elif b.at(-1).real():
                        pe.wait_ge(adj_evac, b.at(-1).count(chunks))
                    o, n = SRC_CHUNKS[j]
                    for k in range(TE):
                        last = t.matmul(ps_adj[:, 0:n], oh_win[:, b.slot, k, :], oh_src[:, b.slot, k, o:o + n], start=(k == 0), stop=(k == TE - 1))
                    last.then_inc(adj_ready, 1)

                def sums(b):
                    pe.wait_ge(m_ready, b.count(2))
                    if b.at(-1).real():
                        pe.wait_ge(agg_evac, b.at(-1).count(1))
                    for k in range(TE):
                        for i, m in enumerate((m_hi, m_lo)):
                            last = t.matmul(ps_agg[:, :], oh_winr[:, b.slot, k, :], m[:, cols(k)], start=(k == 0 and i == 0),
                                            stop=(k == TE - 1 and i == 1))
                    last.then_inc(agg_ready, 1)

                def turn_h(b, c):
                    pe.wait_ge(h1_ready, b.count(TE, c + 1))
                    bank_free(hT_ready, b, c)
                    for k in range(KD):
                        last = t.transpose(ps_tr[c % 2][:, k * P:(k + 1) * P], h1[:, b.slot, c * D + k * P:c * D + (k + 1) * P], ident[:, :])
                    last.then_inc(tr_ready, 1)

                def second(b, c):
                    pe.wait_ge(hT_ready, b.count(TE, c + 1))
                    bank_free(x2_evac, b, c)
                    three_products(nc, ps_x2[c % 2], hT_hi[:, c % 2, :], hT_lo[:, c % 2, :], w2_hi, w2_lo, True, True).then_inc(x2_ready, 1)

                def step(s):
                    for c in range(TE):
                        if s.at(2).real():
                            rest_of_first(s.at(2), c)
                        if s.at(-2).real():
                            if c == 1:
                                sums(s.at(-2))
                            else:
                                adjacency(s.at(-2), max(0, c - 1))
                        b = s if c < TE - 1 else s.at(1)
                        if b.real():
                            turn_h(b, (c + 1) % TE)
                        if s.real():
                            second(s, c)

                def one_pass(p):
                    steps(pe, p, step)
                passes(pe, one_pass)


def tile_steps(eng, first, last, body, lo=2, hi=R - 3):
    for k in range(first, lo):
        body(Blk(k, 0, 0, total=R))
    with eng.Fori(0, (hi - lo + 1) // 2) as it:
        it2 = eng.snap(it * 2)
        for u in range(2):
            body(Blk(lo + u, it2, it, it2, total=R))
    for k in range(hi + 1, last + 1):
        body(Blk(k, 0, 0, total=R))


assert R % 2 == 0 and R >= 6


def three_products(nc, ps, a_hi, a_lo, w_hi, w_lo, first, last):
    for k in range(KD):
        for i, (a, w) in enumerate(((a_hi, w_hi), (a_hi, w_lo), (a_lo, w_hi))):
            ins = nc.tensor.matmul(ps[:, :], a[:, k * P:(k + 1) * P], w[:, k, :], start=(first and k == 0 and i == 0),
                                   stop=(last and k == KD - 1 and i == 2))
    return ins


def bcast(vec):
    return vec.rearrange("(a d) -> a d", a=1).to_broadcast([P, D])


def by_slices(w):
    return w.rearrange("(k p) d -> p k d", p=P)


def split_weights_hi(a, act, w_in, w_raw, w_hi, w_hi_ready, loads=1, halves=(0, 1)):
    for i in halves:
        act.wait_ge(w_in[i], 16 * loads)
        a.copy(w_hi[:, i * KD:(i + 1) * KD, :], w_raw[:, i * KD:(i + 1) * KD, :]).then_inc(w_hi_ready, 1)


def split_weights_lo(v, dve_, w_raw, w_hi, w_lo, w_hi_ready, w_lo_ready, halves=(0, 1), before=0):
    for n, i in enumerate(halves):
        c = slice(i * KD, (i + 1) * KD)
        dve_.wait_ge(w_hi_ready, before + n + 1)
        v.tensor_tensor(w_lo[:, c, :], w_raw[:, c, :], w_hi[:, c, :].bitcast(F32), ALU.subtract).then_inc(w_lo_ready, 1)


def first_layer(nc, sb, pb, sem, ident, half_pi, eps_col, X, X_hi, X_lo, Z, w_raw, w_hi, w_lo, x, deg, rdeg, nrdeg, has, slow,
                agg_dram, adj_dram, adjT_dram, w03, b03, w04, b04, g0, be0, w_next, w_next_in, adjT, adj_first):
    with ExitStack() as ctx:
        b3, b4 = sb("b3", [P, D], F32, ctx), sb("b4", [P, D], F32, ctx)
        rows = [sb(f"n0_{n}", [P, 2, D], F32, ctx) for n in ("xs", "ag")]
        T_hi = [sb(f"n0_T_hi{i}", [P, 2, D], F32R, ctx) for i in range(2)]
        T_lo = [sb(f"n0_T_lo{i}", [P, 2, D], F32R, ctx) for i in range(2)]
        adj_in, adjT_sb = sb("adj_in", [P, 2, NP], F32, ctx), sb("adjT_sb", [P, 2, NP], F32, ctx)
        TH = sb("TH", [P, R * D], F32, ctx)
        adj_flat, adjT_flat = (t[:, :, :].rearrange("p u n -> p (u n)") for t in (adj_in, adjT_sb))
        us, y_out = rows
        y_in, y_sc, gam, bet = (adjT_flat[:, cols(i)] for i in range(4))
        xn = [t[:, cols(4)] for t in (adj_flat, adjT_flat)]
        xb4, xbet = (adj_flat[:, i * D:(i + 2) * D].rearrange("p (u d) -> p u d", d=D) for i in (0, 2))
        st = [sb(f"n0_st{i}", [P, 6], F32, ctx) for i in range(2)]
        mv = [sb(f"n0_mv{i}", [P, 2], F32, ctx) for i in range(2)]
        sd = [sb(f"n0_sd{i}", [P, 1], F32, ctx) for i in range(2)]
        rs = [sb(f"n0_rs{i}", [P, 1], F32, ctx) for i in range(2)]
        nmr = sb("n0_nmr", [P, 1], F32, ctx)
        mdeg, mdeg1, gt = sb("mdeg", [P, 1], F32, ctx), sb("mdeg1", [1, 1], F32, ctx), sb("gt", [1, 1], F32, ctx)
        ps_T = [[pb(f"n0_ps_T{i}{u}", [P, D], ctx) for u in range(2)] for i in range(2)]
        ps_adj, ps_out = pb("n0_ps_adj", [P, NP], ctx), pb("n0_ps_out", [P, D], ctx)
        ps_y, ps_nT, ps_n = [ps_out, ps_T[1][0]], [ps_T[1][1], ps_adj[:, 0:D]], ps_adj[:, D:2 * D]
        row_in = [sem(f"n0_row_in{u}") for u in range(2)]
        a_in = [sem(f"n0_a_in{u}") for u in range(2)]
        aT_out = [sem(f"n0_aT_out{u}") for u in range(2)]
        st_ready, mv_ready, sd_ready, rs_ready = ([sem(f"n0_{n}{i}") for i in range(2)] for n in (
            "st_ready", "mv_ready", "sd_ready", "rs_ready"))
        w_in = [sem(f"n0_w_in{i}") for i in range(2)]
        (x_in, w4_in, c_in, gb_in, w_hi_ready, w_lo_ready, T_ready, hi_ready, lo_ready, z_out, z_ready, sig, atan, t_ready,
         aT_ready, aT_evac, d_ready, c_dve, deg_tr, us_ready, xb_ready, xe_ready, u_T, u_hi, u_lo, y_ready, y_used, sc_ready,
         res_ready, co_ready, x_new, xlo_ready, turn) = [
            sem("n0_" + n) for n in (
                "x_in", "w4_in", "c_in", "gb_in", "w_hi_ready", "w_lo_ready", "T_ready", "hi_ready", "lo_ready", "z_out", "z_ready",
                "sig", "atan", "t_ready", "aT_ready", "aT_evac", "d_ready", "c_dve", "deg_tr", "us_ready", "xb_ready",
                "xe_ready", "u_T", "u_hi", "u_lo", "y_ready", "y_used", "sc_ready", "res_ready", "co_ready", "x_new",
                "xlo_ready", "turn")]

        with nc.Block() as block:
            @block.sync
            def _(sp):
                def step(s):
                    b = s.at(2)
                    if b.real():
                        if b.at(-2).real():
                            sp.wait_ge(T_ready, b.at(-2).count(2))
                        sp.dma_start(rows[0][:, b.slot, :], x[bass.ds(b.number() * P, P), :]).then_inc(row_in[b.slot], 16)
                        sp.dma_start(rows[1][:, b.slot, :], agg_dram[bass.ds(b.number() * P, P), :]).then_inc(row_in[b.slot], 16)
                        if b.at(-2).real():
                            sp.wait_ge(aT_ready, b.at(-2).count(1))
                            sp.wait_ge(d_ready, b.at(-2).count(1))
                        sp.dma_start(adj_in[:, b.slot, :], adj_dram[bass.ds(b.number() * P, P), :]).then_inc(a_in[b.slot], 16)
                    if s.real():
                        sp.dma_start(X[:, cols(s.number())], x[bass.ds(s.number() * P, P), :]).then_inc(x_in, 16)
                        sp.wait_ge(aT_evac, s.count(1))
                        sp.dma_start(adjT_dram[bass.ds(s.number() * P, P), :], adjT_sb[:, s.slot, :]).then_inc(aT_out[s.slot], 16)
                tile_steps(sp, -2, R - 1, step)
                for u in range(2):
                    sp.wait_ge(aT_out[u], 16 * (R // 2))
                for t, b in ((gam, g0), (bet, be0)):
                    sp.dma_start(t, bcast(b)).then_inc(gb_in, 16)
                for u in range(2):
                    sp.dma_start(adjT[:, u, :], adjT_dram[u * P:(u + 1) * P, :]).then_inc(adj_first[u], 16)

                def x_new_load(s):
                    if s.at(-2).real():
                        sp.wait_ge(T_ready, s.at(-2).count(1) + 2 * R)
                        sp.sem_inc(turn, 1)
                    sp.wait_ge(x_new, s.count(2))
                    sp.dma_start(xn[s.slot], X[:, cols(s.number())]).then_inc(row_in[s.slot], 16)
                tile_steps(sp, 0, R - 1, x_new_load)

            @block.scalar
            def _(act):
                a = nc.scalar
                for i in range(2):
                    act.dma_start(w_raw[:, i * KD:(i + 1) * KD, :], by_slices(w03[i * D:(i + 1) * D, :])).then_inc(w_in[i], 16)
                for t, b in ((b3, b03), (b4, b04)):
                    act.dma_start(t[:, :], bcast(b)).then_inc(c_in, 16)

                def step(s):
                    b = s.at(1)
                    if b.real():
                        if b.at(-2).real():
                            act.wait_ge(z_out, b.at(-2).count(1))
                        for i in range(2):
                            if s.it2 is None and s.k == -1:
                                split_weights_hi(a, act, w_in, w_raw, w_hi, w_hi_ready, halves=(i,))
                            act.wait_ge(T_ready, b.count(2, i + 1))
                            a.copy(T_hi[i][:, b.slot, :], ps_T[i][b.slot][:, :]).then_inc(hi_ready, 1)
                    b = s.at(-1)
                    if b.real():
                        act.wait_ge(z_ready, b.count(1))
                        act.sem_inc(turn, 1)
                        a.activation(TH[:, cols(b.number())], Z[:, cols(b.number())], ACT.Sigmoid, scale=-1.0).then_inc(sig, 1)
                        act.wait_ge(sig, b.count(1))
                        act.sem_inc(turn, 1)
                        a.activation(TH[:, cols(b.number())], TH[:, cols(b.number())], ACT.Arctan).then_inc(atan, 1)
                    if s.real():
                        if s.at(-2).real():
                            act.wait_ge(aT_out[s.slot], s.at(-2).slot_count(16))
                        act.wait_ge(aT_ready, s.count(1))
                        a.copy(adjT_sb[:, s.slot, :], ps_adj[:, :]).then_inc(aT_evac, 1)
                tile_steps(act, -1, R, step)
                act.wait_ge(atan, R)
                for r0, r1 in zip((0, *SIN_TILES), (*SIN_TILES, R)):
                    c = slice(r0 * D, r1 * D)
                    a.activation(TH[:, c], TH[:, c], ACT.Sin, scale=-2.0, bias=half_pi[:, :]).then_inc(t_ready, 1)

                def step2(s):
                    b = s.at(1)
                    if b.real():
                        if b.at(-2).real():
                            act.wait_ge(y_ready, b.at(-2).count(1))
                        act.wait_ge(u_T, b.count(1))
                        a.copy(T_hi[0][:, b.slot, :], ps_T[0][b.slot][:, :]).then_inc(u_hi, 1)
                    if s.it2 is None and s.k == 0:
                        act.wait_ge(w_lo_ready, 3)
                        act.wait_ge(w_next_in[0], 16)
                        a.copy(w_hi[:, 0:KD, :], w_raw[:, 0:KD, :]).then_inc(w_hi_ready, 1)
                    b = s.at(-3)
                    if b.real():
                        act.wait_ge(co_ready, b.count(1))
                        act.sem_inc(turn, 1)
                        for t in (X[:, cols(b.number())], X_hi[:, cols(b.number())]):
                            a.activation(t, y_out[:, b.slot, :], ACT.Identity, scale=rs[1][:, :], bias=nmr[:, :]).then_inc(x_new, 1)
                    for j, b in enumerate((s.at(-1), s.at(-2))):
                        if b.real():
                            act.wait_ge(mv_ready[j], b.count(1))
                            a.activation(sd[j][:, :], mv[j][:, 1:2], ACT.Sqrt, bias=eps_col[:, :]).then_inc(sd_ready[j], 1)
                    n = s.at(-4)
                    if n.real():
                        act.wait_ge(T_ready, n.count(1) + 2 * R)
                        a.copy(T_hi[1][:, n.slot, :], ps_nT[n.slot][:, :]).then_inc(hi_ready, 1)
                    n = s.at(-5)
                    if n.real():
                        act.wait_ge(z_out, n.count(1) + R)
                        act.sem_inc(turn, 1)
                        a.copy(Z[:, cols(n.number())], ps_n).then_inc(z_ready, 1)
                tile_steps(act, -1, R + 4, step2, 5, R - 2)

            @block.gpsimd
            def _(pool):
                g = nc.gpsimd

                def wait(s, v):
                    pool.wait_ge(s, v)
                    pool.sem_inc(turn, 1)

                wait(w_lo_ready, 2)
                g.dma_start(w_raw[:, KD:, :], by_slices(w04)).then_inc(w4_in, 16)
                g.dma_start(w_raw[:, 0:KD, :], by_slices(w_next[0])).then_inc(w_next_in[0], 16)
                wait(c_in, 32)
                wait(x_in, 16 * R)
                wait(T_ready, 2 * R)
                wait(aT_ready, R)
                wait(d_ready, R)

                def step2(s):
                    if s.it2 is None and s.k == 0:
                        wait(w_lo_ready, 3)
                        g.dma_start(w_raw[:, KD:, :], by_slices(w_next[1])).then_inc(w_next_in[1], 16)
                        wait(gb_in, 32)
                    b = s.at(2)
                    if b.real():
                        if b.at(-2).real():
                            wait(u_T, b.at(-2).count(1))
                        if b.k in (0, *SIN_TILES):
                            wait(t_ready, (0, *SIN_TILES).index(b.k) + 1)
                        g.tensor_tensor(us[:, b.slot, :], Z[:, cols(b.number())], TH[:, cols(b.number())], ALU.mult).then_inc(us_ready, 1)
                    b = s.at(1)
                    if b.real():
                        if b.at(-2).real():
                            wait(y_used, b.at(-2).count(1))
                        g.tensor_tensor(xb4[:, b.slot, :], X[:, cols(b.number())], b4[:, :], ALU.add).then_inc(xb_ready, 1)
                    b = s
                    if b.real():
                        if b.at(-2).real():
                            wait(res_ready, b.at(-2).count(1))
                        g.tensor_tensor(xbet[:, b.slot, :], X[:, cols(b.number())], bet[:, :], ALU.add).then_inc(xe_ready, 1)
                    b = s.at(-3)
                    if b.real():
                        wait(x_new, b.count(2))
                        g.tensor_tensor(X_lo[:, cols(b.number())], X[:, cols(b.number())], X_hi[:, cols(b.number())].bitcast(F32),
                                        ALU.subtract).then_inc(xlo_ready, 1)
                tile_steps(pool, -2, R + 2, step2, 4)

            @block.vector
            def _(dve_):
                v = nc.vector
                def step(s):
                    b = s.at(-1)
                    if b.real():
                        if b.it2 is None and b.k == 0:
                            dve_.wait_ge(c_in, 32)
                        dve_.wait_ge(z_out, b.count(1))
                        v.tensor_tensor(Z[:, cols(b.number())], ps_out[:, :], b3[:, :], ALU.add).then_inc(z_ready, 1)
                    b = s.at(1)
                    if b.real():
                        for i in range(2):
                            if s.it2 is None and s.k == -1:
                                split_weights_lo(v, dve_, w_raw, w_hi, w_lo, w_hi_ready, w_lo_ready, (i,), i)
                            dve_.wait_ge(hi_ready, b.count(2, i + 1))
                            v.tensor_tensor(T_lo[i][:, b.slot, :], ps_T[i][b.slot][:, :], T_hi[i][:, b.slot, :].bitcast(F32),
                                            ALU.subtract).then_inc(lo_ready, 1)
                    if s.real():
                        dve_.wait_ge(a_in[s.slot], s.slot_count(16))
                        dve_.sem_inc(turn, 1)
                        v.tensor_reduce(deg[:, bass.ds(s.number(), 1)], adj_in[:, s.slot, :], AX.X, ALU.add).then_inc(d_ready, 1)
                tile_steps(dve_, -1, R, step)
                dve_.wait_ge(z_out, R)
                dve_.wait_ge(w4_in, 16)
                v.tensor_copy(w_hi[:, KD:, :], w_raw[:, KD:, :]).then_inc(w_hi_ready, 1)
                v.wait_ge(d_ready, R)
                v.tensor_reduce(mdeg[:, :], deg[:, :], AX.X, ALU.max).then_inc(deg_tr, 1)
                v.tensor_scalar(has[:, :], deg[:, :], 0.0, None, ALU.is_gt)
                v.tensor_scalar(rdeg[:, :], deg[:, :], 1.0, None, ALU.max).then_inc(c_dve, 1)
                dve_.wait_ge(w_hi_ready, 3)
                v.tensor_tensor(w_lo[:, KD:, :], w_raw[:, KD:, :], w_hi[:, KD:, :].bitcast(F32), ALU.subtract).then_inc(w_lo_ready, 1)
                dve_.wait_ge(c_dve, 1)
                v.reciprocal(rdeg[:, :], rdeg[:, :]).then_inc(c_dve, 1)
                dve_.wait_ge(c_dve, 2)
                v.tensor_scalar(nrdeg[:, :], rdeg[:, :], -1.0, None, ALU.mult)
                dve_.wait_ge(deg_tr, 2)
                v.tensor_reduce(mdeg1[:, :], ps_adj[0:1, 0:P], AX.X, ALU.max).then_inc(deg_tr, 1)
                dve_.wait_ge(deg_tr, 3)
                v.tensor_scalar(gt[:, :], mdeg1[:, :], float(EXACT), None, ALU.is_gt).then_inc(c_dve, 1)
                dve_.wait_ge(c_dve, 3)
                v.tensor_copy(slow[:, :], gt[:, :]).then_inc(c_dve, 1)

                def step2(s):
                    nxt, inner, scaled, res, new = s.at(1), s.at(-1), s.at(-2), s.at(-3), s.at(-5)
                    if s.it2 is None and s.k == 1:
                        split_weights_lo(v, dve_, w_raw, w_hi, w_lo, w_hi_ready, w_lo_ready, (0,), 3)
                    if new.real():
                        dve_.wait_ge(hi_ready, new.count(1) + 2 * R)
                        v.tensor_tensor(T_lo[1][:, new.slot, :], ps_nT[new.slot][:, :], T_hi[1][:, new.slot, :].bitcast(F32),
                                        ALU.subtract).then_inc(lo_ready, 1)
                    if nxt.real():
                        dve_.wait_ge(u_hi, nxt.count(1))
                        v.tensor_tensor(T_lo[0][:, nxt.slot, :], ps_T[0][nxt.slot][:, :], T_hi[0][:, nxt.slot, :].bitcast(F32),
                                        ALU.subtract).then_inc(u_lo, 1)
                    if res.real():
                        dve_.wait_ge(sd_ready[1], res.count(1))
                        if res.at(-1).real():
                            dve_.wait_ge(x_new, res.at(-1).count(2))
                        v.reciprocal(rs[1][:, :], sd[1][:, :]).then_inc(rs_ready[1], 1)
                    if scaled.real():
                        dve_.wait_ge(sd_ready[0], scaled.count(1))
                        v.reciprocal(rs[0][:, :], sd[0][:, :]).then_inc(rs_ready[0], 1)
                        if scaled.at(-1).real():
                            dve_.wait_ge(res_ready, scaled.at(-1).count(1))
                        v.scalar_tensor_tensor(y_sc[:, :], y_in[:, :], mv[0][:, 0:1], gam[:, :], ALU.subtract, ALU.mult).then_inc(sc_ready, 1)
                    if res.real():
                        dve_.wait_ge(rs_ready[1], res.count(1))
                        v.scalar_tensor_tensor(nmr[:, :], mv[1][:, 0:1], -1.0, rs[1][:, :], ALU.mult, ALU.mult).then_inc(co_ready, 1)
                    if inner.real():
                        dve_.wait_ge(y_ready, inner.count(1))
                        dve_.wait_ge(xb_ready, inner.count(1))
                        if inner.at(-1).real():
                            dve_.wait_ge(sc_ready, inner.at(-1).count(1))
                        v.tensor_tensor(y_in[:, :], ps_y[inner.slot][:, :], xb4[:, inner.slot, :], ALU.add).then_inc(y_used, 1)
                    if scaled.real():
                        dve_.wait_ge(rs_ready[0], scaled.count(1))
                        dve_.wait_ge(sc_ready, scaled.count(1))
                        dve_.wait_ge(xe_ready, scaled.count(1))
                        v.scalar_tensor_tensor(y_out[:, scaled.slot, :], y_sc[:, :], rs[0][:, :], xbet[:, scaled.slot, :],
                                               ALU.mult, ALU.add).then_inc(res_ready, 1)
                    if inner.real():
                        dve_.wait_ge(y_used, inner.count(1))
                        v.bn_stats(st[0][:, :], y_in[:, :]).then_inc(st_ready[0], 1)
                    if scaled.real():
                        dve_.wait_ge(res_ready, scaled.count(1))
                        v.bn_stats(st[1][:, :], y_out[:, scaled.slot, :]).then_inc(st_ready[1], 1)
                    if inner.real():
                        dve_.wait_ge(st_ready[0], inner.count(1))
                        dve_.sem_inc(turn, 1)
                        v.bn_aggr(mv[0][:, :], st[0][:, :]).then_inc(mv_ready[0], 1)
                    if scaled.real():
                        dve_.wait_ge(st_ready[1], scaled.count(1))
                        if res.real():
                            dve_.wait_ge(co_ready, res.count(1))
                        dve_.sem_inc(turn, 1)
                        v.bn_aggr(mv[1][:, :], st[1][:, :]).then_inc(mv_ready[1], 1)
                dve_.wait_ge(gb_in, 32)
                tile_steps(dve_, -1, R + 4, step2, 5, R - 2)

            @block.tensor
            def _(pe):
                t = nc.tensor

                def turn_both(b):
                    if b.real():
                        pe.wait_ge(row_in[b.slot], b.slot_count(32))
                        for i in range(2):
                            for k in range(KD):
                                last = t.transpose(ps_T[i][b.slot][:, k * P:(k + 1) * P], rows[i][:, b.slot, k * P:(k + 1) * P], ident[:, :])
                            last.then_inc(T_ready, 1)

                def step(s):
                    first = s.it2 is None and s.k == 0
                    if not first:
                        turn_both(s.at(1))
                    if s.real():
                        pe.wait_ge(a_in[s.slot], s.slot_count(16))
                        if s.at(-1).real():
                            pe.wait_ge(aT_evac, s.at(-1).count(1))
                        for k in range(R):
                            last = t.transpose(ps_adj[:, k * P:(k + 1) * P], adj_in[:, s.slot, k * P:(k + 1) * P], ident[:, :])
                        last.then_inc(aT_ready, 1)
                        if s.at(-1).real():
                            pe.wait_ge(z_ready, s.at(-1).count(1))
                        for i in range(2):
                            if first:
                                pe.wait_ge(w_lo_ready, i + 1)
                            pe.wait_ge(lo_ready, s.count(2, i + 1))
                            last = three_products(nc, ps_out, T_hi[i][:, s.slot, :], T_lo[i][:, s.slot, :], w_hi[:, i * KD:(i + 1) * KD, :],
                                                  w_lo[:, i * KD:(i + 1) * KD, :], i == 0, i == 1)
                        last.then_inc(z_out, 1)
                    if first:
                        turn_both(s.at(1))
                tile_steps(pe, -1, R - 1, step)
                pe.wait_ge(deg_tr, 1)
                pe.wait_ge(aT_evac, R)
                t.transpose(ps_adj[0:1, 0:P], mdeg[:, :], ident[:, :]).then_inc(deg_tr, 1)
                pe.wait_ge(z_ready, R)

                def step2(s):
                    b = s.at(1)
                    if b.real():
                        pe.wait_ge(us_ready, b.count(1))
                        for k in range(KD):
                            last = t.transpose(ps_T[0][b.slot][:, k * P:(k + 1) * P], us[:, b.slot, k * P:(k + 1) * P], ident[:, :])
                        last.then_inc(u_T, 1)
                    if s.real():
                        if s.it2 is None and s.k == 0:
                            pe.wait_ge(w_lo_ready, 3)
                        if s.at(-2).real():
                            pe.wait_ge(y_used, s.at(-2).count(1))
                        pe.wait_ge(u_lo, s.count(1))
                        three_products(nc, ps_y[s.slot], T_hi[0][:, s.slot, :], T_lo[0][:, s.slot, :], w_hi[:, KD:, :], w_lo[:, KD:, :],
                                       True, True).then_inc(y_ready, 1)
                    n = s.at(-4)
                    if n.real():
                        pe.wait_ge(row_in[n.slot], n.slot_count(16) + 32 * (R // 2))
                        for k in range(KD):
                            last = t.transpose(ps_nT[n.slot][:, k * P:(k + 1) * P], xn[n.slot][:, k * P:(k + 1) * P], ident[:, :])
                        last.then_inc(T_ready, 1)
                    if s.it2 is None and s.k == 4:
                        pe.wait_ge(w_lo_ready, 4)
                    n = s.at(-5)
                    if n.real():
                        pe.wait_ge(z_ready, n.count(1) + R - 1)
                        pe.wait_ge(lo_ready, n.count(1) + 2 * R)
                        three_products(nc, ps_n, T_hi[1][:, n.slot, :], T_lo[1][:, n.slot, :], w_hi[:, 0:KD, :], w_lo[:, 0:KD, :],
                                       True, True).then_inc(z_out, 1)
                pe.wait_ge(deg_tr, 3)
                tile_steps(pe, -1, R + 4, step2, 5, R - 2)


MEAN_SEMS = ("v_in", "w_hi_ready", "w_lo_ready", "m_out", "ms_ready", "T_ready", "hi_ready", "lo_ready", "o_out", "o_used",
             "y_ready", "st_ready", "mv_ready", "sd_ready", "rs_ready", "co_ready", "x_new", "xlo_ready", "turn", "stored",
             "xk_ready", "a_in0", "a_in1", "xs_in0", "xs_in1")


def mean_layer(nc, sb, pb, sem, sems, layer, ident, eps_col, X, X_hi, X_lo, new_hi, new_lo, Y, w_raw, w_hi, w_lo,
               rdeg, nrdeg, has, slow, adjT_dram, w_in, w_next, adjT, adj_first, vecs, out):
    use = (0, 1) if layer == 3 else (1,)
    n_use = len(use)
    n_ = f"n{layer}_"
    with ExitStack() as ctx:
        vec = [sb(f"{n_}vec{i}", [P, D], F32, ctx) for i in range(len(vecs))]
        rows = [sb(n_ + n, [P, 2, D], F32, ctx) if i in use or layer == 1 else None for i, n in enumerate(("xs", "ms"))]
        T_hi = [sb(f"{n_}T_hi{i}", [P, 2, D], F32R, ctx) if i in use or layer == 1 else None for i in range(2)]
        T_lo = [sb(f"{n_}T_lo{i}", [P, 2, D], F32R, ctx) if i in use or layer == 1 else None for i in range(2)]
        y = Y[:, 0:2 * D].rearrange("p (u d) -> p u d", d=D) if layer == 3 else sb(n_ + "y", [P, 2, D], F32, ctx)
        st, mv = sb(n_ + "st", [P, 6], F32, ctx), sb(n_ + "mv", [P, 2], F32, ctx)
        sd, rs, nmr = sb(n_ + "sd", [P, 1], F32, ctx), sb(n_ + "rs", [P, 1], F32, ctx), sb(n_ + "nmr", [P, 1], F32, ctx)
        ps_T = [[pb(f"{n_}ps_T{i}{u}", [P, D], ctx) for u in range(2)] for i in range(2)]
        ps_m, ps_out = ([pb(f"{n_}{n}{u}", [P, D], ctx) for u in range(2)] for n in ("ps_m", "ps_out"))
        (v_in, w_hi_ready, w_lo_ready, m_out, ms_ready, T_ready, hi_ready, lo_ready, o_out, o_used,
         y_ready, st_ready, mv_ready, sd_ready, rs_ready, co_ready, x_new, xlo_ready, turn, stored,
         xk_ready, a_in0, a_in1, xs_in0, xs_in1) = sems
        a_in, xs_in = (a_in0, a_in1), (xs_in0, xs_in1)
        if layer == 2:
            xb = sb("xb", [P, 2, D], F32, ctx)
        if layer == 3:
            keep = sb("keep", [P, R], F32, ctx)
            xk = Y[:, 2 * D:3 * D]
        if layer == 1:
            sq = sb("sq", [P, 2, D], F32, ctx)
            total = sb("total", [P, D], F32, ctx)
            ones, valid = sb("ones", [P, P], F32, ctx), sb("valid", [P, P], F32, ctx)
            mean, scale = sb("mean", [P, D], F32, ctx), sb("scale", [P, D], F32, ctx)
            t_sc, t_be, t_act = sb("t_sc", [P, 2, D], F32, ctx), rows[1], sb("t_act", [P, D], F32, ctx)
            ps_s, ps_v = ps_m
            (ones_ready, total_ready, s_out, c_ready, sq_ready, v_part, v_out, var_ready, scale_ready, tsc_ready, tbe_ready,
             tact_ready) = [
                sem("bn_" + n) for n in ("ones_ready", "total_ready", "s_out", "c_ready", "sq_ready", "v_part", "v_out",
                                         "var_ready", "scale_ready", "tsc_ready", "tbe_ready", "tact_ready")]

        with nc.Block() as block:
            @block.sync
            def _(sp):
                def adj_load(b):
                    if b.real() and b.at(-2).real():
                        sp.wait_ge(m_out, b.at(-2).count(1))
                        sp.dma_start(adjT[:, b.slot, :], adjT_dram[bass.ds(b.number() * P, P), :]).then_inc(a_in[b.slot], 16)

                def x_load(b):
                    if b.real() and 0 in use:
                        if b.at(-2).real():
                            sp.wait_ge(T_ready, b.at(-2).count(2))
                        sp.dma_start(rows[0][:, b.slot, :], X[:, cols(b.number())]).then_inc(xs_in[b.slot], 16)

                def vec_load():
                    for t, b in zip(vec, vecs):
                        sp.dma_start(t[:, :], bcast(b)).then_inc(v_in, 16)

                def step(s):
                    adj_load(s.at(2))
                    x_load(s.at(2))
                    if s.it2 is None and s.k == -1:
                        vec_load()
                    b = s.at(-3)
                    if layer == 3 and b.real():
                        sp.wait_ge(x_new, b.count(1))
                        if b.it2 is None and b.k == R - 1:
                            sp.dma_start(out[(R - 1) * P:N, :], X[0:LASTR, (R - 1) * D:]).then_inc(stored, 16)
                        else:
                            sp.dma_start(out[bass.ds(b.number() * P, P), :], X[:, cols(b.number())]).then_inc(stored, 16)
                tile_steps(sp, -2, R + 2, step, 4 if layer == 3 else 2)
                if layer == 3:
                    sp.wait_ge(stored, 16 * R)
                else:
                    for u in range(2):
                        sp.wait_ge(m_out, R - 1 + u)
                        sp.dma_start(adjT[:, u, :], adjT_dram[u * P:(u + 1) * P, :]).then_inc(adj_first[u], 16)
                if layer == 1:
                    def x_new_load(s):
                        if s.at(-2).real():
                            sp.wait_ge(T_ready, s.at(-2).count(1) + R)
                            sp.sem_inc(turn, 1)
                        sp.wait_ge(x_new, s.count(2))
                        sp.dma_start(rows[0][:, s.slot, :], X[:, cols(s.number())]).then_inc(xs_in[s.slot], 16)
                    tile_steps(sp, 0, R - 1, x_new_load)

            @block.scalar
            def _(act):
                a = nc.scalar
                split_weights_hi(a, act, w_in, w_raw, w_hi, w_hi_ready, layer, use)

                def deviation(b):
                    if b.real():
                        act.wait_ge(mv_ready, b.count(1))
                        a.activation(sd[:, :], mv[:, 1:2], ACT.Sqrt, bias=eps_col[:, :]).then_inc(sd_ready, 1)

                def result(b):
                    if b.real():
                        act.wait_ge(co_ready, b.count(1))
                        act.sem_inc(turn, 1)
                        for t in [X[:, cols(b.number())]] + ([new_hi[:, cols(b.number())]] if layer < 3 else []):
                            a.activation(t, y[:, b.slot, :], ACT.Identity, scale=rs[:, :], bias=nmr[:, :]).then_inc(x_new, 1)

                def step(s):
                    b = s.at(1)
                    if b.real():
                        if b.at(-2).real():
                            act.wait_ge(o_out, b.at(-2).count(1))
                        for n, i in enumerate(use):
                            act.wait_ge(T_ready, b.count(n_use, n + 1))
                            a.copy(T_hi[i][:, b.slot, :], ps_T[i][b.slot][:, :]).then_inc(hi_ready, 1)
                    if layer > 1:
                        result(s.at(-2))
                        deviation(s.at(-1))
                tile_steps(act, -1, R + 1, step)
                if layer == 1:
                    act.wait_ge(o_out, R)
                    split_weights_hi(a, act, w_in, w_raw, w_hi, w_hi_ready, layer + 1, (0,))

                    def square(s):
                        if s.at(-2).real():
                            act.wait_ge(v_part, s.at(-2).count(1))
                        act.wait_ge(c_ready, s.count(1))
                        act.sem_inc(turn, 1)
                        a.activation(sq[:, s.slot, :], Y[:, cols(s.number())], ACT.Square).then_inc(sq_ready, 1)
                    tile_steps(act, 0, R - 1, square)
                    act.wait_ge(v_out, 1)
                    a.activation(scale[:, :], ps_v[:, :], ACT.Sqrt, scale=1.0 / N, bias=eps_col[:, :]).then_inc(var_ready, 1)

                    def high_new(b):
                        if b.real():
                            act.wait_ge(T_ready, b.count(1) + R)
                            a.copy(T_hi[0][:, b.slot, :], ps_T[0][b.slot][:, :]).then_inc(hi_ready, 1)

                    def keep_product(b):
                        if b.real():
                            act.wait_ge(o_out, b.count(1) + R)
                            act.sem_inc(turn, 1)
                            a.copy(Y[:, cols(b.number())], ps_out[b.slot][:, :]).then_inc(o_used, 1)

                    def step_act(s):
                        high_new(s.at(-3))
                        result(s.at(-1))
                        deviation(s)
                        keep_product(s.at(-4))
                    tile_steps(act, 0, R + 3, step_act, 4)

            @block.gpsimd
            def _(pool):
                g = nc.gpsimd

                def wait(s, v):
                    pool.wait_ge(s, v)
                    pool.sem_inc(turn, 1)

                def low(b):
                    if b.real():
                        wait(x_new, b.count(2))
                        g.tensor_tensor(new_lo[:, cols(b.number())], X[:, cols(b.number())], new_hi[:, cols(b.number())].bitcast(F32),
                                        ALU.subtract).then_inc(xlo_ready, 1)
                if layer < 3:
                    wait(w_lo_ready, n_use)
                    for i, w in enumerate(w_next):
                        g.dma_start(w_raw[:, i * KD:(i + 1) * KD, :], by_slices(w)).then_inc(w_in[i], 16)
                if layer == 1:
                    g.memset(total[:, :], 0.0).then_inc(total_ready, 1)
                    g.memset(ones[:, :], 1.0).then_inc(ones_ready, 1)
                    pool.wait_ge(ones_ready, 1)
                    g.affine_select(out=valid[:, :], in_=ones[:, :], compare_op=ALU.is_ge, fill=0.0, base=LASTR - 1,
                                    pattern=[[0, P]], channel_multiplier=-1).then_inc(ones_ready, 1)
                    with pool.Fori(0, R - 1) as r:
                        wait(xk_ready, r + 1)
                        wait(total_ready, r + 1)
                        g.tensor_tensor(total[:, :], total[:, :], Y[:, cols(r)], ALU.add).then_inc(total_ready, 1)
                    wait(v_in, 16 * len(vecs))

                    def step_act(s):
                        b = s.at(1)
                        if b.real():
                            if b.at(-2).real():
                                wait(tact_ready, b.at(-2).count(1))
                            wait(tsc_ready, b.count(1))
                            g.tensor_tensor(t_be[:, b.slot, :], t_sc[:, b.slot, :], vec[2][:, :], ALU.add).then_inc(tbe_ready, 1)
                        low(s.at(-2))
                    tile_steps(pool, -1, R + 1, step_act)
                elif layer == 2:
                    wait(v_in, 16 * len(vecs) + 1)

                    def step(s):
                        if s.real():
                            if s.at(-2).real():
                                wait(y_ready, s.at(-2).count(1))
                            g.tensor_tensor(xb[:, s.slot, :], X[:, cols(s.number())], vec[0][:, :], ALU.add).then_inc(xk_ready, 1)
                        low(s.at(-2))
                    tile_steps(pool, 0, R + 1, step)

            @block.vector
            def _(dve_):
                v = nc.vector
                if layer == 3:
                    v.tensor_scalar(keep[:, :], has[:, :], -1.0, 2.0, ALU.mult, ALU.add)

                def mean_of(b):
                    if b.real():
                        if b.at(-2).real():
                            dve_.wait_ge(T_ready, b.at(-2).count(n_use))
                        dve_.wait_ge(m_out, b.count(1))
                        dve_.sem_inc(turn, 1)
                        if layer == 3:
                            v.scalar_tensor_tensor(rows[1][:, b.slot, :], ps_m[b.slot][:, :], nrdeg[:, bass.ds(b.number(), 1)],
                                                   X[:, cols(b.number())], ALU.mult, ALU.add).then_inc(ms_ready, 1)
                        else:
                            v.tensor_scalar(rows[1][:, b.slot, :], ps_m[b.slot][:, :], rdeg[:, bass.ds(b.number(), 1)], None,
                                            ALU.mult).then_inc(ms_ready, 1)

                def low(b, i):
                    if b.real() and i in use:
                        dve_.wait_ge(hi_ready, b.count(n_use, use.index(i) + 1))
                        v.tensor_tensor(T_lo[i][:, b.slot, :], ps_T[i][b.slot][:, :], T_hi[i][:, b.slot, :].bitcast(F32),
                                        ALU.subtract).then_inc(lo_ready, 1)

                def reciprocal(b):
                    if b.real():
                        if b.at(-1).real():
                            dve_.wait_ge(x_new, b.at(-1).count(1 if layer == 3 else 2))
                        dve_.wait_ge(sd_ready, b.count(1))
                        v.reciprocal(rs[:, :], sd[:, :]).then_inc(rs_ready, 1)

                def shift(b):
                    if b.real():
                        dve_.wait_ge(rs_ready, b.count(1))
                        v.scalar_tensor_tensor(nmr[:, :], mv[:, 0:1], -1.0, rs[:, :], ALU.mult, ALU.mult).then_inc(co_ready, 1)

                def moments(b):
                    if b.real():
                        dve_.wait_ge(y_ready, b.count(1))
                        v.bn_stats(st[:, :], y[:, b.slot, :]).then_inc(st_ready, 1)

                def variance(b):
                    if b.real():
                        if b.at(-1).real():
                            dve_.wait_ge(co_ready, b.at(-1).count(1))
                        dve_.wait_ge(st_ready, b.count(1))
                        dve_.sem_inc(turn, 1)
                        v.bn_aggr(mv[:, :], st[:, :]).then_inc(mv_ready, 1)

                def out_of(b):
                    if b.real():
                        dve_.wait_ge(o_out, b.count(1))
                        if layer == 1:
                            v.tensor_tensor(Y[:, cols(b.number())], ps_out[b.slot][:, :], Y[:, cols(b.number())], ALU.add).then_inc(o_used, 1)
                            return
                        if b.at(-2).real():
                            dve_.wait_ge(x_new, b.at(-2).count(1 if layer == 3 else 2))
                        v.tensor_tensor(y[:, b.slot, :], ps_out[b.slot][:, :], Y[:, cols(b.number())] if layer == 2 else vec[0][:, :],
                                        ALU.add).then_inc(o_used, 1)

                def x_kept(b):
                    if layer == 3 and b.real():
                        if b.at(-1).real():
                            dve_.wait_ge(y_ready, b.at(-1).count(1))
                        dve_.sem_inc(turn, 1)
                        v.tensor_scalar(xk[:, :], X[:, cols(b.number())], keep[:, bass.ds(b.number(), 1)], None, ALU.mult).then_inc(xk_ready, 1)

                def y_of(b):
                    if layer == 1 and b.real():
                        dve_.wait_ge(o_used, b.count(1))
                        v.tensor_tensor(Y[:, cols(b.number())], Y[:, cols(b.number())], vec[0][:, :], ALU.add).then_inc(xk_ready, 1)
                    elif b.real():
                        dve_.wait_ge(o_used, b.count(1))
                        if layer == 2:
                            dve_.wait_ge(xk_ready, b.count(1))
                            v.tensor_tensor(y[:, b.slot, :], y[:, b.slot, :], xb[:, b.slot, :], ALU.add).then_inc(y_ready, 1)
                        else:
                            dve_.wait_ge(xk_ready, b.count(1))
                            dve_.sem_inc(turn, 1)
                            v.scalar_tensor_tensor(y[:, b.slot, :], y[:, b.slot, :], has[:, bass.ds(b.number(), 1)], xk[:, :],
                                                   ALU.mult, ALU.add).then_inc(y_ready, 1)

                def step(s):
                    if s.it2 is None and s.k == -1:
                        split_weights_lo(v, dve_, w_raw, w_hi, w_lo, w_hi_ready, w_lo_ready, use)
                        dve_.wait_ge(v_in, 16 * len(vecs))
                        if layer > 1:
                            v.tensor_tensor(vec[0][:, :], vec[0][:, :], vec[1][:, :], ALU.add).then_inc(v_in, 1)
                            dve_.wait_ge(v_in, 16 * len(vecs) + 1)
                    out_of(s.at(-1))
                    x_kept(s.at(-1))
                    if layer > 1:
                        reciprocal(s.at(-2))
                    mean_of(s.at(2))
                    y_of(s.at(-1))
                    if layer > 1:
                        shift(s.at(-2))
                    low(s.at(1), 0)
                    if layer > 1:
                        moments(s.at(-1))
                    low(s.at(1), 1)
                    if layer > 1:
                        variance(s.at(-1))
                tile_steps(dve_, -2, R + 1, step, 4 if layer > 1 else 2)
                if layer == 1:
                    split_weights_lo(v, dve_, w_raw, w_hi, w_lo, w_hi_ready, w_lo_ready, (0,), 1)
                    dve_.wait_ge(s_out, 1)
                    v.tensor_scalar(mean[:, :], ps_s[:, :], 1.0 / N, None, ALU.mult).then_inc(scale_ready, 1)
                    dve_.wait_ge(scale_ready, 1)
                    with dve_.Fori(0, R) as r:
                        v.tensor_tensor(Y[:, cols(r)], Y[:, cols(r)], mean[:, :], ALU.subtract).then_inc(c_ready, 1)
                    dve_.wait_ge(var_ready, 1)
                    v.reciprocal(mean[:, :], scale[:, :]).then_inc(scale_ready, 1)
                    dve_.wait_ge(scale_ready, 2)
                    v.tensor_tensor(scale[:, :], mean[:, :], vec[1][:, :], ALU.mult).then_inc(scale_ready, 1)
                    dve_.wait_ge(scale_ready, 3)

                    def step_act(s):
                        b = s.at(1)
                        if b.real():
                            if b.at(-2).real():
                                dve_.wait_ge(tbe_ready, b.at(-2).count(1))
                            v.tensor_tensor(t_sc[:, b.slot, :], Y[:, cols(b.number())], scale[:, :], ALU.mult).then_inc(tsc_ready, 1)
                        if s.real():
                            dve_.wait_ge(tbe_ready, s.count(1))
                            if s.at(-1).real():
                                dve_.wait_ge(y_ready, s.at(-1).count(1))
                            v.scalar_tensor_tensor(t_act[:, :], t_be[:, s.slot, :], 0.01, t_be[:, s.slot, :], ALU.mult, ALU.max).then_inc(tact_ready, 1)
                        reciprocal(s.at(-1))
                        if s.real():
                            if s.at(-2).real():
                                dve_.wait_ge(x_new, s.at(-2).count(2))
                            dve_.wait_ge(tact_ready, s.count(1))
                            v.scalar_tensor_tensor(y[:, s.slot, :], X[:, cols(s.number())], 2.0, t_act[:, :], ALU.mult, ALU.add).then_inc(y_ready, 1)
                        shift(s.at(-1))
                        moments(s)
                        b = s.at(-3)
                        if b.real():
                            dve_.wait_ge(hi_ready, b.count(1) + R)
                            v.tensor_tensor(T_lo[0][:, b.slot, :], ps_T[0][b.slot][:, :], T_hi[0][:, b.slot, :].bitcast(F32),
                                            ALU.subtract).then_inc(lo_ready, 1)
                        variance(s)
                    tile_steps(dve_, -1, R + 2, step_act, 4)

            @block.tensor
            def _(pe):
                t = nc.tensor
                is_slow = pe.value_load(slow[0:1, 0:1], min_val=0, max_val=1)

                def sums(b):
                    if b.real():
                        if b.at(-2).real():
                            pe.wait_ge(a_in[b.slot], b.at(-2).slot_count(16))
                        else:
                            pe.wait_ge(adj_first[b.slot], 16 * layer)
                        if b.at(-2).real():
                            pe.wait_ge(ms_ready, b.at(-2).count(1))
                        pe.sem_inc(turn, 1)
                        with pe.If(is_slow):
                            sums_in(b, F32)
                        with pe.Else():
                            sums_in(b, F32R)

                def sums_in(b, dt):
                    for k in range(R):
                        for i, xx in enumerate((X_hi, X_lo)):
                            last = t.matmul(ps_m[b.slot][:, :], adjT[:, b.slot, k * P:(k + 1) * P].bitcast(dt), xx[:, cols(k)].bitcast(dt),
                                            start=(k == 0 and i == 0), stop=(k == R - 1 and i == 1))
                    last.then_inc(m_out, 1)

                def turn_both(b):
                    if b.real():
                        for i in use:
                            if i == 0:
                                pe.wait_ge(xs_in[b.slot], b.slot_count(16))
                            else:
                                pe.wait_ge(ms_ready, b.count(1))
                            for k in range(KD):
                                last = t.transpose(ps_T[i][b.slot][:, k * P:(k + 1) * P], rows[i][:, b.slot, k * P:(k + 1) * P], ident[:, :])
                            last.then_inc(T_ready, 1)

                def products(b):
                    if b.real():
                        if b.at(-2).real():
                            pe.wait_ge(o_used, b.at(-2).count(1))
                        for n, i in enumerate(use):
                            if b.it2 is None and b.k == 0:
                                pe.wait_ge(w_lo_ready, n + 1)
                            pe.wait_ge(lo_ready, b.count(n_use, n + 1))
                            last = three_products(nc, ps_out[b.slot], T_hi[i][:, b.slot, :], T_lo[i][:, b.slot, :],
                                                  w_hi[:, i * KD:(i + 1) * KD, :], w_lo[:, i * KD:(i + 1) * KD, :], n == 0, i == 1)
                        last.then_inc(o_out, 1)

                def step(s):
                    sums(s.at(2))
                    turn_both(s.at(1))
                    products(s)
                tile_steps(pe, -2, R - 1, step)
                if layer == 1:
                    pe.wait_ge(ones_ready, 2)
                    pe.wait_ge(xk_ready, R)
                    t.matmul(ps_s[:, :], valid[:, :], Y[:, cols(R - 1)], start=True, stop=False)
                    pe.wait_ge(total_ready, R)
                    t.matmul(ps_s[:, :], ones[:, :], total[:, :], start=False, stop=True).then_inc(s_out, 1)

                    def square_sums(s):
                        pe.wait_ge(sq_ready, s.count(1))
                        final = s.it2 is None and s.k == R - 1
                        t.matmul(ps_v[:, :], (valid if final else ones)[:, :], sq[:, s.slot, :], start=(s.it2 is None and s.k == 0),
                                 stop=final).then_inc(v_out if final else v_part, 1)
                    tile_steps(pe, 0, R - 1, square_sums)

                    def next_product(s):
                        b = s.at(1)
                        if b.real():
                            pe.wait_ge(xs_in[b.slot], b.slot_count(16))
                            for k in range(KD):
                                last = t.transpose(ps_T[0][b.slot][:, k * P:(k + 1) * P], rows[0][:, b.slot, k * P:(k + 1) * P], ident[:, :])
                            last.then_inc(T_ready, 1)
                        if s.real():
                            if s.it2 is None and s.k == 0:
                                pe.wait_ge(w_lo_ready, 2)
                            if s.at(-2).real():
                                pe.wait_ge(o_used, s.at(-2).count(1) + R)
                            pe.wait_ge(lo_ready, s.count(1) + R)
                            three_products(nc, ps_out[s.slot], T_hi[0][:, s.slot, :], T_lo[0][:, s.slot, :], w_hi[:, 0:KD, :],
                                           w_lo[:, 0:KD, :], True, True).then_inc(o_out, 1)
                    tile_steps(pe, -1, R - 1, next_product)


def kernel(**inputs):
    import numpy as np
    import concourse.bacc as bacc
    from concourse.bass_utils import run_bass_kernel_spmd as run

    nc = bacc.Bacc("TRN2", target_bir_lowering=False, num_devices=1)
    a = {k: np.ascontiguousarray(v) for k, v in inputs.items()}
    edges = np.zeros((ED, NB * BE), a["edge_attr_64"].dtype)
    edges[:, :E] = a["edge_attr_64"].T
    nodes = np.zeros((NP, D), a["x"].dtype)
    nodes[:N] = a["x"]
    w1 = a["L0_gnn_W1"]
    arrays = {
        "x": nodes, "src": a["src"], "dst": a["dst"], "eaT": edges,
        "w0a": w1[0:D], "w0b": w1[D:2 * D], "w0c": w1[2 * D:], "b01": a["L0_gnn_b1"],
        "w02": a["L0_gnn_W2"], "b02": a["L0_gnn_b2"], "w03": a["L0_gnn_W3"], "b03": a["L0_gnn_b3"],
        "w04": a["L0_gnn_W4"], "b04": a["L0_gnn_b4"], "g0": a["L0_gnn_gamma"], "be0": a["L0_gnn_beta"],
        "w1l": a["L1_gnn_W_l"], "b1l": a["L1_gnn_b_l"], "w1r": a["L1_gnn_W_r"], "g1": a["L1_gnn_gamma"],
        "be1": a["L1_gnn_beta"], "w21": a["L2_gnn_W1"].T, "b21": a["L2_gnn_b1"], "w22": a["L2_gnn_W2"].T,
        "b22": a["L2_gnn_b2"], "w31": a["L3_gnn_W1"], "b31": a["L3_gnn_b1"], "w32": a["L3_gnn_W2"],
        "b32": a["L3_gnn_b2"],
    }
    arrays = {"in_" + k: np.ascontiguousarray(v) for k, v in arrays.items()}
    args = [nc.dram_tensor(k, v.shape, mybir.dt.from_np(v.dtype), kind="ExternalInput").ap() for k, v in arrays.items()]
    out = nc.dram_tensor("out_x", [N, D], F32, kind="ExternalOutput").ap()
    gnn(nc, *args, out)
    return run(nc, [arrays], core_ids=[0]).results[0]["out_x"]
```
